# Optimizing a Trainium2 kernel written in Bass

```python
import numpy as np
import jax
import jax.numpy as jnp

def _softmax(x, axis=-1):
    return jax.nn.softmax(x, axis=axis)

def _gelu(x):
    return jax.nn.gelu(x, approximate=True)

def _silu(x):
    return jax.nn.silu(x)

def _sigmoid(x):
    return jax.nn.sigmoid(x)

def _layernorm(x, axis=-1, eps=1e-05):
    m = jnp.mean(x, axis=axis, keepdims=True)
    v = jnp.var(x, axis=axis, keepdims=True)
    return (x - m) / jnp.sqrt(v + eps)

def _scatter_add(tgt, idx, src, axis=0):
    return tgt.at[idx].add(src)

def _segment_sum(src, seg, n):
    return jax.ops.segment_sum(src, seg, n)
kernel_name = 'mk_adj_preln_d4_adj_r2_24fd2e'

def setup_inputs(seed: int=0):
    np.random.seed(seed)
    _w = jnp.asarray

    def _rec_inputs():
        import jax
        import jax.numpy as jnp
        _gk = jax.random.key(seed)
        x = -0.0001015 + 0.9999 * jax.random.normal(jax.random.fold_in(_gk, 1), (128, 128, 128), jnp.float32)
        _a = jax.random.bernoulli(jax.random.fold_in(_gk, 2), 0.125, (128, 128))
        _a = jnp.logical_or(_a, jnp.swapaxes(_a, -1, -2))
        _a = jnp.logical_or(_a, jnp.eye(128, dtype=bool))
        _af = _a.astype(jnp.float32)
        _af = _af * jax.random.uniform(jax.random.fold_in(_gk, 3), (128, 128), jnp.float32, 0.05, 0.997825)
        adj = _af
        return (x, adj)
    x, adj = _rec_inputs()

    def _L0_gnn_setup():
        import jax, jax.numpy as jnp
        import numpy as np
        B, J, F_IN, F_OUT = (8192, 17, 128, 128)
        key = jax.random.key(seed)
        k1, k2, k3, k4 = jax.random.split(key, 4)
        gain = 1.414
        bound = gain * np.sqrt(6.0 / (F_IN + F_OUT))
        W = jax.random.uniform(k2, (3, F_IN, F_OUT), dtype=jnp.float32, minval=-bound, maxval=bound)
        stdv = 1.0 / np.sqrt(F_OUT)
        bias = jax.random.uniform(k4, (F_OUT,), dtype=jnp.float32, minval=-stdv, maxval=stdv)
        return {'x': jax.random.normal(k1, (B, J, F_IN), dtype=jnp.float32), 'W': W, 'adj': jax.random.uniform(k3, (J, J), dtype=jnp.float32), 'bias': bias}
    _L0_gnn_all = _L0_gnn_setup()
    _L0_gnn_in = {k: v for k, v in _L0_gnn_all.items() if k in ('W', 'bias')}
    del _L0_gnn_all

    def _L1_gnn_setup():
        import jax, jax.numpy as jnp
        import numpy as np
        EPS = 1e-05

        def _batchnorm(x, gamma, beta):
            mu = jnp.mean(x, axis=0)
            var = jnp.var(x, axis=0)
            return (x - mu) * jax.lax.rsqrt(var + EPS) * gamma + beta
        key = jax.random.key(seed)
        ks = jax.random.split(key, 4)
        b, n, d, h, o = (32, 1024, 128, 256, 128)
        features = jax.random.normal(ks[0], (b, n, d), dtype=jnp.float32)
        A = jax.random.uniform(ks[1], (n, n), dtype=jnp.float32)
        lim1 = float(np.sqrt(6.0 / (d + h)))
        W1 = jax.random.uniform(ks[2], (h, d), minval=-lim1, maxval=lim1, dtype=jnp.float32)
        b1 = jnp.zeros((h,), jnp.float32)
        lim2 = float(np.sqrt(6.0 / (h + o)))
        W2 = jax.random.uniform(ks[3], (o, h), minval=-lim2, maxval=lim2, dtype=jnp.float32)
        b2 = jnp.zeros((o,), jnp.float32)
        g1 = jnp.ones((h,), jnp.float32)
        be1 = jnp.zeros((h,), jnp.float32)
        g2 = jnp.ones((o,), jnp.float32)
        be2 = jnp.zeros((o,), jnp.float32)
        return {'features': features, 'A': A, 'W1': W1, 'b1': b1, 'g1': g1, 'be1': be1, 'W2': W2, 'b2': b2, 'g2': g2, 'be2': be2}
    _L1_gnn_all = _L1_gnn_setup()
    _L1_gnn_in = {k: v for k, v in _L1_gnn_all.items() if k in ('W1', 'b1', 'g1', 'be1', 'W2', 'b2', 'g2', 'be2')}
    del _L1_gnn_all

    def _L2_gnn_setup():
        import jax, jax.numpy as jnp
        import numpy as np
        B, T, D, H = (64, 1024, 128, 128)
        MAX_SKIP = 4

        def _lstm_last(Wih, Whh, bih, bhh, xs):
            N, _, Hd = xs.shape
            bias = bih + bhh

            def step(carry, x_t):
                h, c = carry
                g = x_t @ Wih.T + h @ Whh.T + bias
                i, f, gg, o = jnp.split(g, 4, axis=-1)
                c = jax.nn.sigmoid(f) * c + jax.nn.sigmoid(i) * jnp.tanh(gg)
                h = jax.nn.sigmoid(o) * jnp.tanh(c)
                return ((h, c), None)
            init = (jnp.zeros((N, Hd), xs.dtype), jnp.zeros((N, Hd), xs.dtype))
            (h_last, _), _ = jax.lax.scan(step, init, jnp.swapaxes(xs, 0, 1))
            return h_last
        key = jax.random.key(seed)
        ks = jax.random.split(key, 8)
        s = 0.05
        x = jax.random.normal(ks[0], (B, T, D), jnp.float32)
        adj = jax.random.uniform(ks[1], (T, T), jnp.float32) / T
        Wg0 = jax.random.normal(ks[2], (D, H), jnp.float32) * s
        bg0 = jnp.zeros((H,), jnp.float32)
        Wg1 = jax.random.normal(ks[3], (H, H), jnp.float32) * s
        bg1 = jnp.zeros((H,), jnp.float32)
        Wih = jax.random.normal(ks[4], (MAX_SKIP, 4 * H, H), jnp.float32) * s
        Whh = jax.random.normal(ks[5], (MAX_SKIP, 4 * H, H), jnp.float32) * s
        bih = jax.random.normal(ks[6], (MAX_SKIP, 4 * H), jnp.float32) * s
        bhh = jax.random.normal(ks[7], (MAX_SKIP, 4 * H), jnp.float32) * s
        return dict(x=x, adj=adj, Wg0=Wg0, bg0=bg0, Wg1=Wg1, bg1=bg1, Wih=Wih, Whh=Whh, bih=bih, bhh=bhh)
    _L2_gnn_all = _L2_gnn_setup()
    _L2_gnn_in = {k: v for k, v in _L2_gnn_all.items() if k in ('Wg0', 'bg0', 'Wg1', 'bg1', 'Wih', 'Whh', 'bih', 'bhh')}
    del _L2_gnn_all

    def _L3_gnn_setup():
        import jax, jax.numpy as jnp
        import numpy as np
        BT, N, D, HEADS, E = (512, 64, 128, 4, 256)
        LRELU_SLOPE = 0.2
        EPS = 1e-08
        key = jax.random.key(seed)
        ks = jax.random.split(key, 8)
        d = D
        return {'H': jax.random.normal(ks[0], (BT, N, d), jnp.float32), 'W_lin': jax.random.normal(ks[1], (d, d), jnp.float32) / np.sqrt(d).astype(np.float32), 'W_val': jax.random.normal(ks[2], (d, d), jnp.float32) / np.sqrt(d).astype(np.float32), 'a': jax.random.normal(ks[3], (HEADS, d // HEADS), jnp.float32), 'W_out': jax.random.normal(ks[4], (d, d), jnp.float32) / np.sqrt(d).astype(np.float32), 'A0': jax.random.uniform(ks[5], (N, N), jnp.float32), 'src': jax.random.randint(ks[6], (E,), 0, N, jnp.int32), 'dst': jax.random.randint(ks[7], (E,), 0, N, jnp.int32)}
    _L3_gnn_all = _L3_gnn_setup()
    _L3_gnn_in = {k: v for k, v in _L3_gnn_all.items() if k in ('W_lin', 'W_val', 'a', 'W_out', 'src', 'dst')}
    del _L3_gnn_all
    return {'x': x, 'adj': adj, 'L0_gnn_W': _L0_gnn_in['W'], 'L0_gnn_bias': _L0_gnn_in['bias'], 'L1_gnn_W1': _L1_gnn_in['W1'], 'L1_gnn_b1': _L1_gnn_in['b1'], 'L1_gnn_g1': _L1_gnn_in['g1'], 'L1_gnn_be1': _L1_gnn_in['be1'], 'L1_gnn_W2': _L1_gnn_in['W2'], 'L1_gnn_b2': _L1_gnn_in['b2'], 'L1_gnn_g2': _L1_gnn_in['g2'], 'L1_gnn_be2': _L1_gnn_in['be2'], 'L2_gnn_Wg0': _L2_gnn_in['Wg0'], 'L2_gnn_bg0': _L2_gnn_in['bg0'], 'L2_gnn_Wg1': _L2_gnn_in['Wg1'], 'L2_gnn_bg1': _L2_gnn_in['bg1'], 'L2_gnn_Wih': _L2_gnn_in['Wih'], 'L2_gnn_Whh': _L2_gnn_in['Whh'], 'L2_gnn_bih': _L2_gnn_in['bih'], 'L2_gnn_bhh': _L2_gnn_in['bhh'], 'L3_gnn_W_lin': _L3_gnn_in['W_lin'], 'L3_gnn_W_val': _L3_gnn_in['W_val'], 'L3_gnn_a': _L3_gnn_in['a'], 'L3_gnn_W_out': _L3_gnn_in['W_out'], 'L3_gnn_src': _L3_gnn_in['src'], 'L3_gnn_dst': _L3_gnn_in['dst']}

def reference(x, adj, L0_gnn_W, L0_gnn_bias, L1_gnn_W1, L1_gnn_b1, L1_gnn_g1, L1_gnn_be1, L1_gnn_W2, L1_gnn_b2, L1_gnn_g2, L1_gnn_be2, L2_gnn_Wg0, L2_gnn_bg0, L2_gnn_Wg1, L2_gnn_bg1, L2_gnn_Wih, L2_gnn_Whh, L2_gnn_bih, L2_gnn_bhh, L3_gnn_W_lin, L3_gnn_W_val, L3_gnn_a, L3_gnn_W_out, L3_gnn_src, L3_gnn_dst):
    import jax
    import jax.numpy as jnp

    def _L0_gnn_ref(x, W, adj, bias):
        import jax, jax.numpy as jnp
        import numpy as np
        B, J, F_IN, F_OUT = (8192, 17, 128, 128)
        adj_0 = jnp.diag(jnp.diagonal(adj))
        adj_1 = jnp.triu(adj, k=1)
        adj_2 = jnp.tril(adj, k=-1)
        h = jnp.einsum('bjf,kfo->kbjo', x, W)
        out = jnp.einsum('ij,bjo->bio', adj_0, h[0]) + jnp.einsum('ij,bjo->bio', adj_1, h[1]) + jnp.einsum('ij,bjo->bio', adj_2, h[2])
        return out + bias[None, None, :]

    def _L1_gnn_ref(features, A, W1, b1, g1, be1, W2, b2, g2, be2):
        import jax, jax.numpy as jnp
        import numpy as np
        EPS = 1e-05

        def _batchnorm(x, gamma, beta):
            mu = jnp.mean(x, axis=0)
            var = jnp.var(x, axis=0)
            return (x - mu) * jax.lax.rsqrt(var + EPS) * gamma + beta
        b, n, d = features.shape
        A_norm = A + jnp.eye(n, dtype=A.dtype)
        deg = jnp.sum(A_norm, axis=0) + jnp.sum(A_norm, axis=1) - jnp.diagonal(A_norm)
        dinv = jax.lax.rsqrt(deg)
        A_hat = A_norm * dinv[:, None] * dinv[None, :]
        agg = jnp.einsum('nm,bmd->bnd', A_hat, features)
        x = agg.reshape(-1, d)
        h = jax.nn.relu(_batchnorm(x @ W1.T + b1, g1, be1))
        out = h @ W2.T + b2
        out = _batchnorm(out, g2, be2)
        return out.reshape(b, n, -1)

    def _L2_gnn_ref(x, adj, Wg0, bg0, Wg1, bg1, Wih, Whh, bih, bhh):
        import jax, jax.numpy as jnp
        import numpy as np
        B, T, D, H = (64, 1024, 128, 128)
        MAX_SKIP = 4

        def _lstm_last(Wih, Whh, bih, bhh, xs):
            N, _, Hd = xs.shape
            bias = bih + bhh

            def step(carry, x_t):
                h, c = carry
                g = x_t @ Wih.T + h @ Whh.T + bias
                i, f, gg, o = jnp.split(g, 4, axis=-1)
                c = jax.nn.sigmoid(f) * c + jax.nn.sigmoid(i) * jnp.tanh(gg)
                h = jax.nn.sigmoid(o) * jnp.tanh(c)
                return ((h, c), None)
            init = (jnp.zeros((N, Hd), xs.dtype), jnp.zeros((N, Hd), xs.dtype))
            (h_last, _), _ = jax.lax.scan(step, init, jnp.swapaxes(xs, 0, 1))
            return h_last
        h = jax.nn.relu(jnp.einsum('ts,bsh->bth', adj, x @ Wg0 + bg0))
        h = jax.nn.relu(jnp.einsum('ts,bsh->bth', adj, h @ Wg1 + bg1))
        Bv, Tv, Hd = h.shape
        for p in range(1, MAX_SKIP + 1):
            nw = Tv // p
            wins = h[:, :nw * p, :].reshape(Bv * nw, p, Hd)
            last = _lstm_last(Wih[p - 1], Whh[p - 1], bih[p - 1], bhh[p - 1], wins)
            idx = jnp.arange(nw) * p + (p - 1)
            h = h.at[:, idx, :].set(last.reshape(Bv, nw, Hd))
        return h

    def _L3_gnn_ref(H, W_lin, W_val, a, W_out, A0, src, dst):
        import jax, jax.numpy as jnp
        import numpy as np
        BT, N, D, HEADS, E = (512, 64, 128, 4, 256)
        LRELU_SLOPE = 0.2
        EPS = 1e-08
        bt, n, d = H.shape
        h, dh = a.shape
        Xq = (H @ W_lin.T).reshape(bt, n, h, dh)
        Xv = (H @ W_val.T).reshape(bt, n, h, dh)
        Qs = Xq[:, src]
        Kt = Xq[:, dst]
        e = jnp.einsum('behd,hd->beh', jax.nn.leaky_relu(Qs + Kt, LRELU_SLOPE), a)
        e = e + jnp.log(A0[src, dst] + EPS)[None, :, None]
        e_t = e.transpose(1, 0, 2)
        m = jax.ops.segment_max(e_t, src, num_segments=n)
        ex = jnp.exp(e_t - m[src])
        denom = jax.ops.segment_sum(ex, src, num_segments=n)
        attn = ex / denom[src]
        Vt = Xv[:, dst].transpose(1, 0, 2, 3)
        Y = jax.ops.segment_sum(attn[..., None] * Vt, src, num_segments=n)
        Y = Y.transpose(1, 0, 2, 3).reshape(bt, n, d)
        return Y @ W_out.T
    h = jnp.maximum(_layernorm(x, axis=-1), 0.0)
    x = x + _L0_gnn_ref(h, L0_gnn_W, adj, L0_gnn_bias)
    h = jnp.maximum(_layernorm(x, axis=-1), 0.0)
    x = x + _L1_gnn_ref(h, adj, L1_gnn_W1, L1_gnn_b1, L1_gnn_g1, L1_gnn_be1, L1_gnn_W2, L1_gnn_b2, L1_gnn_g2, L1_gnn_be2)
    h = jnp.maximum(_layernorm(x, axis=-1), 0.0)
    x = x + _L2_gnn_ref(h, adj, L2_gnn_Wg0, L2_gnn_bg0, L2_gnn_Wg1, L2_gnn_bg1, L2_gnn_Wih, L2_gnn_Whh, L2_gnn_bih, L2_gnn_bhh)
    h = jnp.maximum(_layernorm(x, axis=-1), 0.0)
    x = x + _L3_gnn_ref(h, L3_gnn_W_lin, L3_gnn_W_val, L3_gnn_a, L3_gnn_W_out, adj, L3_gnn_src, L3_gnn_dst)
    return x

_drawn_inputs = setup_inputs


def setup_inputs(seed=0):
    import zlib

    import numpy as np

    out = dict(_drawn_inputs(seed))
    spreads = {'L1_gnn_b1': (0.0, 2.0),
     'L1_gnn_g1': (1.0, 0.567),
     'L1_gnn_be1': (0.0, 0.76),
     'L1_gnn_b2': (0.0, 2.0),
     'L1_gnn_g2': (1.0, 0.2),
     'L1_gnn_be2': (0.0, 0.6),
     'L2_gnn_bg0': (0.0, 0.376),
     'L2_gnn_bg1': (0.0, 2.0)}
    factors = {'L0_gnn_bias': 8.0,
     'L2_gnn_Whh': 22.525,
     'L2_gnn_bih': 8.0,
     'L2_gnn_bhh': 21.422,
     'L3_gnn_W_lin': 6.928,
     'L3_gnn_a': 6.355}
    for name, (base, spread) in spreads.items():
        noise = np.random.default_rng([zlib.crc32(name.encode()), seed]).standard_normal(out[name].shape)
        drawn = base * np.exp(spread * noise) if base else spread * noise
        out[name] = jnp.asarray(drawn.astype(out[name].dtype))
    for name, factor in factors.items():
        out[name] = (out[name] * factor).astype(out[name].dtype)
    return out
```

```python
from contextlib import ExitStack

import concourse.bass as bass
from concourse import mybir

ALU = mybir.AluOpType
ACT = mybir.ActivationFunctionType
F32 = mybir.dt.float32
F32R = mybir.dt.float32r
I32 = mybir.dt.int32
P = 128
EPS = 1e-5
EPS_EDGE = 1e-8
TB = 4
TW = TB * P
BIG = 1.0e30

C_B1, C_G1, C_BE1 = 0, 2, 4
C_B2, C_G2, C_BE2 = 6, 7, 8
C_BIH, C_BHH = 9, 25
NCOLS = 41
R_L0, R_G0, R_G1 = 0, 1, 2


class Shared:
    sems = ()

    def sem(self, name):
        handle = self.nc.alloc_semaphore(name)
        self.sems += (handle,)
        return handle

    def recycle_semaphores(self):
        self.nc.clear_and_free_semaphores(list(self.sems))
        self.nc.all_engine_barrier()
        self.sems = ()


def each(n, make):
    return [make(i) for i in range(n)]


def layernorm_coefficients(k, ctx, name):
    nc = k.nc
    t = {n: ctx.enter_context(nc.sbuf_tensor(f"{name}_{n}", [P, k.B], F32))
         for n in ("sum", "m2", "diff", "sq", "var")}
    done = k.sem(f"{name}_coef_dve")
    powed = k.sem(f"{name}_coef_pow")
    ready = k.sem(f"{name}_coef_ready")
    mean_e, m2_e = k.st6[:, :, 1], k.st6[:, :, 2]
    mean_o, m2_o = k.st6[:, :, 4], k.st6[:, :, 5]

    def on_vector(dve):
        dve.tensor_tensor(t["sum"][:, :], mean_e, mean_o, ALU.add).then_inc(done, 1)
        dve.tensor_tensor(t["diff"][:, :], mean_e, mean_o, ALU.subtract).then_inc(done, 1)
        dve.tensor_tensor(t["m2"][:, :], m2_e, m2_o, ALU.add).then_inc(done, 1)
        dve.wait_ge(done, 3)
        dve.scalar_tensor_tensor(t["sq"][:, :], t["diff"][:, :], 0.25, t["diff"][:, :],
                                 ALU.mult, ALU.mult).then_inc(done, 1)
        dve.tensor_scalar(t["m2"][:, :], t["m2"][:, :], 1.0 / P, EPS, ALU.mult, ALU.add).then_inc(done, 1)
        dve.wait_ge(done, 5)
        dve.tensor_tensor(t["var"][:, :], t["m2"][:, :], t["sq"][:, :], ALU.add).then_inc(done, 1)
        dve.wait_ge(powed, 1)
        dve.scalar_tensor_tensor(k.nmr[:, :], t["sum"][:, :], -0.5, k.rstd[:, :],
                                 ALU.mult, ALU.mult).then_inc(ready, 1)

    def on_pool(pool):
        pool.wait_ge(done, 6)
        pool.tensor_tensor(out=k.rstd[:, :], in0=t["var"][:, :], in1=k.mhalf[:, :], op=ALU.pow).then_inc(powed, 1)

    return on_vector, on_pool, ready


def normalise_tile(act, k, h, b0):
    for j in range(TB):
        last = act.activation(h[:, j, :], k.X[:, bass.ds(b0, TB), :][:, j, :], ACT.Relu,
                              bias=k.nmr[:, bass.ds(b0, TB)][:, j:j + 1], scale=k.rstd[:, bass.ds(b0, TB)][:, j:j + 1])
    return last


def stats_tile(dve, k, b0):
    for j in range(TB):
        last = dve.bn_stats(k.st6[:, bass.ds(b0, TB), :][:, j, :], k.X[:, bass.ds(b0, TB), :][:, j, :])
    return last


def stage_setup(k, ctx, d):
    nc, X = k.nc, k.X
    sem = lambda n: k.sem(n)
    sb = lambda n, s, t=F32: ctx.enter_context(nc.sbuf_tensor(n, s, t))
    CH = 8
    CB = k.B // CH
    x_in = each(CH, lambda c: sem(f"x_in{c}"))
    adj_in, w_in, cols_in = sem("adj_in"), sem("w_in"), sem("cols_in")
    cst, masks, deg, dinv_p, dinv_bc, ahat = (sem(n) for n in ("cst", "masks", "deg", "dinv_p", "dinv_bc", "ahat"))
    stats_done, diag_ready, sep, primed = (sem(n) for n in ("setup_stats", "diag_ready", "setup_sep", "primed"))
    adj = sb("adj_rows", [P, P])
    onesPP = k.ones
    rs = sb("deg_parts", [P, 4])
    tmp = sb("setup_tmp", [P, P])
    tmp2 = sb("setup_tmp2", [P, P])
    dinv = sb("dinv", [P, 1])
    bank_dg, bank_di = k.bank[0], k.bank[1]

    with nc.Block() as block:
        @block.sync
        def _(sp):
            sp.dma_start(adj[:, :], d["adj"]).then_inc(adj_in, 16)
            sp.dma_start(k.adjT[:, :], d["adjT"]).then_inc(adj_in, 16)
            for c in range(CH):
                sp.dma_start(X[:, c * CB:(c + 1) * CB, :], d["x"][:, c * CB:(c + 1) * CB, :]).then_inc(x_in[c], 16)

        @block.scalar
        def _(act):
            act.wait_ge(cst, 1)
            act.activation(k.ones[:, 0:1], k.ones[:, 0:1], ACT.Sigmoid).then_inc(primed, 1)
            act.dma_start(k.cols[:, :], d["cols"]).then_inc(cols_in, 16)
            act.dma_start(k.rows[:, :, :], d["rows"].partition_broadcast(P)).then_inc(cols_in, 16)
            act.dma_start(k.W0[:, :, :], d["L0_W"].rearrange("k f o -> f k o")).then_inc(w_in, 16)
            act.dma_start(k.W1T[:, :], d["W1T"]).then_inc(w_in, 16)
            act.dma_start(k.W2T[:, :, :], d["W2T"].rearrange("(h c) o -> c h o", h=2)).then_inc(w_in, 16)
            act.dma_start(k.Wg[:, 0, :], d["Wg0"]).then_inc(w_in, 16)
            act.dma_start(k.Wg[:, 1, :], d["Wg1"]).then_inc(w_in, 16)
            act.wait_ge(w_in, 5 * 16)
            act.wait_ge(cols_in, 2 * 16)

        @block.gpsimd
        def _(pool):
            pool.memset(k.mhalf[:, :], -0.5)
            pool.memset(onesPP[:, :], 0.0).then_inc(cst, 1)
            pool.wait_ge(primed, 1)
            pool.memset(onesPP[:, :], 1.0).then_inc(cst, 1)
            pool.memset(k.ident[:, :], 0.0).then_inc(sep, 1)
            pool.wait_ge(sep, 1)
            pool.affine_select(out=k.ident[:, :], in_=k.ident[:, :], compare_op=ALU.not_equal, fill=1.0,
                               base=0, pattern=[[-1, P]], channel_multiplier=1).then_inc(cst, 1)
            pool.wait_ge(adj_in, 32)
            pool.affine_select(out=k.A12T[:, 0, :], in_=k.adjT[:, :], compare_op=ALU.is_gt, fill=0.0,
                               base=0, pattern=[[-1, P]], channel_multiplier=1).then_inc(masks, 1)
            pool.affine_select(out=k.A12T[:, 1, :], in_=k.adjT[:, :], compare_op=ALU.is_gt, fill=0.0,
                               base=0, pattern=[[1, P]], channel_multiplier=-1).then_inc(masks, 1)
            pool.wait_ge(deg, 5)
            pool.tensor_tensor(out=dinv[:, :], in0=rs[:, 3:4], in1=k.mhalf[:, 0:1], op=ALU.pow).then_inc(dinv_p, 1)

        @block.tensor
        def _(pe):
            pe.wait_ge(cst, 3)
            pe.wait_ge(deg, 1)
            pe.matmul(bank_dg[:, 0:P], onesPP[:, :], tmp[:, :], start=True, stop=True).then_inc(diag_ready, 1)
            pe.wait_ge(dinv_bc, 1)
            pe.matmul(bank_di[:, 0:P], onesPP[:, :], tmp2[:, :], start=True, stop=True).then_inc(diag_ready, 1)

        @block.vector
        def _(dve):
            dve.wait_ge(adj_in, 32)
            dve.wait_ge(cst, 3)
            dve.tensor_tensor(tmp[:, :], adj[:, :], k.ident[:, :], ALU.mult).then_inc(deg, 1)
            dve.wait_ge(deg, 1)
            dve.reduce_sum(rs[:, 0:1], adj[:, :], mybir.AxisListType.X)
            dve.reduce_sum(rs[:, 1:2], k.adjT[:, :], mybir.AxisListType.X)
            dve.reduce_sum(rs[:, 2:3], tmp[:, :], mybir.AxisListType.X).then_inc(deg, 1)
            dve.wait_ge(deg, 2)
            dve.tensor_tensor(rs[:, 0:1], rs[:, 0:1], rs[:, 1:2], ALU.add).then_inc(deg, 1)
            dve.wait_ge(deg, 3)
            dve.tensor_tensor(rs[:, 3:4], rs[:, 0:1], rs[:, 2:3], ALU.subtract).then_inc(deg, 1)
            dve.wait_ge(deg, 4)
            dve.tensor_scalar(rs[:, 3:4], rs[:, 3:4], 1.0, None, ALU.add).then_inc(deg, 1)
            dve.tensor_tensor(k.AhatT[:, :], k.adjT[:, :], k.ident[:, :], ALU.add).then_inc(ahat, 1)
            dve.wait_ge(dinv_p, 1)
            dve.tensor_scalar(tmp2[:, :], k.ident[:, :], dinv[:, :], None, ALU.mult).then_inc(dinv_bc, 1)
            dve.wait_ge(ahat, 1)
            dve.tensor_scalar(k.AhatT[:, :], k.AhatT[:, :], dinv[:, :], None, ALU.mult).then_inc(ahat, 1)
            dve.wait_ge(diag_ready, 1)
            dve.tensor_copy(k.diag_bc[:, :], bank_dg[:, 0:P])
            dve.wait_ge(diag_ready, 2)
            dve.wait_ge(ahat, 2)
            dve.tensor_tensor(k.AhatT[:, :], bank_di[:, 0:P], k.AhatT[:, :], ALU.mult).then_inc(ahat, 1)
            for c in range(CH):
                dve.wait_ge(x_in[c], 16)
                with dve.Fori(0, CB // TB) as i:
                    last = stats_tile(dve, k, c * CB + i * TB)
            last.then_inc(stats_done, 1)


def stage_layer0(k, ctx):
    nc, X = k.nc, k.X
    S = 2
    sem = lambda n: k.sem(n)
    sb = lambda n, s: ctx.enter_context(nc.sbuf_tensor(n, s, F32))
    h = each(S, lambda s: sb(f"l0_h{s}", [P, TB, P]))
    Z0 = each(S, lambda s: sb(f"l0_z0{s}", [P, TB, P]))
    Z12 = each(S, lambda s: sb(f"l0_z12{s}", [P, TB, 2, P]))
    psT, psA, psB, psO = k.bank[0:2], k.bank[2:4], k.bank[4:6], k.bank[6:8]
    h_ready = each(S, lambda s: sem(f"l0_h_ready{s}"))
    T_ready, AB_ready = each(S, lambda s: sem(f"l0_T_ready{s}")), each(S, lambda s: sem(f"l0_AB_ready{s}"))
    Z0_ready, Z12_ready = each(S, lambda s: sem(f"l0_Z0_ready{s}")), each(S, lambda s: sem(f"l0_Z12_ready{s}"))
    out_ready, biased, updated = (each(S, lambda s: sem(f"l0_{n}{s}")) for n in ("out_ready", "biased", "updated"))
    coef_dve, coef_pool, coef_ready = layernorm_coefficients(k, ctx, "l0")
    n_it = k.B // TB // S

    with nc.Block() as block:
        @block.gpsimd
        def _(pool):
            coef_pool(pool)
            with pool.Fori(0, n_it) as i:
                for s in range(S):
                    b0 = (i * S + s) * TB
                    pool.wait_ge(h_ready[s], i + 1)
                    pool.tensor_tensor(out=X[:, bass.ds(b0, TB), :], in0=X[:, bass.ds(b0, TB), :],
                                       in1=k.rows[:, R_L0:R_L0 + 1, :].broadcast_to([P, TB, P]),
                                       op=ALU.add).then_inc(biased[s], 1)

        @block.scalar
        def _(act):
            act.wait_ge(coef_ready, 1)
            with act.Fori(0, n_it) as i:
                for s in range(S):
                    normalise_tile(act, k, h[s], (i * S + s) * TB).then_inc(h_ready[s], 1)
                for s in range(S):
                    act.wait_ge(AB_ready[s], i + 1)
                    act.activation(Z12[s][:, 0:2, :, :], psA[s][:, :], ACT.Copy)
                    act.activation(Z12[s][:, 2:4, :, :], psB[s][:, :], ACT.Copy).then_inc(Z12_ready[s], 1)

        @block.tensor
        def _(pe):
            with pe.Fori(0, n_it) as i:
                for s in range(S):
                    pe.wait_ge(h_ready[s], i + 1)
                    for j in range(TB):
                        last = pe.transpose(psT[s][:, j * P:(j + 1) * P], h[s][:, j, :], k.ident[:, :])
                    last.then_inc(T_ready[s], 1)
                    for j in range(TB):
                        ps = (psA, psB)[j // 2][s]
                        last = pe.matmul(ps[:, (j % 2) * 2 * P:(j % 2 + 1) * 2 * P], h[s][:, j, :],
                                         k.A12T[:, :, :], start=True, stop=True)
                        if j == TB - 1:
                            last.then_inc(AB_ready[s], 1)
                for s in range(S):
                    pe.wait_ge(Z0_ready[s], i + 1)
                    pe.wait_ge(Z12_ready[s], i + 1)
                    for j in range(TB):
                        o = psO[s][:, j * P:(j + 1) * P]
                        pe.matmul(o, Z0[s][:, j, :], k.W0[:, 0, :], start=True, stop=False)
                        pe.matmul(o, Z12[s][:, j, 0, :], k.W0[:, 1, :], start=False, stop=False)
                        last = pe.matmul(o, Z12[s][:, j, 1, :], k.W0[:, 2, :], start=False, stop=True)
                    last.then_inc(out_ready[s], 1)

        @block.vector
        def _(dve):
            coef_dve(dve)
            with dve.Fori(0, n_it) as i:
                for s in range(S):
                    dve.wait_ge(T_ready[s], i + 1)
                    dve.tensor_tensor(Z0[s][:, :, :], psT[s][:, :].rearrange("p (b n) -> p b n", b=TB),
                                      k.diag_bc[:, :].unsqueeze(1).broadcast_to([P, TB, P]),
                                      ALU.mult).then_inc(Z0_ready[s], 1)
                for s in range(S):
                    b0 = (i * S + s) * TB
                    xt = X[:, bass.ds(b0, TB), :]
                    dve.wait_ge(biased[s], i + 1)
                    dve.wait_ge(out_ready[s], i + 1)
                    dve.tensor_tensor(xt, psO[s][:, :].rearrange("p (b n) -> p b n", b=TB), xt,
                                      ALU.add).then_inc(updated[s], 1)
                    dve.wait_ge(updated[s], i + 1)
                    stats_tile(dve, k, b0)


def stage_gcn_hidden(k, ctx, Y, bn6):
    nc, X = k.nc, k.X
    S = 2
    sem = lambda n: k.sem(n)
    sb = lambda n, s: ctx.enter_context(nc.sbuf_tensor(n, s, F32))
    h = each(S, lambda s: sb(f"l1_h{s}", [P, TB, P]))
    ZT = each(S, lambda s: sb(f"l1_z{s}", [P, TW]))
    psZ, psY0, psY1 = k.bank[0:2], k.bank[2:4], k.bank[4:6]
    h_ready, Z_ready, ZT_ready, Y0_ready, Y1_ready, Y0_stored, Y1_stored = (
        each(S, lambda s: sem(f"l1_{n}{s}")) for n in ("h", "Z", "ZT", "Y0", "Y1", "Y0s", "Y1s"))
    coef_dve, coef_pool, coef_ready = layernorm_coefficients(k, ctx, "l1")
    n_it = k.B // TB // S

    with nc.Block() as block:
        @block.gpsimd
        def _(pool):
            coef_pool(pool)

        @block.scalar
        def _(act):
            act.wait_ge(coef_ready, 1)
            with act.Fori(0, n_it) as i:
                for s in range(S):
                    normalise_tile(act, k, h[s], (i * S + s) * TB).then_inc(h_ready[s], 1)
                for s in range(S):
                    act.wait_ge(Y0_ready[s], i + 1)
                    act.activation(Y[:, 0, bass.ds((i * S + s) * TW, TW)], psY0[s][:, :], ACT.Identity,
                                   bias=k.cols[:, C_B1:C_B1 + 1]).then_inc(Y0_stored[s], 1)

        @block.tensor
        def _(pe):
            with pe.Fori(0, n_it) as i:
                for s in range(S):
                    pe.wait_ge(h_ready[s], i + 1)
                    for j in range(TB):
                        last = pe.matmul(psZ[s][:, j * P:(j + 1) * P], h[s][:, j, :], k.AhatT[:, :],
                                         start=True, stop=True)
                    last.then_inc(Z_ready[s], 1)
                for s in range(S):
                    pe.wait_ge(ZT_ready[s], i + 1)
                    pe.matmul(psY0[s][:, :], k.W1T[:, 0:P], ZT[s][:, :], start=True, stop=True).then_inc(Y0_ready[s], 1)
                    pe.matmul(psY1[s][:, :], k.W1T[:, P:2 * P], ZT[s][:, :], start=True, stop=True).then_inc(Y1_ready[s], 1)

        @block.vector
        def _(dve):
            coef_dve(dve)
            with dve.Fori(0, n_it) as i:
                for s in range(S):
                    dve.wait_ge(Z_ready[s], i + 1)
                    dve.tensor_copy(ZT[s][:, :], psZ[s][:, :]).then_inc(ZT_ready[s], 1)
                for s in range(S):
                    t = i * S + s
                    y0, y1 = (Y[:, c, bass.ds(t * TW, TW)] for c in range(2))
                    dve.wait_ge(Y1_ready[s], i + 1)
                    dve.tensor_scalar(y1, psY1[s][:, :], k.cols[:, C_B1 + 1:C_B1 + 2], None,
                                      ALU.add).then_inc(Y1_stored[s], 1)
                    dve.wait_ge(Y0_stored[s], i + 1)
                    dve.bn_stats(bn6[:, 0, bass.ds(t, 1), :], y0)
                    dve.wait_ge(Y1_stored[s], i + 1)
                    dve.bn_stats(bn6[:, 1, bass.ds(t, 1), :], y1)


def batchnorm_coefficients(k, ctx, name, bn6, halves, c_gamma, c_beta, coef):
    nc = k.nc
    mv = ctx.enter_context(nc.sbuf_tensor(f"{name}_mv", [P, halves, 2], F32))
    sem = lambda n: k.sem(f"{name}_{n}")
    aggregated, shifted, powed, scaled, ready = (sem(n) for n in ("aggr", "shift", "pow", "scale", "bn_ready"))

    def on_vector(dve):
        for c in range(halves):
            last = dve.bn_aggr(mv[:, c, :], bn6[:, c, :, :])
        last.then_inc(aggregated, 1)
        dve.wait_ge(aggregated, 1)
        dve.tensor_scalar(mv[:, :, 1], mv[:, :, 1], EPS, None, ALU.add).then_inc(shifted, 1)
        dve.wait_ge(powed, 1)
        dve.tensor_tensor(coef[:, :, 0], k.cols[:, c_gamma:c_gamma + halves], mv[:, :, 1], ALU.mult).then_inc(scaled, 1)
        dve.wait_ge(scaled, 1)
        dve.tensor_tensor(mv[:, :, 0], mv[:, :, 0], coef[:, :, 0], ALU.mult).then_inc(scaled, 1)
        dve.wait_ge(scaled, 2)
        dve.tensor_tensor(coef[:, :, 1], k.cols[:, c_beta:c_beta + halves], mv[:, :, 0], ALU.subtract).then_inc(ready, 1)

    def on_pool(pool):
        pool.wait_ge(shifted, 1)
        pool.tensor_tensor(out=mv[:, :, 1], in0=mv[:, :, 1], in1=k.mhalf[:, 0:halves], op=ALU.pow).then_inc(powed, 1)

    return on_vector, on_pool, ready


def stage_gcn_out(k, ctx, Y, bn6, bno6):
    nc = k.nc
    S = 2
    sem = lambda n: k.sem(n)
    sb = lambda n, s: ctx.enter_context(nc.sbuf_tensor(n, s, F32))
    h2 = each(S, lambda s: sb(f"l1b_h{s}", [P, 2, TW]))
    coef = sb("l1b_coef", [P, 2, 2])
    psO = k.bank[0:2]
    h2_ready, O_ready, O_stored = (each(S, lambda s: sem(f"l1b_{n}{s}")) for n in ("h", "O", "Os"))
    coef_dve, coef_pool, coef_ready = batchnorm_coefficients(k, ctx, "bn1", bn6, 2, C_G1, C_BE1, coef)
    h2_free = each(S, lambda s: sem(f"l1b_free{s}"))
    n_it = k.B // TB // S

    with nc.Block() as block:
        @block.gpsimd
        def _(pool):
            coef_pool(pool)

        @block.scalar
        def _(act):
            act.wait_ge(coef_ready, 1)
            with act.Fori(0, n_it) as i:
                for s in range(S):
                    act.wait_ge(h2_free[s], i + 1)
                    for c in range(2):
                        last = act.activation(h2[s][:, c, :], Y[:, c, bass.ds((i * S + s) * TW, TW)], ACT.Relu,
                                              bias=coef[:, c, 1:2], scale=coef[:, c, 0:1])
                    last.then_inc(h2_ready[s], 1)

        @block.tensor
        def _(pe):
            with pe.Fori(0, n_it) as i:
                for s in range(S):
                    pe.wait_ge(h2_ready[s], i + 1)
                    pe.matmul(psO[s][:, :], k.W2T[:, 0, :], h2[s][:, 0, :], start=True, stop=False)
                    pe.matmul(psO[s][:, :], k.W2T[:, 1, :], h2[s][:, 1, :], start=False, stop=True).then_inc(O_ready[s], 1)

        @block.vector
        def _(dve):
            coef_dve(dve)
            for s in range(S):
                dve.sem_inc(h2_free[s], 1)
            with dve.Fori(0, n_it) as i:
                for s in range(S):
                    t = i * S + s
                    o = Y[:, 0, bass.ds(t * TW, TW)]
                    dve.wait_ge(O_ready[s], i + 1)
                    dve.tensor_scalar(o, psO[s][:, :], k.cols[:, C_B2:C_B2 + 1], None, ALU.add).then_inc(O_stored[s], 1)
                    dve.wait_ge(O_stored[s], i + 1)
                    dve.bn_stats(bno6[:, 0, bass.ds(t, 1), :], o).then_inc(h2_free[s], 1)


def stage_gcn_residual(k, ctx, Y, bno6):
    nc = k.nc
    coef = ctx.enter_context(nc.sbuf_tensor("l1c_coef", [P, 1, 2], F32))
    coef_dve, coef_pool, coef_ready = batchnorm_coefficients(k, ctx, "bn2", bno6, 1, C_G2, C_BE2, coef)
    add_transposed(k, ctx, "l1c", lambda t: Y[:, 0, bass.ds(t * TW, TW)],
                   dict(bias=coef[:, 0, 1:2], scale=coef[:, 0, 0:1]), (coef_dve, coef_pool, coef_ready))


def add_transposed(k, ctx, name, source, affine, coefs=None):
    nc, X = k.nc, k.X
    S = 2
    sem = lambda n: k.sem(n)
    o = each(S, lambda s: ctx.enter_context(nc.sbuf_tensor(f"{name}_o{s}", [P, TW], F32)))
    psR = k.bank[0:2]
    o_ready, R_ready, updated, slot_free = (each(S, lambda s: sem(f"{name}_{n}{s}")) for n in ("o", "R", "upd", "free"))
    n_it = k.B // TB // S

    with nc.Block() as block:
        if coefs:
            @block.gpsimd
            def _(pool):
                coefs[1](pool)

        @block.scalar
        def _(act):
            if coefs:
                act.wait_ge(coefs[2], 1)
            with act.Fori(0, n_it) as i:
                for s in range(S):
                    act.wait_ge(slot_free[s], i + 1)
                    act.activation(o[s][:, :], source(i * S + s), ACT.Identity, **affine).then_inc(o_ready[s], 1)

        @block.tensor
        def _(pe):
            with pe.Fori(0, n_it) as i:
                for s in range(S):
                    pe.wait_ge(o_ready[s], i + 1)
                    for j in range(TB):
                        last = pe.transpose(psR[s][:, j * P:(j + 1) * P], o[s][:, j * P:(j + 1) * P], k.ident[:, :])
                    last.then_inc(R_ready[s], 1)

        @block.vector
        def _(dve):
            if coefs:
                coefs[0](dve)
            for s in range(S):
                dve.sem_inc(slot_free[s], 1)
            with dve.Fori(0, n_it) as i:
                for s in range(S):
                    b0 = (i * S + s) * TB
                    xt = X[:, bass.ds(b0, TB), :]
                    dve.wait_ge(R_ready[s], i + 1)
                    dve.tensor_tensor(xt, psR[s][:, :].rearrange("p (b n) -> p b n", b=TB), xt,
                                      ALU.add).then_inc(updated[s], 1)
                    dve.wait_ge(updated[s], i + 1)
                    stats_tile(dve, k, b0).then_inc(slot_free[s], 1)


def stage_conv(k, ctx, HT):
    nc = k.nc
    S = 4
    sem = lambda n: k.sem(n)
    sb = lambda n, s: ctx.enter_context(nc.sbuf_tensor(n, s, F32))
    h, hT, V, G, V2 = (each(S, lambda s: sb(f"l2_{n}{s}", [P, TB, P])) for n in ("h", "hT", "V", "G", "V2"))
    names = ("h", "Tp", "hT", "Vp", "V", "Gp", "G", "V2p", "V2", "Hp", "H")
    R = {n: each(S, lambda s: sem(f"l2_{n}{s}")) for n in names}
    coef_dve, coef_pool, coef_ready = layernorm_coefficients(k, ctx, "l2")
    n_it = k.B // TB // S
    even, odd = k.bank[0:4], k.bank[4:8]
    as_tile = lambda ps: ps[:, :].rearrange("p (b n) -> p b n", b=TB)

    with nc.Block() as block:
        @block.gpsimd
        def _(pool):
            coef_pool(pool)

        @block.scalar
        def _(act):
            act.wait_ge(coef_ready, 1)
            with act.Fori(0, n_it) as i:
                for s in range(S):
                    normalise_tile(act, k, h[s], (i * S + s) * TB).then_inc(R["h"][s], 1)
                for s in range(S):
                    act.wait_ge(R["Gp"][s], i + 1)
                    act.activation(G[s][:, :, :], as_tile(even[s]), ACT.Relu).then_inc(R["G"][s], 1)
                for s in range(S):
                    act.wait_ge(R["Hp"][s], i + 1)
                    act.activation(HT[:, bass.ds((i * S + s) * TW, TW)], even[s][:, :], ACT.Relu).then_inc(R["H"][s], 1)

        @block.tensor
        def _(pe):
            with pe.Fori(0, n_it) as i:
                for s in range(S):
                    pe.wait_ge(R["h"][s], i + 1)
                    for j in range(TB):
                        last = pe.transpose(even[s][:, j * P:(j + 1) * P], h[s][:, j, :], k.ident[:, :])
                    last.then_inc(R["Tp"][s], 1)
                for s in range(S):
                    pe.wait_ge(R["hT"][s], i + 1)
                    for j in range(TB):
                        last = pe.matmul(odd[s][:, j * P:(j + 1) * P], hT[s][:, j, :], k.Wg[:, 0, :], start=True, stop=True)
                    last.then_inc(R["Vp"][s], 1)
                for s in range(S):
                    pe.wait_ge(R["V"][s], i + 1)
                    for j in range(TB):
                        last = pe.matmul(even[s][:, j * P:(j + 1) * P], V[s][:, j, :], k.adjT[:, :], start=True, stop=True)
                    last.then_inc(R["Gp"][s], 1)
                for s in range(S):
                    pe.wait_ge(R["G"][s], i + 1)
                    for j in range(TB):
                        last = pe.matmul(odd[s][:, j * P:(j + 1) * P], G[s][:, j, :], k.Wg[:, 1, :], start=True, stop=True)
                    last.then_inc(R["V2p"][s], 1)
                for s in range(S):
                    pe.wait_ge(R["V2"][s], i + 1)
                    for j in range(TB):
                        last = pe.matmul(even[s][:, j * P:(j + 1) * P], V2[s][:, j, :], k.adjT[:, :], start=True, stop=True)
                    last.then_inc(R["Hp"][s], 1)

        @block.vector
        def _(dve):
            coef_dve(dve)
            with dve.Fori(0, n_it) as i:
                for s in range(S):
                    dve.wait_ge(R["Tp"][s], i + 1)
                    dve.tensor_copy(hT[s][:, :, :], as_tile(even[s])).then_inc(R["hT"][s], 1)
                for src, dst, row in (("Vp", "V", R_G0), ("V2p", "V2", R_G1)):
                    buf = V if dst == "V" else V2
                    for s in range(S):
                        dve.wait_ge(R[src][s], i + 1)
                        dve.tensor_tensor(buf[s][:, :, :], as_tile(odd[s]),
                                          k.rows[:, row:row + 1, :].broadcast_to([P, TB, P]),
                                          ALU.add).then_inc(R[dst][s], 1)


GATE_I, GATE_F, GATE_G, GATE_O = range(4)


def split_float32(eng, full, hi, lo, copied, copied_count, tally=None):
    eng.tensor_copy(hi, full).then_inc(copied, 1)
    eng.wait_ge(copied, copied_count)
    if tally is not None:
        eng.sem_inc(tally, 1)
    return eng.tensor_tensor(out=lo, in0=full, in1=hi.bitcast(F32), op=ALU.subtract)


def stage_lstm(k, ctx, HT, p, bufs, sems, used):
    nc, B = k.nc, k.B
    S = 2
    nw = P // p
    nb = max(n for n in (4, 8, 16) if n * nw <= TW)
    N = nb * nw
    n_it = B // nb // S
    bias = k.lstm_bias[:, p - 1, :]
    gates, cell, hid, hid_hi, hid_lo, x_hi, x_lo = (bufs[n] for n in ("gates", "cell", "hid", "hid_hi", "hid_lo", "x_hi", "x_lo"))
    done, act_out, cell_ready, tanh_ready, h_ready, hh_ready, hl_ready, fc_ready, ig_ready, xh_ready, xl_ready = (
        sems[n] for n in ("done", "act", "cell", "tanh", "h", "hh", "hl", "fc", "ig", "xh", "xl"))
    u_done, u_seq, u_rec = used["done"], used["seq"], used["rec"]
    windows = HT[:, :].rearrange("h (b t) -> h b t", t=P)
    order = [GATE_G, GATE_I, GATE_F, GATE_O]

    def node(b0, step):
        if p == 1:
            return windows[:, bass.ds(b0, nb), :]
        return windows[:, bass.ds(b0, nb), 0:nw * p].rearrange("h b (w q) -> h b w q", q=p)[:, :, :, step]

    as3 = lambda ap: ap.rearrange("h (b w) -> h b w", w=nw)

    def n_gate(g, i, step):
        return u_done[g] + (i * (p - 1) + step if g == GATE_F else i * p + step + 1)

    def n_seq(i, step):
        return u_seq + i * p + step + 1

    def n_rec(i, step):
        return u_rec + i * (p - 1) + step

    def gates_of(step):
        return [g for g in order if step or g != GATE_F]

    with nc.Block() as block:
        @block.gpsimd
        def _(pool):
            with pool.Fori(0, n_it) as i:
                for step in range(p):
                    for s in range(S):
                        x = node((i * S + s) * nb, step)
                        pool.wait_ge(sems["x_free"][s], n_seq(i, step))
                        split_float32(pool, x, as3(x_hi[s][:, 0:N]), as3(x_lo[s][:, 0:N]),
                                      xh_ready[s], n_seq(i, step), sems["x_tally"][s]).then_inc(xl_ready[s], 1)

        @block.tensor
        def _(pe):
            if p == 1:
                for s in range(S):
                    pe.sem_inc(sems["x_free"][s], 1)

            def product(out, W, g, v_hi, v_lo, start, stop):
                hi, lo = (W[n][:, p - 1, g * P:(g + 1) * P] for n in range(2))
                pe.matmul(out, hi, v_hi[:, 0:N], start=start, stop=False)
                pe.matmul(out, lo, v_hi[:, 0:N], start=False, stop=False)
                return pe.matmul(out, hi, v_lo[:, 0:N], start=False, stop=stop)

            with pe.Fori(0, n_it) as i:
                for step in range(p):
                    for s in range(S):
                        pe.wait_ge(xl_ready[s], n_seq(i, step))
                        for g in gates_of(step):
                            pe.wait_ge(act_out[s][g], n_gate(g, i, step))
                            last = product(k.bank[4 * s + g][:, 0:N], k.Wih, g, x_hi[s], x_lo[s], True, step == 0)
                            if step == 0 and g != GATE_O:
                                last.then_inc(done[s][g], 1)
                        last.then_inc(sems["x_free"][s], 1)
                        if step == 0:
                            pe.wait_ge(sems["x_free"][s], n_seq(i, step) + 1)
                            pe.sem_inc(done[s][GATE_O], 1)
                        else:
                            pe.wait_ge(hl_ready[s], n_rec(i, step))
                            for g in gates_of(step):
                                product(k.bank[4 * s + g][:, 0:N], k.Whh, g, hid_hi[s], hid_lo[s],
                                        False, True).then_inc(done[s][g], 1)

        @block.scalar
        def _(act):
            if p == 1:
                for s in range(S):
                    for g in range(4):
                        act.sem_inc(act_out[s][g], 1)
            with act.Fori(0, n_it) as i:
                for step in range(p):
                    for s in range(S):
                        for g in gates_of(step):
                            act.wait_ge(done[s][g], n_gate(g, i, step))
                            act.activation(gates[s][:, g, 0:N], k.bank[4 * s + g][:, 0:N],
                                           ACT.Tanh if g == GATE_G else ACT.Sigmoid,
                                           bias=bias[:, g:g + 1]).then_inc(act_out[s][g], 1)
                        act.wait_ge(cell_ready[s], n_seq(i, step))
                        act.activation(gates[s][:, GATE_G, 0:N], cell[s][:, 0:N], ACT.Tanh).then_inc(tanh_ready[s], 1)

        @block.vector
        def _(dve):
            with dve.Fori(0, n_it) as i:
                for step in range(p):
                    for s in range(S):
                        G = lambda g: gates[s][:, g, 0:N]
                        c = cell[s][:, 0:N]
                        dve.wait_ge(act_out[s][GATE_G], n_gate(GATE_G, i, step) + 1)
                        dve.wait_ge(act_out[s][GATE_I], n_gate(GATE_I, i, step) + 1)
                        if step == 0:
                            dve.tensor_tensor(c, G(GATE_I), G(GATE_G), ALU.mult).then_inc(cell_ready[s], 1)
                        else:
                            dve.tensor_tensor(G(GATE_I), G(GATE_I), G(GATE_G), ALU.mult).then_inc(ig_ready[s], 1)
                            dve.wait_ge(act_out[s][GATE_F], n_gate(GATE_F, i, step) + 1)
                            dve.tensor_tensor(c, G(GATE_F), c, ALU.mult).then_inc(fc_ready[s], 1)
                            dve.wait_ge(ig_ready[s], n_rec(i, step))
                            dve.wait_ge(fc_ready[s], n_rec(i, step))
                            dve.tensor_tensor(c, G(GATE_I), c, ALU.add).then_inc(cell_ready[s], 1)
                        dve.wait_ge(act_out[s][GATE_O], n_gate(GATE_O, i, step) + 1)
                        dve.wait_ge(tanh_ready[s], n_seq(i, step))
                        if step == p - 1:
                            dve.tensor_tensor(node((i * S + s) * nb, step), as3(G(GATE_O)), as3(G(GATE_G)), ALU.mult)
                        else:
                            hd = hid[s][:, 0:N]
                            dve.tensor_tensor(hd, G(GATE_O), G(GATE_G), ALU.mult).then_inc(h_ready[s], 1)
                            dve.wait_ge(h_ready[s], n_rec(i, step + 1))
                            split_float32(dve, hd, hid_hi[s][:, 0:N], hid_lo[s][:, 0:N], hh_ready[s],
                                          n_rec(i, step + 1)).then_inc(hl_ready[s], 1)

    used["seq"] += n_it * p
    used["rec"] += n_it * (p - 1)
    for g in range(4):
        used["done"][g] += n_it * (p - 1 if g == GATE_F else p)


def stage_lstm_weights(k, ctx, d):
    nc = k.nc
    raw = each(2, lambda s: ctx.enter_context(nc.sbuf_tensor(f"w_raw{s}", [P, 4, 4 * P], F32)))
    loaded, copied, split = each(2, lambda s: k.sem(f"lstm_w_in{s}")), k.sem("w_copied"), k.sem("w_split")
    with nc.Block() as block:
        @block.sync
        def _(sp):
            sp.dma_start(raw[0][:, :, :], d["WihT"].rearrange("p d g -> d p g")).then_inc(loaded[0], 16)
            sp.dma_start(raw[1][:, :, :], d["WhhT"].rearrange("p d g -> d p g")).then_inc(loaded[1], 16)

        @block.vector
        def _(dve):
            dve.tensor_tensor(k.lstm_bias[:, :, :].rearrange("h p g -> h (p g)"), k.cols[:, C_BIH:C_BIH + 16],
                              k.cols[:, C_BHH:C_BHH + 16], ALU.add)
            for n, W in enumerate((k.Wih, k.Whh)):
                dve.wait_ge(loaded[n], 16)
                split_float32(dve, raw[n][:, :, :], W[0][:, :, :], W[1][:, :, :], copied, n + 1)


def stage_edges(k, ctx, d, e):
    nc = k.nc
    E, EC = k.E, k.E // P
    sem = lambda n: k.sem(n)
    sb = lambda n, s, t=F32: ctx.enter_context(nc.sbuf_tensor(n, s, t))
    loaded, w_in, iotas, step, pe_done, lned, evac = (sem(n) for n in (
        "edges_in", "l3_w_in", "iotas", "edge_step", "edge_pe", "edge_ln", "edge_evac"))
    row_i, col_i = sb("edge_row_i", [P, 2, E], I32), sb("edge_col_i", [P, 2, EC], I32)
    row, col = sb("edge_row", [P, 2, E]), sb("edge_col", [P, 2, EC])
    order_row, order_col = sb("order_row", [P, E]), sb("order_col", [P, EC])
    key_row, key_col = sb("key_row", [P, E]), sb("key_col", [P, EC])
    iota_part, rank = sb("iota_part", [P, 1]), sb("rank", [P, EC])
    less, perm, colbc = sb("less", [P, E]), sb("perm", [P, EC, E]), sb("colbc", [P, 2, EC, P])
    sorted_row = sb("sorted_row", [P, 2, E])
    weight = sb("edge_weight", [P, E])
    psS, psD, psU, psW, psT = k.bank[0:5]

    with nc.Block() as block:
        @block.sync
        def _(sp):
            for n, name in enumerate(("src", "dst")):
                sp.dma_start(row_i[:, n, :], d[name].rearrange("(a e) -> a e", a=1).partition_broadcast(P)
                             .rearrange("p a e -> p (a e)")).then_inc(loaded, 16)
                sp.dma_start(col_i[:, n, :], d[name + "_col"]).then_inc(loaded, 16)
            sp.dma_start(e.Wqv[:, :], d["Wqv"]).then_inc(w_in, 16)
            sp.dma_start(e.WoT[:, :], d["WoT"]).then_inc(w_in, 16)
            sp.dma_start(e.a_col[:, :], d["a_col"]).then_inc(w_in, 16)
            sp.wait_ge(w_in, 3 * 16)

        @block.gpsimd
        def _(pool):
            pool.iota(order_row[:, :], [[1, E]], base=0, channel_multiplier=0, allow_small_or_imprecise_dtypes=True).then_inc(iotas, 1)
            pool.iota(order_col[:, :], [[P, EC]], base=0, channel_multiplier=1, allow_small_or_imprecise_dtypes=True).then_inc(iotas, 1)
            pool.iota(iota_part[:, :], [[0, 1]], base=0, channel_multiplier=1, allow_small_or_imprecise_dtypes=True).then_inc(iotas, 1)
            pool.wait_ge(w_in, 3 * 16)
            pool.affine_select(out=e.a_blk[:, :], in_=e.a_col[:, 0:1].broadcast_to([P, k.HEADS]), compare_op=ALU.is_ge,
                               fill=0.0, base=0, pattern=[[-k.DH, k.HEADS]], channel_multiplier=1).then_inc(iotas, 1)
            pool.wait_ge(iotas, 4)
            pool.affine_select(out=e.a_blk[:, :], in_=e.a_blk[:, :], compare_op=ALU.is_gt,
                               fill=0.0, base=k.DH, pattern=[[k.DH, k.HEADS]], channel_multiplier=-1).then_inc(iotas, 1)

        @block.vector
        def _(dve):
            n = 0

            def chained(ins):
                nonlocal n
                n += 1
                ins.then_inc(step, 1)
                dve.wait_ge(step, n)

            dve.wait_ge(loaded, 4 * 16)
            dve.wait_ge(iotas, 3)
            dve.tensor_copy(row[:, :, :], row_i[:, :, :])
            chained(dve.tensor_copy(col[:, :, :], col_i[:, :, :]))
            dve.scalar_tensor_tensor(key_row[:, :], row[:, 0, :], float(E), order_row[:, :], ALU.mult, ALU.add)
            dve.tensor_copy(colbc[:, :, :, :], col[:, :, :].unsqueeze(3).broadcast_to([P, 2, EC, P]))
            chained(dve.scalar_tensor_tensor(key_col[:, :], col[:, 0, :], float(E), order_col[:, :], ALU.mult, ALU.add))
            for c in range(EC):
                chained(dve.tensor_scalar(less[:, :], key_row[:, :], key_col[:, c:c + 1], 0.0, ALU.is_lt, ALU.add,
                                          accum_out=rank[:, c:c + 1]))
            for c in range(EC):
                dve.tensor_scalar(perm[:, c, :], order_row[:, :], rank[:, c:c + 1], None, ALU.is_equal).then_inc(evac, 1)
            dve.wait_ge(pe_done, 2)
            dve.tensor_copy(sorted_row[:, 0, :], psS[:, 0:E])
            chained(dve.tensor_copy(sorted_row[:, 1, :], psD[:, 0:E]))
            dve.tensor_scalar(e.ST[:, :], sorted_row[:, 0, :], iota_part[:, :], None, ALU.is_equal)
            chained(dve.tensor_scalar(e.DT[:, :], sorted_row[:, 1, :], iota_part[:, :], None, ALU.is_equal))
            dve.tensor_tensor(e.PT[:, :], e.ST[:, :], e.DT[:, :], ALU.add).then_inc(evac, 1)
            chained(dve.memset(e.cont[:, :], 0.0))
            chained(dve.tensor_tensor(e.cont[:, 1:E], sorted_row[:, 0, 1:E], sorted_row[:, 0, 0:E - 1], ALU.is_equal))
            dve.tensor_scalar(e.reset[:, :], e.cont[:, :], -1.0, BIG, ALU.add, ALU.mult)
            chained(dve.tensor_scalar(e.is_last[:, :], e.cont[:, 1:E + 1], -1.0, 1.0, ALU.mult, ALU.add))
            dve.wait_ge(pe_done, 3)
            dve.tensor_tensor(weight[:, :], psU[:, 0:E], e.ST[:, :], ALU.mult).then_inc(evac, 1)
            dve.wait_ge(pe_done, 5)
            dve.tensor_copy(e.S1[:, :, :], psT[:, 0:EC * P].rearrange("p (c n) -> p c n", c=EC))
            dve.wait_ge(pe_done, 4)
            chained(dve.tensor_scalar(weight[:, :], psW[:, 0:E], EPS_EDGE, None, ALU.add))
            dve.sem_inc(evac, 1)

        @block.tensor
        def _(pe):
            pe.wait_ge(evac, EC)
            for n, ps in enumerate((psS, psD)):
                for c in range(EC):
                    last = pe.matmul(ps[:, 0:E], colbc[:, n, c, :], perm[:, c, :], start=c == 0, stop=c == EC - 1)
                last.then_inc(pe_done, 1)
            pe.wait_ge(evac, EC + 1)
            pe.matmul(psU[:, 0:E], k.adjT[:, :], e.DT[:, :], start=True, stop=True).then_inc(pe_done, 1)
            pe.wait_ge(evac, EC + 2)
            pe.matmul(psW[:, 0:E], k.ones[:, :], weight[:, :], start=True, stop=True).then_inc(pe_done, 1)
            for c in range(EC):
                last = pe.transpose(psT[:, c * P:(c + 1) * P], e.ST[:, c * P:(c + 1) * P], k.ident[:, :])
            last.then_inc(pe_done, 1)

        @block.scalar
        def _(act):
            act.wait_ge(evac, EC + 3)
            act.activation(e.log_w[:, :], weight[:, :], ACT.Ln)


def stage_scores(k, ctx, Xv, scores, e):
    nc = k.nc
    S = 2
    E, EC, HEADS = k.E, k.E // P, k.HEADS
    sem = lambda n: k.sem(n)
    sb = lambda n, s: ctx.enter_context(nc.sbuf_tensor(n, s, F32))
    h, hT, Xq = (each(S, lambda s: sb(f"l3_{n}{s}", [P, TB, P])) for n in ("h", "hT", "Xq"))
    L = each(S, lambda s: sb(f"l3_L{s}", [P, TB, E]))
    names = ("h", "Tp", "hT", "QV", "Qa", "Qb", "Gp", "Lc0", "Lc1", "L", "sc", "sv")
    R = {n: each(S, lambda s: sem(f"l3_{n}{s}")) for n in names}
    coef_dve, coef_pool, coef_ready = layernorm_coefficients(k, ctx, "l3")
    n_it = k.B // TB // S
    psT, psA, psB = k.bank[0:2], k.bank[2:4], k.bank[4:6]

    with nc.Block() as block:
        @block.gpsimd
        def _(pool):
            coef_pool(pool)

        @block.scalar
        def _(act):
            act.wait_ge(coef_ready, 1)
            with act.Fori(0, n_it) as i:
                for s in range(S):
                    normalise_tile(act, k, h[s], (i * S + s) * TB).then_inc(R["h"][s], 1)
                for s in range(S):
                    b0 = (i * S + s) * TB
                    act.wait_ge(R["QV"][s], i + 1)
                    qv = psA[s][:, :].rearrange("p (b t c) -> p b t c", b=2, t=2)
                    act.activation(Xq[s][:, 0:2, :], qv[:, :, 0, :], ACT.Copy)
                    act.activation(Xv[:, bass.ds(b0, 2), :], qv[:, :, 1, :], ACT.Copy).then_inc(R["Qa"][s], 1)
                for s in range(S):
                    act.wait_ge(R["Gp"][s], i + 1)
                    act.activation(L[s][:, 0:2, :], psA[s][:, :], ACT.Copy).then_inc(R["Lc0"][s], 1)
                    act.activation(L[s][:, 2:4, :], psB[s][:, :], ACT.Copy).then_inc(R["Lc1"][s], 1)

        @block.tensor
        def _(pe):
            with pe.Fori(0, n_it) as i:
                for s in range(S):
                    pe.wait_ge(R["h"][s], i + 1)
                    pe.wait_ge(R["sv"][s], i + 1)
                    for j in range(TB):
                        last = pe.transpose(psT[s][:, j * P:(j + 1) * P], h[s][:, j, :], k.ident[:, :])
                    last.then_inc(R["Tp"][s], 1)
                for s in range(S):
                    pe.wait_ge(R["hT"][s], i + 1)
                    for j in range(TB):
                        ps = (psA, psB)[j // 2][s]
                        last = pe.matmul(ps[:, (j % 2) * 2 * P:(j % 2 + 1) * 2 * P], hT[s][:, j, :], e.Wqv[:, :],
                                         start=True, stop=True)
                    last.then_inc(R["QV"][s], 1)
                for s in range(S):
                    pe.wait_ge(R["Qa"][s], i + 1)
                    pe.wait_ge(R["Qb"][s], i + 1)
                    for j in range(TB):
                        ps = (psA, psB)[j // 2][s]
                        last = pe.matmul(ps[:, (j % 2) * E:(j % 2 + 1) * E], Xq[s][:, j, :], e.PT[:, :],
                                         start=True, stop=True)
                    last.then_inc(R["Gp"][s], 1)
                for s in range(S):
                    pe.wait_ge(R["L"][s], i + 1)
                    for c in range(EC):
                        for j in range(TB):
                            at = (c * TB + j) * HEADS
                            last = pe.matmul(psT[s][:, at:at + HEADS], L[s][:, j, c * P:(c + 1) * P], e.a_blk[:, :],
                                             start=True, stop=True)
                    last.then_inc(R["sc"][s], 1)

        @block.vector
        def _(dve):
            coef_dve(dve)
            for s in range(S):
                dve.sem_inc(R["sv"][s], 1)
            with dve.Fori(0, n_it) as i:
                for s in range(S):
                    dve.wait_ge(R["Tp"][s], i + 1)
                    dve.tensor_copy(hT[s][:, :, :], psT[s][:, :].rearrange("p (b n) -> p b n", b=TB)).then_inc(R["hT"][s], 1)
                for s in range(S):
                    b0 = (i * S + s) * TB
                    dve.wait_ge(R["QV"][s], i + 1)
                    qv = psB[s][:, :].rearrange("p (b t c) -> p b t c", b=2, t=2)
                    dve.tensor_copy(Xq[s][:, 2:4, :], qv[:, :, 0, :])
                    dve.tensor_copy(Xv[:, bass.ds(b0 + 2, 2), :], qv[:, :, 1, :]).then_inc(R["Qb"][s], 1)
                for s in range(S):
                    for half in range(2):
                        l = L[s][:, 2 * half:2 * half + 2, :]
                        dve.wait_ge(R[f"Lc{half}"][s], i + 1)
                        last = dve.scalar_tensor_tensor(l, l, 0.2, l, ALU.mult, ALU.max)
                    last.then_inc(R["L"][s], 1)
                for s in range(S):
                    t = i * S + s
                    dve.wait_ge(R["sc"][s], i + 1)
                    dve.tensor_copy(scores[:, :, bass.ds(t * TB * HEADS, TB * HEADS)],
                                    psT[s][:, 0:EC * TB * HEADS].rearrange("p (c x) -> p c x", c=EC)).then_inc(R["sv"][s], 1)


def stage_softmax(k, ctx, scores, e):
    nc = k.nc
    E, EC = k.E, k.E // P
    NQ = k.B * k.HEADS // P
    sem = lambda n: k.sem(n)
    sb = lambda n, s: ctx.enter_context(nc.sbuf_tensor(n, s, F32))
    r, m, w = (each(NQ, lambda q: sb(f"sm_{n}{q}", [P, E])) for n in ("r", "m", "w"))
    turned, shifted, exped, attn_ready, back, step = (sem(f"sm_{n}") for n in ("turned", "shifted", "exp", "attn", "back", "step"))

    with nc.Block() as block:
        @block.tensor
        def _(pe):
            for q in range(NQ):
                for c in range(EC):
                    last = pe.transpose(k.bank[q][:, c * P:(c + 1) * P], scores[:, c, q * P:(q + 1) * P], k.ident[:, :])
                last.then_inc(turned, 1)
            for q in range(NQ):
                pe.wait_ge(attn_ready, q + 1)
                for c in range(EC):
                    last = pe.transpose(k.bank[4 + q][:, c * P:(c + 1) * P], r[q][:, c * P:(c + 1) * P], k.ident[:, :])
                last.then_inc(back, 1)

        @block.scalar
        def _(act):
            for q in range(NQ):
                act.wait_ge(shifted, q + 1)
                act.activation(r[q][:, :], r[q][:, :], ACT.Exp).then_inc(exped, 1)

        @block.vector
        def _(dve):
            n = 0

            def wave(make):
                nonlocal n
                for q in range(NQ):
                    make(q).then_inc(step, 1)
                n += NQ

            def after(q):
                dve.wait_ge(step, n - NQ + q + 1)

            def score_in(q):
                dve.wait_ge(turned, q + 1)
                return dve.tensor_tensor(r[q][:, :], k.bank[q][:, 0:E], e.log_w[:, :], ALU.add)

            def max_forward(q):
                after(q)
                return dve.tensor_tensor_scan(m[q][:, :], e.reset[:, 0:E], r[q][:, :], 0.0, ALU.add, ALU.max)

            def max_backward(q):
                after(q)
                return dve.tensor_tensor_scan(w[q][:, ::-1], e.reset[:, E:0:-1], m[q][:, ::-1], 0.0, ALU.add, ALU.max)

            def subtract_max(q):
                after(q)
                return dve.tensor_tensor(r[q][:, :], r[q][:, :], w[q][:, :], ALU.subtract)

            wave(score_in)
            wave(max_forward)
            wave(max_backward)
            n_before = n
            for q in range(NQ):
                dve.wait_ge(step, n_before - NQ + q + 1)
                dve.tensor_tensor(r[q][:, :], r[q][:, :], w[q][:, :], ALU.subtract).then_inc(shifted, 1)

            def sum_forward(q):
                dve.wait_ge(exped, q + 1)
                return dve.tensor_tensor_scan(m[q][:, :], e.cont[:, 0:E], r[q][:, :], 0.0, ALU.mult, ALU.add)

            def keep_last(q):
                after(q)
                return dve.tensor_tensor(m[q][:, :], m[q][:, :], e.is_last[:, :], ALU.mult)

            def sum_backward(q):
                after(q)
                return dve.tensor_tensor_scan(w[q][:, ::-1], e.cont[:, E:0:-1], m[q][:, ::-1], 0.0, ALU.mult, ALU.add)

            def invert(q):
                after(q)
                return dve.reciprocal(w[q][:, :], w[q][:, :])

            wave(sum_forward)
            wave(keep_last)
            wave(sum_backward)
            wave(invert)
            for q in range(NQ):
                dve.wait_ge(step, n - NQ + q + 1)
                dve.tensor_tensor(r[q][:, :], r[q][:, :], w[q][:, :], ALU.mult).then_inc(attn_ready, 1)
            for q in range(NQ):
                dve.wait_ge(back, q + 1)
                dve.tensor_copy(scores[:, :, q * P:(q + 1) * P],
                                k.bank[4 + q][:, 0:E].rearrange("p (c x) -> p c x", c=EC))


def stage_attend(k, ctx, Xv, attn, e, out):
    nc, X = k.nc, k.X
    S = 2
    EC, HEADS, DH = k.E // P, k.HEADS, k.DH
    sem = lambda n: k.sem(n)
    sb = lambda n, s: ctx.enter_context(nc.sbuf_tensor(n, s, F32))
    Vw, YT = each(S, lambda s: sb(f"at_v{s}", [P, EC, TW])), each(S, lambda s: sb(f"at_y{s}", [P, TB, P]))
    R = {n: each(S, lambda s: sem(f"at_{n}{s}")) for n in ("V0", "V1", "Vw", "Yp", "YT", "Op", "O")}
    stored = sem("out_stored")
    n_it = k.B // TB // S
    psV0, psV1, psY, psO = k.bank[0:2], k.bank[2:4], k.bank[4:6], k.bank[6:8]

    with nc.Block() as block:
        @block.tensor
        def _(pe):
            with pe.Fori(0, n_it) as i:
                for s in range(S):
                    v = Xv[:, bass.ds((i * S + s) * TB, TB), :]
                    pe.matmul(psV0[s][:, :], e.DT[:, 0:P], v, start=True, stop=True).then_inc(R["V0"][s], 1)
                    pe.matmul(psV1[s][:, :], e.DT[:, P:2 * P], v, start=True, stop=True).then_inc(R["V1"][s], 1)
                for s in range(S):
                    pe.wait_ge(R["Vw"][s], i + 1)
                    for j in range(TB):
                        for c in range(EC):
                            last = pe.matmul(psY[s][:, j * P:(j + 1) * P], Vw[s][:, c, j * P:(j + 1) * P], e.S1[:, c, :],
                                             start=c == 0, stop=c == EC - 1)
                    last.then_inc(R["Yp"][s], 1)
                for s in range(S):
                    pe.wait_ge(R["YT"][s], i + 1)
                    for j in range(TB):
                        last = pe.matmul(psO[s][:, j * P:(j + 1) * P], YT[s][:, j, :], e.WoT[:, :], start=True, stop=True)
                    last.then_inc(R["Op"][s], 1)

        @block.scalar
        def _(act):
            with act.Fori(0, n_it) as i:
                for s in range(S):
                    act.wait_ge(R["Yp"][s], i + 1)
                    act.activation(YT[s][:, :, :], psY[s][:, :].rearrange("p (b n) -> p b n", b=TB), ACT.Copy).then_inc(R["YT"][s], 1)

        @block.vector
        def _(dve):
            with dve.Fori(0, n_it) as i:
                for s in range(S):
                    t = i * S + s
                    for c, ps in enumerate((psV0, psV1)):
                        dve.wait_ge(R[f"V{c}"][s], i + 1)
                        w = attn[:, c, bass.ds(t * TB * HEADS, TB * HEADS)]
                        last = dve.tensor_tensor(Vw[s][:, c, :].rearrange("p (x y) -> p x y", y=DH),
                                                 ps[s][:, :].rearrange("p (x y) -> p x y", y=DH),
                                                 w.unsqueeze(2).broadcast_to([P, TB * HEADS, DH]), ALU.mult)
                    last.then_inc(R["Vw"][s], 1)
                for s in range(S):
                    xt = X[:, bass.ds((i * S + s) * TB, TB), :]
                    dve.wait_ge(R["Op"][s], i + 1)
                    dve.tensor_tensor(xt, psO[s][:, :].rearrange("p (b n) -> p b n", b=TB), xt, ALU.add).then_inc(R["O"][s], 1)

        @block.sync
        def _(sp):
            with sp.Fori(0, n_it) as i:
                for s in range(S):
                    b0 = (i * S + s) * TB
                    sp.wait_ge(R["O"][s], i + 1)
                    sp.dma_start(out[:, bass.ds(b0, TB), :], X[:, bass.ds(b0, TB), :]).then_inc(stored, 16)
            sp.wait_ge(stored, n_it * S * 16)


def build(nc, d, out):
    _, B, _ = d["x"].shape
    k, e = Shared(), Shared()
    k.nc, k.B, k.E, k.HEADS = nc, B, d["src"].shape[0], 4
    k.DH = P // k.HEADS
    with ExitStack() as ctx:
        sb = lambda n, s: ctx.enter_context(nc.sbuf_tensor(n, s, F32))
        k.X = sb("X", [P, B, P])
        k.adjT, k.AhatT, k.ident, k.ones = (sb(n, [P, P]) for n in ("adjT", "AhatT", "ident", "ones"))
        k.W1T, k.W2T, k.Wg = sb("W1T", [P, 2 * P]), sb("W2T", [P, 2, P]), sb("Wg", [P, 2, P])
        k.cols, k.rows = sb("cols", [P, NCOLS]), sb("rows", [P, 3, P])
        k.st6, k.rstd, k.nmr, k.mhalf = sb("st6", [P, B, 6]), sb("rstd", [P, B]), sb("nmr", [P, B]), sb("mhalf", [P, B])
        k.bank = each(8, lambda n: ctx.enter_context(nc.psum_tensor(f"bank{n}", [P, TW], F32)))

        with ExitStack() as c0:
            k.W0 = c0.enter_context(nc.sbuf_tensor("W0", [P, 3, P], F32))
            k.A12T = c0.enter_context(nc.sbuf_tensor("A12T", [P, 2, P], F32))
            k.diag_bc = c0.enter_context(nc.sbuf_tensor("diag_bc", [P, P], F32))
            with ExitStack() as c:
                stage_setup(k, c, d)
            with ExitStack() as c:
                stage_layer0(k, c)

        with ExitStack() as c1:
            bn6 = c1.enter_context(nc.sbuf_tensor("bn6", [P, 2, B // TB, 6], F32))
            bno6 = c1.enter_context(nc.sbuf_tensor("bno6", [P, 1, B // TB, 6], F32))
            Y = c1.enter_context(nc.sbuf_tensor("Y", [P, 2, B * P], F32))
            with ExitStack() as c:
                stage_gcn_hidden(k, c, Y, bn6)
            with ExitStack() as c:
                stage_gcn_out(k, c, Y, bn6, bno6)
            with ExitStack() as c:
                stage_gcn_residual(k, c, Y, bno6)

        k.recycle_semaphores()
        with ExitStack() as c2:
            sb2 = lambda n, s: c2.enter_context(nc.sbuf_tensor(n, s, F32))
            HT = sb2("HT", [P, B * P])
            sbr = lambda n, s: c2.enter_context(nc.sbuf_tensor(n, s, F32R))
            k.Wih, k.Whh = ([sbr(f"{n}_{part}", [P, 4, 4 * P]) for part in ("hi", "lo")] for n in ("Wih", "Whh"))
            k.lstm_bias = sb2("lstm_bias", [P, 4, 4])
            with ExitStack() as c:
                stage_conv(k, c, HT)
            with ExitStack() as c:
                stage_lstm_weights(k, c, d)
            with ExitStack() as c:
                bufs = {"gates": each(2, lambda s: c.enter_context(nc.sbuf_tensor(f"gates{s}", [P, 4, TW], F32)))}
                for n in ("cell", "hid", "hid_hi", "hid_lo", "x_hi", "x_lo"):
                    bufs[n] = each(2, lambda s: c.enter_context(nc.sbuf_tensor(f"lstm_{n}{s}", [P, TW], F32R if "_" in n else F32)))
                sems = {n: each(2, lambda s: each(4, lambda g: k.sem(f"lstm_{n}{s}{g}")))
                        for n in ("done", "act")}
                for n in ("cell", "tanh", "h", "hh", "hl", "fc", "ig", "xh", "xl", "x_free", "x_tally"):
                    sems[n] = each(2, lambda s: k.sem(f"lstm_{n}_ready{s}"))
                used = {"done": [0] * 4, "seq": 0, "rec": 0}
                for p in range(1, 5):
                    stage_lstm(k, c, HT, p, bufs, sems, used)
            with ExitStack() as c:
                add_transposed(k, c, "l2r", lambda t: HT[:, bass.ds(t * TW, TW)], {})

        k.recycle_semaphores()
        with ExitStack() as c3:
            sb3 = lambda n, s: c3.enter_context(nc.sbuf_tensor(n, s, F32))
            E, EC = k.E, k.E // P
            e.Wqv, e.WoT, e.a_col, e.a_blk = sb3("Wqv", [P, 2 * P]), sb3("WoT", [P, P]), sb3("a_col", [P, 1]), sb3("a_blk", [P, k.HEADS])
            e.ST, e.DT, e.PT = (sb3(n, [P, E]) for n in ("ST", "DT", "PT"))
            e.S1, e.cont, e.reset, e.is_last, e.log_w = (sb3("S1", [P, EC, P]), sb3("cont", [P, E + 1]), sb3("reset", [P, E + 1]),
                                                         sb3("is_last", [P, E]), sb3("log_w", [P, E]))
            scores, Xv = sb3("scores", [P, EC, B * k.HEADS]), sb3("Xv", [P, B, P])
            with ExitStack() as c:
                stage_edges(k, c, d, e)
            with ExitStack() as c:
                stage_scores(k, c, Xv, scores, e)
            with ExitStack() as c:
                stage_softmax(k, c, scores, e)
            with ExitStack() as c:
                stage_attend(k, c, Xv, scores, e, out)


def kernel(**inputs):
    import numpy as np
    import concourse.bacc as bacc
    from concourse.bass_utils import run_bass_kernel_spmd

    g = {n: np.asarray(a) for n, a in inputs.items()}
    B, N, D = g["x"].shape
    per_channel = [g["L1_gnn_b1"].reshape(2, P), g["L1_gnn_g1"].reshape(2, P), g["L1_gnn_be1"].reshape(2, P),
                   g["L1_gnn_b2"].reshape(1, P), g["L1_gnn_g2"].reshape(1, P), g["L1_gnn_be2"].reshape(1, P),
                   g["L2_gnn_bih"].reshape(16, P), g["L2_gnn_bhh"].reshape(16, P)]
    layout = {
        "x": g["x"].transpose(1, 0, 2),
        "adj": g["adj"], "adjT": g["adj"].T,
        "cols": np.concatenate(per_channel, axis=0).T,
        "rows": np.stack([g["L0_gnn_bias"], g["L2_gnn_bg0"], g["L2_gnn_bg1"]]),
        "L0_W": g["L0_gnn_W"], "W1T": g["L1_gnn_W1"].T, "W2T": g["L1_gnn_W2"].T,
        "Wg0": g["L2_gnn_Wg0"], "Wg1": g["L2_gnn_Wg1"],
        "WihT": g["L2_gnn_Wih"].transpose(0, 2, 1), "WhhT": g["L2_gnn_Whh"].transpose(0, 2, 1),
        "Wqv": np.concatenate([g["L3_gnn_W_lin"].T, g["L3_gnn_W_val"].T], axis=1), "WoT": g["L3_gnn_W_out"].T,
        "a_col": g["L3_gnn_a"].reshape(D, 1),
        "src": g["L3_gnn_src"], "dst": g["L3_gnn_dst"],
        "src_col": g["L3_gnn_src"].reshape(-1, P).T, "dst_col": g["L3_gnn_dst"].reshape(-1, P).T,
    }
    nc = bacc.Bacc("TRN2", target_bir_lowering=False, num_devices=1, dynamic_dma_scratch_size=2048)
    arrays, d = {}, {}
    for name, a in layout.items():
        arrays[f"in_{name}"] = np.ascontiguousarray(a)
        d[name] = nc.dram_tensor(f"in_{name}", a.shape, mybir.dt.from_np(a.dtype), kind="ExternalInput").ap()
    out = nc.dram_tensor("out", (N, B, D), F32, kind="ExternalOutput").ap()
    build(nc, d, out)
    r = run_bass_kernel_spmd(nc, [arrays], core_ids=[0])
    return np.ascontiguousarray(r.results[0]["out"].transpose(1, 0, 2))
```

```python
from contextlib import ExitStack

import concourse.bass as bass
from concourse import mybir

ALU = mybir.AluOpType
ACT = mybir.ActivationFunctionType
F32 = mybir.dt.float32
F32R = mybir.dt.float32r
I32 = mybir.dt.int32
P = 128
EPS = 1e-5
EPS_EDGE = 1e-8
TB = 4
TW = TB * P
BIG = 1.0e30

C_B1, C_G1, C_BE1 = 0, 2, 4
C_B2, C_G2, C_BE2 = 6, 7, 8
C_BIH, C_BHH = 9, 25
NCOLS = 41
R_L0, R_G0, R_G1 = 0, 1, 2


class Shared:
    sems = ()

    def sem(self, name):
        handle = self.nc.alloc_semaphore(name)
        self.sems += (handle,)
        return handle

    def recycle_semaphores(self):
        self.nc.clear_and_free_semaphores(list(self.sems))
        self.nc.all_engine_barrier()
        self.sems = ()


def each(n, make):
    return [make(i) for i in range(n)]


class LayerNormTail:

    GROUPS = 5

    def __init__(self, k, ctx, name, S, nb=TB, per=2):
        sb = lambda n: ctx.enter_context(k.nc.sbuf_tensor(f"{name}_{n}", [P, per * nb], F32))
        self.k, self.S, self.nb, self.per, self.batches = k, S, nb, per, S // per
        self.st6 = ctx.enter_context(k.nc.sbuf_tensor(f"{name}_st6", [P, S * nb, 6], F32))
        self.sum, self.diff, self.m2 = sb("sum"), sb("diff"), sb("m2")
        self.stats_ready = each(S, lambda s: k.sem(f"{name}_stats{s}"))
        self.stats_free, self.ready = (each(S // per, lambda q: k.sem(f"{name}_{n}{q}")) for n in ("stfree", "coef"))
        self.step, self.tally, self.dve_tally = (k.sem(f"{name}_{n}") for n in ("step", "tally", "dve_tally"))

    def open(self, pool):
        for free in self.stats_free:
            pool.sem_inc(free, 1)

    def wait(self, eng, s, turn):
        eng.wait_ge(self.ready[s // self.per], turn + 1)

    def stats(self, dve, xt, s, turn):
        dve.wait_ge(self.stats_free[s // self.per], turn + 1)
        dve.sem_inc(self.dve_tally, 1)
        for j in range(self.nb):
            last = dve.bn_stats(self.st6[:, s * self.nb + j, :], xt[:, j, :])
        last.then_inc(self.stats_ready[s], 1)

    def coefficients(self, pool, turn):
        for q in range(self.batches):
            self.batch(pool, turn, q)

    def batch(self, pool, turn, q):
        k, c = self.k, self.k.ln_const
        width = self.per * self.nb
        st6 = self.st6[:, q * width:(q + 1) * width, :]
        su, di, m2 = self.sum[:, :], self.diff[:, :], self.m2[:, :]
        base = (turn * self.batches + q) * self.GROUPS
        rows = bass.ds((turn * self.batches + q) * width, width)
        rstd, nmr = k.rstd[:, rows], k.nmr[:, rows]

        def tt(out, a, b, op):
            return pool.tensor_tensor(out=out, in0=a, in1=b, op=op)

        def group(n):
            pool.wait_ge(self.step, base + n)
            pool.sem_inc(self.tally, 1)

        for s in range(q * self.per, (q + 1) * self.per):
            pool.wait_ge(self.stats_ready[s], turn + 1)
        pool.sem_inc(self.tally, 1)
        tt(su, st6[:, :, 1], st6[:, :, 4], ALU.add)
        tt(di, st6[:, :, 1], st6[:, :, 4], ALU.subtract)
        tt(m2, st6[:, :, 2], st6[:, :, 5], ALU.add).then_inc(self.step, 1)
        group(1)
        pool.sem_inc(self.stats_free[q], 1)
        tt(di, di, di, ALU.mult)
        pool.tensor_scalar(su, su, -1.0, 0.0, ALU.mult, ALU.add)
        pool.tensor_scalar(m2, m2, 4.0 / P, 4.0 * EPS, ALU.mult, ALU.add).then_inc(self.step, 1)
        group(2)
        tt(m2, m2, di, ALU.add).then_inc(self.step, 1)
        group(3)
        tt(m2, m2, c["-half"][:, 0:width], ALU.pow).then_inc(self.step, 1)
        group(4)
        tt(rstd, m2, c["two"][:, 0:width], ALU.mult)
        tt(nmr, su, m2, ALU.mult).then_inc(self.step, 1)
        pool.wait_ge(self.step, base + 5)
        pool.sem_inc(self.ready[q], 1)


def normalise_tile(act, k, h, b0):
    for j in range(TB):
        last = act.activation(h[:, j, :], k.X[:, bass.ds(b0, TB), :][:, j, :], ACT.Relu,
                              bias=k.nmr[:, bass.ds(b0, TB)][:, j:j + 1], scale=k.rstd[:, bass.ds(b0, TB)][:, j:j + 1])
    return last


def looped(eng, n, turn, lag=False):
    with eng.Fori(0, n - 1) as i:
        turn(i, True)
    turn(n - 1, False)


def stage_setup(k, ctx, d):
    nc, X = k.nc, k.X
    sem = lambda n: k.sem(n)
    sb = lambda n, s, t=F32: ctx.enter_context(nc.sbuf_tensor(n, s, t))
    CH = 8
    CB = k.B // CH
    x_in = each(CH, lambda c: sem(f"x_in{c}"))
    adj_in, w_in, cols_in = sem("adj_in"), sem("w_in"), sem("cols_in")
    cst, masks, deg, dinv_p, dinv_bc, ahat = (sem(n) for n in ("cst", "masks", "deg", "dinv_p", "dinv_bc", "ahat"))
    diag_ready, sep, primed = (sem(n) for n in ("diag_ready", "setup_sep", "primed"))
    adj = sb("adj_rows", [P, P])
    onesPP = k.ones
    rs = sb("deg_parts", [P, 4])
    CB_ = k.B // 8
    ln = LayerNormTail(k, ctx, "x", 2, CB_)
    tmp = sb("setup_tmp", [P, P])
    tmp2 = sb("setup_tmp2", [P, P])
    dinv = sb("dinv", [P, 1])
    bank_dg, bank_di = k.bank[0], k.bank[1]

    with nc.Block() as block:
        @block.sync
        def _(sp):
            sp.dma_start(adj[:, :], d["adj"]).then_inc(adj_in, 16)
            sp.dma_start(k.adjT[:, :], d["adjT"]).then_inc(adj_in, 16)
            for c in range(CH):
                sp.dma_start(X[:, c * CB:(c + 1) * CB, :], d["x"][:, c * CB:(c + 1) * CB, :]).then_inc(x_in[c], 16)

        @block.scalar
        def _(act):
            act.wait_ge(cst, 1)
            act.activation(k.ones[:, 0:1], k.ones[:, 0:1], ACT.Sigmoid).then_inc(primed, 1)
            act.dma_start(k.cols[:, :], d["cols"]).then_inc(cols_in, 16)
            act.dma_start(k.rows[:, :, :], d["rows"].partition_broadcast(P)).then_inc(cols_in, 16)
            act.dma_start(k.W0[:, :, :], d["L0_W"].rearrange("k f o -> f k o")).then_inc(w_in, 16)
            act.dma_start(k.W1T[:, :], d["W1T"]).then_inc(w_in, 16)
            act.dma_start(k.W2T[:, :, :], d["W2T"].rearrange("(h c) o -> c h o", h=2)).then_inc(w_in, 16)
            act.dma_start(k.Wg[:, 0, :], d["Wg0"]).then_inc(w_in, 16)
            act.dma_start(k.Wg[:, 1, :], d["Wg1"]).then_inc(w_in, 16)
            act.wait_ge(w_in, 5 * 16)
            act.wait_ge(cols_in, 2 * 16)

        @block.gpsimd
        def _(pool):
            for name, value in (("-half", -0.5), ("two", 2.0)):
                pool.memset(k.ln_const[name][:, :], value)
            pool.memset(k.zero[:, :], 0.0)
            ln.open(pool)
            pool.memset(onesPP[:, :], 0.0).then_inc(cst, 1)
            pool.wait_ge(primed, 1)
            pool.memset(onesPP[:, :], 1.0).then_inc(cst, 1)
            pool.memset(k.ident[:, :], 0.0).then_inc(sep, 1)
            pool.wait_ge(sep, 1)
            pool.affine_select(out=k.ident[:, :], in_=k.ident[:, :], compare_op=ALU.not_equal, fill=1.0,
                               base=0, pattern=[[-1, P]], channel_multiplier=1).then_inc(cst, 1)
            pool.wait_ge(adj_in, 32)
            pool.affine_select(out=k.A12T[:, 0, :], in_=k.adjT[:, :], compare_op=ALU.is_gt, fill=0.0,
                               base=0, pattern=[[-1, P]], channel_multiplier=1).then_inc(masks, 1)
            pool.affine_select(out=k.A12T[:, 1, :], in_=k.adjT[:, :], compare_op=ALU.is_gt, fill=0.0,
                               base=0, pattern=[[1, P]], channel_multiplier=-1).then_inc(masks, 1)
            pool.wait_ge(deg, 5)
            pool.tensor_tensor(out=dinv[:, :], in0=rs[:, 3:4], in1=k.ln_const["-half"][:, 0:1], op=ALU.pow).then_inc(dinv_p, 1)
            for c in range(CH):
                if c % 2:
                    ln.coefficients(pool, c // 2)

        @block.tensor
        def _(pe):
            pe.wait_ge(cst, 3)
            pe.wait_ge(deg, 1)
            pe.matmul(bank_dg[:, 0:P], onesPP[:, :], tmp[:, :], start=True, stop=True).then_inc(diag_ready, 1)
            pe.wait_ge(dinv_bc, 1)
            pe.matmul(bank_di[:, 0:P], onesPP[:, :], tmp2[:, :], start=True, stop=True).then_inc(diag_ready, 1)

        @block.vector
        def _(dve):
            dve.wait_ge(adj_in, 32)
            dve.wait_ge(cst, 3)
            dve.tensor_tensor(tmp[:, :], adj[:, :], k.ident[:, :], ALU.mult).then_inc(deg, 1)
            dve.wait_ge(deg, 1)
            dve.reduce_sum(rs[:, 0:1], adj[:, :], mybir.AxisListType.X)
            dve.reduce_sum(rs[:, 1:2], k.adjT[:, :], mybir.AxisListType.X)
            dve.reduce_sum(rs[:, 2:3], tmp[:, :], mybir.AxisListType.X).then_inc(deg, 1)
            dve.wait_ge(deg, 2)
            dve.tensor_tensor(rs[:, 0:1], rs[:, 0:1], rs[:, 1:2], ALU.add).then_inc(deg, 1)
            dve.wait_ge(deg, 3)
            dve.tensor_tensor(rs[:, 3:4], rs[:, 0:1], rs[:, 2:3], ALU.subtract).then_inc(deg, 1)
            dve.wait_ge(deg, 4)
            dve.tensor_scalar(rs[:, 3:4], rs[:, 3:4], 1.0, None, ALU.add).then_inc(deg, 1)
            dve.tensor_tensor(k.AhatT[:, :], k.adjT[:, :], k.ident[:, :], ALU.add).then_inc(ahat, 1)
            dve.wait_ge(dinv_p, 1)
            dve.tensor_scalar(tmp2[:, :], k.ident[:, :], dinv[:, :], None, ALU.mult).then_inc(dinv_bc, 1)
            dve.wait_ge(ahat, 1)
            dve.tensor_scalar(k.AhatT[:, :], k.AhatT[:, :], dinv[:, :], None, ALU.mult).then_inc(ahat, 1)
            dve.wait_ge(diag_ready, 1)
            dve.tensor_copy(k.diag_bc[:, :], bank_dg[:, 0:P])
            dve.wait_ge(diag_ready, 2)
            dve.wait_ge(ahat, 2)
            dve.tensor_tensor(k.AhatT[:, :], bank_di[:, 0:P], k.AhatT[:, :], ALU.mult).then_inc(ahat, 1)
            for c in range(CH):
                dve.wait_ge(x_in[c], 16)
                ln.stats(dve, X[:, c * CB:(c + 1) * CB, :], c % 2, c // 2)


def stage_layer0(k, ctx):
    nc, X = k.nc, k.X
    S = 2
    sem = lambda n: k.sem(n)
    sb = lambda n, s: ctx.enter_context(nc.sbuf_tensor(n, s, F32))
    h = each(S, lambda s: sb(f"l0_h{s}", [P, TB, P]))
    Z0 = each(S, lambda s: sb(f"l0_z0{s}", [P, TB, P]))
    Z12 = each(S, lambda s: sb(f"l0_z12{s}", [P, TB, 2, P]))
    psT, psA, psB, psO = k.bank[0:2], k.bank[2:4], k.bank[4:6], k.bank[6:8]
    h_ready = each(S, lambda s: sem(f"l0_h_ready{s}"))
    T_ready, AB_ready = each(S, lambda s: sem(f"l0_T_ready{s}")), each(S, lambda s: sem(f"l0_AB_ready{s}"))
    Z0_ready, Z12_ready = each(S, lambda s: sem(f"l0_Z0_ready{s}")), each(S, lambda s: sem(f"l0_Z12_ready{s}"))
    out_ready, biased, updated = (each(S, lambda s: sem(f"l0_{n}{s}")) for n in ("out_ready", "biased", "updated"))
    ln = LayerNormTail(k, ctx, "l0", S)
    n_it = k.B // TB // S

    with nc.Block() as block:
        @block.gpsimd
        def _(pool):
            ln.open(pool)
            with pool.Fori(0, n_it) as i:
                for s in range(S):
                    b0 = (i * S + s) * TB
                    pool.wait_ge(h_ready[s], i + 1)
                    pool.sem_inc(ln.tally, 1)
                    pool.tensor_tensor(out=X[:, bass.ds(b0, TB), :], in0=X[:, bass.ds(b0, TB), :],
                                       in1=k.rows[:, R_L0:R_L0 + 1, :].broadcast_to([P, TB, P]),
                                       op=ALU.add).then_inc(biased[s], 1)
                ln.coefficients(pool, i)

        @block.scalar
        def _(act):
            def normalise(i):
                for s in range(S):
                    normalise_tile(act, k, h[s], (i * S + s) * TB).then_inc(h_ready[s], 1)

            def turn(i, ahead):
                for s in range(S):
                    act.wait_ge(AB_ready[s], i + 1)
                    act.activation(Z12[s][:, 0:2, :, :], psA[s][:, :], ACT.Copy)
                    act.activation(Z12[s][:, 2:4, :, :], psB[s][:, :], ACT.Copy).then_inc(Z12_ready[s], 1)
                if ahead:
                    normalise(i + 1)

            normalise(0)
            looped(act, n_it, turn)

        @block.tensor
        def _(pe):
            with pe.Fori(0, n_it) as i:
                for s in range(S):
                    pe.wait_ge(h_ready[s], i + 1)
                    for j in range(TB):
                        last = pe.transpose(psT[s][:, j * P:(j + 1) * P], h[s][:, j, :], k.ident[:, :])
                    last.then_inc(T_ready[s], 1)
                    for j in range(TB):
                        ps = (psA, psB)[j // 2][s]
                        last = pe.matmul(ps[:, (j % 2) * 2 * P:(j % 2 + 1) * 2 * P], h[s][:, j, :],
                                         k.A12T[:, :, :], start=True, stop=True)
                        if j == TB - 1:
                            last.then_inc(AB_ready[s], 1)
                for s in range(S):
                    pe.wait_ge(Z0_ready[s], i + 1)
                    pe.wait_ge(Z12_ready[s], i + 1)
                    for j in range(TB):
                        o = psO[s][:, j * P:(j + 1) * P]
                        pe.matmul(o, Z0[s][:, j, :], k.W0[:, 0, :], start=True, stop=False)
                        pe.matmul(o, Z12[s][:, j, 0, :], k.W0[:, 1, :], start=False, stop=False)
                        last = pe.matmul(o, Z12[s][:, j, 1, :], k.W0[:, 2, :], start=False, stop=True)
                    last.then_inc(out_ready[s], 1)

        @block.vector
        def _(dve):
            with dve.Fori(0, n_it) as i:
                for s in range(S):
                    dve.wait_ge(T_ready[s], i + 1)
                    dve.tensor_tensor(Z0[s][:, :, :], psT[s][:, :].rearrange("p (b n) -> p b n", b=TB),
                                      k.diag_bc[:, :].unsqueeze(1).broadcast_to([P, TB, P]),
                                      ALU.mult).then_inc(Z0_ready[s], 1)
                for s in range(S):
                    b0 = (i * S + s) * TB
                    xt = X[:, bass.ds(b0, TB), :]
                    dve.wait_ge(biased[s], i + 1)
                    dve.wait_ge(out_ready[s], i + 1)
                    dve.tensor_tensor(xt, psO[s][:, :].rearrange("p (b n) -> p b n", b=TB), xt,
                                      ALU.add).then_inc(updated[s], 1)
                for s in range(S):
                    dve.wait_ge(updated[s], i + 1)
                    ln.stats(dve, X[:, bass.ds((i * S + s) * TB, TB), :], s, i)


def stage_gcn_hidden(k, ctx, Y, bn6):
    nc, X = k.nc, k.X
    S = 2
    sem = lambda n: k.sem(n)
    sb = lambda n, s: ctx.enter_context(nc.sbuf_tensor(n, s, F32))
    h = each(S, lambda s: sb(f"l1_h{s}", [P, TB, P]))
    ZT = each(S, lambda s: sb(f"l1_z{s}", [P, TW]))
    psZ, psY0, psY1 = k.bank[0:2], k.bank[2:4], k.bank[4:6]
    h_ready, Z_ready, ZT_ready, Y_ready, Y_stored = (
        each(S, lambda s: sem(f"l1_{n}{s}")) for n in ("h", "Z", "ZT", "Y", "Ys"))
    n_it = k.B // TB // S
    tally = sem("l1_tally")
    y_at = lambda c, i, s: Y[c][:, bass.ds((i * S + s) * TW, TW)]

    with nc.Block() as block:
        @block.scalar
        def _(act):
            def normalise(i):
                for s in range(S):
                    normalise_tile(act, k, h[s], (i * S + s) * TB).then_inc(h_ready[s], 1)

            def turn(i, ahead):
                for s in range(S):
                    if ahead:
                        act.wait_ge(Z_ready[s], i + 1)
                        normalise_tile(act, k, h[s], ((i + 1) * S + s) * TB).then_inc(h_ready[s], 1)
                for s in range(S):
                    act.wait_ge(Y_ready[s], i + 1)
                    for c, ps in enumerate((psY0, psY1)):
                        last = act.activation(y_at(c, i, s), ps[s][:, :], ACT.Identity,
                                              bias=k.cols[:, C_B1 + c:C_B1 + c + 1])
                    last.then_inc(Y_stored[s], 1)

            for s in range(S):
                act.sem_inc(Y_stored[s], 1)
            normalise(0)
            looped(act, n_it, turn)

        @block.tensor
        def _(pe):
            with pe.Fori(0, n_it) as i:
                for s in range(S):
                    pe.wait_ge(h_ready[s], i + 1)
                    for j in range(TB):
                        last = pe.matmul(psZ[s][:, j * P:(j + 1) * P], h[s][:, j, :], k.AhatT[:, :],
                                         start=True, stop=True)
                    last.then_inc(Z_ready[s], 1)
                for s in range(S):
                    pe.wait_ge(ZT_ready[s], i + 1)
                    pe.wait_ge(Y_stored[s], i + 1)
                    pe.matmul(psY0[s][:, :], k.W1T[:, 0:P], ZT[s][:, :], start=True, stop=True)
                    pe.matmul(psY1[s][:, :], k.W1T[:, P:2 * P], ZT[s][:, :], start=True, stop=True).then_inc(Y_ready[s], 1)

        @block.vector
        def _(dve):
            def copy_z(i):
                for s in range(S):
                    dve.wait_ge(Z_ready[s], i + 1)
                    dve.tensor_copy(ZT[s][:, :], psZ[s][:, :]).then_inc(ZT_ready[s], 1)

            def y_stats(i):
                for s in range(S):
                    dve.wait_ge(Y_stored[s], i + 2)
                    dve.sem_inc(tally, 1)
                    for c in range(2):
                        dve.bn_stats(bn6[:, c, bass.ds(i * S + s, 1), :], y_at(c, i, s))

            copy_z(0)
            with dve.Fori(0, n_it - 1) as i:
                copy_z(i + 1)
                y_stats(i)
            y_stats(n_it - 1)


def batchnorm_coefficients(k, ctx, name, bn6, halves, c_gamma, c_beta, coef):
    nc = k.nc
    mv = ctx.enter_context(nc.sbuf_tensor(f"{name}_mv", [P, halves, 2], F32))
    sem = lambda n: k.sem(f"{name}_{n}")
    aggregated, shifted, powed, scaled, ready = (sem(n) for n in ("aggr", "shift", "pow", "scale", "bn_ready"))

    def on_vector(dve):
        for c in range(halves):
            last = dve.bn_aggr(mv[:, c, :], bn6[:, c, :, :])
        last.then_inc(aggregated, 1)
        dve.wait_ge(aggregated, 1)
        dve.tensor_scalar(mv[:, :, 1], mv[:, :, 1], EPS, None, ALU.add).then_inc(shifted, 1)
        dve.wait_ge(powed, 1)
        dve.tensor_tensor(coef[:, :, 0], k.cols[:, c_gamma:c_gamma + halves], mv[:, :, 1], ALU.mult).then_inc(scaled, 1)
        dve.wait_ge(scaled, 1)
        dve.tensor_tensor(mv[:, :, 0], mv[:, :, 0], coef[:, :, 0], ALU.mult).then_inc(scaled, 1)
        dve.wait_ge(scaled, 2)
        dve.tensor_tensor(coef[:, :, 1], k.cols[:, c_beta:c_beta + halves], mv[:, :, 0], ALU.subtract).then_inc(ready, 1)

    def on_pool(pool):
        pool.wait_ge(shifted, 1)
        pool.tensor_tensor(out=mv[:, :, 1], in0=mv[:, :, 1], in1=k.ln_const["-half"][:, 0:halves], op=ALU.pow).then_inc(powed, 1)

    return on_vector, on_pool, ready


def stage_gcn_out(k, ctx, Y, bn6, bno6):
    nc = k.nc
    S = 2
    sem = lambda n: k.sem(n)
    sb = lambda n, s: ctx.enter_context(nc.sbuf_tensor(n, s, F32))
    h2 = each(S, lambda s: sb(f"l1b_h{s}", [P, 2, TW]))
    coef = sb("l1b_coef", [P, 2, 2])
    psO = k.bank[0:2]
    h2_ready, O_ready, O_stored = (each(S, lambda s: sem(f"l1b_{n}{s}")) for n in ("h", "O", "Os"))
    coef_dve, coef_pool, coef_ready = batchnorm_coefficients(k, ctx, "bn1", bn6, 2, C_G1, C_BE1, coef)
    tally = sem("l1b_tally")
    n_it = k.B // TB // S

    with nc.Block() as block:
        @block.gpsimd
        def _(pool):
            coef_pool(pool)

        @block.scalar
        def _(act):
            act.wait_ge(coef_ready, 1)
            with act.Fori(0, n_it) as i:
                for s in range(S):
                    act.wait_ge(O_ready[s], i + 1)
                    for c in range(2):
                        last = act.activation(h2[s][:, c, :], Y[c][:, bass.ds((i * S + s) * TW, TW)], ACT.Relu,
                                              bias=coef[:, c, 1:2], scale=coef[:, c, 0:1])
                    last.then_inc(h2_ready[s], 1)

        @block.tensor
        def _(pe):
            for s in range(S):
                pe.sem_inc(O_ready[s], 1)
            with pe.Fori(0, n_it) as i:
                for s in range(S):
                    pe.wait_ge(h2_ready[s], i + 1)
                    pe.wait_ge(O_stored[s], i + 1)
                    pe.matmul(psO[s][:, :], k.W2T[:, 0, :], h2[s][:, 0, :], start=True, stop=False)
                    pe.matmul(psO[s][:, :], k.W2T[:, 1, :], h2[s][:, 1, :], start=False, stop=True).then_inc(O_ready[s], 1)

        @block.vector
        def _(dve):
            coef_dve(dve)
            for s in range(S):
                dve.sem_inc(O_stored[s], 1)
            with dve.Fori(0, n_it) as i:
                for s in range(S):
                    t = i * S + s
                    o = Y[0][:, bass.ds(t * TW, TW)]
                    dve.wait_ge(O_ready[s], i + 2)
                    dve.tensor_scalar(o, psO[s][:, :], k.cols[:, C_B2:C_B2 + 1], None, ALU.add).then_inc(O_stored[s], 1)
                    dve.wait_ge(O_stored[s], i + 2)
                    dve.sem_inc(tally, 1)
                    dve.bn_stats(bno6[:, 0, bass.ds(t, 1), :], o)


class Residual:

    def __init__(self, k, ctx, name, S, source, affine, banks):
        self.k, self.S, self.source, self.affine, self.banks = k, S, source, affine, banks
        self.o = each(S, lambda s: ctx.enter_context(k.nc.sbuf_tensor(f"{name}_o{s}", [P, TW], F32)))
        self.o_ready, self.R_ready, self.updated = (each(S, lambda s: k.sem(f"{name}_{n}{s}")) for n in ("o", "R", "upd"))
        self.ln = LayerNormTail(k, ctx, name, S)

    def fetch(self, act, i, s):
        act.activation(self.o[s][:, :], self.source(i * self.S + s), ACT.Identity, **self.affine).then_inc(self.o_ready[s], 1)

    def turn_over(self, pe, i, s):
        pe.wait_ge(self.o_ready[s], i + 1)
        for j in range(TB):
            last = pe.transpose(self.banks[s][:, j * P:(j + 1) * P], self.o[s][:, j * P:(j + 1) * P], self.k.ident[:, :])
        last.then_inc(self.R_ready[s], 1)

    def update(self, dve, i):
        xt = each(self.S, lambda s: self.k.X[:, bass.ds((i * self.S + s) * TB, TB), :])
        for s0 in range(0, self.S, 2):
            for s in range(s0, s0 + 2):
                dve.wait_ge(self.R_ready[s], i + 1)
                dve.tensor_tensor(xt[s], self.banks[s][:, :].rearrange("p (b n) -> p b n", b=TB), xt[s],
                                  ALU.add).then_inc(self.updated[s], 1)
            for s in range(s0, s0 + 2):
                dve.wait_ge(self.updated[s], i + 1)
                self.ln.stats(dve, xt[s], s, i)

    def coefficients(self, pool, i):
        self.ln.coefficients(pool, i)


def stage_conv(k, ctx, O, bno6, HT):
    nc = k.nc
    S = 4
    sem = lambda n: k.sem(n)
    sb = lambda n, s: ctx.enter_context(nc.sbuf_tensor(n, s, F32))
    h, hT, V = (each(S, lambda s: sb(f"l2_{n}{s}", [P, TB, P])) for n in ("h", "hT", "V"))
    G, V2 = hT, V
    names = ("h", "Tp", "hT", "Vp", "V", "Gp", "G", "V2p", "V2", "Hp", "H")
    R = {n: each(S, lambda s: sem(f"l2_{n}{s}")) for n in names}
    n_it = k.B // TB // S
    even, odd = k.bank[0:4], k.bank[4:8]
    as_tile = lambda ps: ps[:, :].rearrange("p (b n) -> p b n", b=TB)
    coef = sb("l1c_coef", [P, 1, 2])
    bn_dve, bn_pool, bn_ready = batchnorm_coefficients(k, ctx, "bn2", bno6, 1, C_G2, C_BE2, coef)
    res = Residual(k, ctx, "l1r", S, lambda t: O[:, bass.ds(t * TW, TW)],
                   dict(bias=coef[:, 0, 1:2], scale=coef[:, 0, 0:1]), odd)

    with nc.Block() as block:
        @block.gpsimd
        def _(pool):
            res.ln.open(pool)
            bn_pool(pool)
            with pool.Fori(0, n_it) as i:
                res.coefficients(pool, i)

        @block.scalar
        def _(act):
            def normalise(i, s):
                res.ln.wait(act, s, i)
                normalise_tile(act, k, h[s], (i * S + s) * TB).then_inc(R["h"][s], 1)

            def hidden(i, s):
                act.wait_ge(R["Hp"][s], i + 1)
                act.activation(HT[:, bass.ds((i * S + s) * TW, TW)], even[s][:, :], ACT.Relu).then_inc(R["H"][s], 1)

            def turn(i, ahead):
                if ahead:
                    for s in range(S):
                        act.wait_ge(R["Tp"][s], i + 1)
                        res.fetch(act, i + 1, s)
                for s in range(S):
                    act.wait_ge(R["Gp"][s], i + 1)
                    act.activation(G[s][:, :, :], as_tile(even[s]), ACT.Relu).then_inc(R["G"][s], 1)
                for s in range(S):
                    if ahead and s % 2 == 0:
                        normalise(i + 1, s)
                        normalise(i + 1, s + 1)
                    if ahead and s % 2 == 0:
                        for r in range(s, s + 2):
                            hidden(i, r)
                    elif not ahead:
                        hidden(i, s)

            for s in range(S):
                act.sem_inc(R["H"][s], 1)
            act.wait_ge(bn_ready, 1)
            for s in range(S):
                res.fetch(act, 0, s)
            for s in range(S):
                normalise(0, s)
            looped(act, n_it, turn)

        @block.tensor
        def _(pe):
            def turn(i, ahead):
                for s in range(S):
                    pe.wait_ge(R["h"][s], i + 1)
                    pe.wait_ge(R["H"][s], i + 1)
                    for j in range(TB):
                        last = pe.transpose(even[s][:, j * P:(j + 1) * P], h[s][:, j, :], k.ident[:, :])
                    last.then_inc(R["Tp"][s], 1)
                for s in range(S):
                    pe.wait_ge(R["hT"][s], i + 1)
                    for j in range(TB):
                        last = pe.matmul(odd[s][:, j * P:(j + 1) * P], hT[s][:, j, :], k.Wg[:, 0, :], start=True, stop=True)
                    last.then_inc(R["Vp"][s], 1)
                for s in range(S):
                    pe.wait_ge(R["V"][s], i + 1)
                    if ahead:
                        res.turn_over(pe, i + 1, s)
                    for j in range(TB):
                        last = pe.matmul(even[s][:, j * P:(j + 1) * P], V[s][:, j, :], k.adjT[:, :], start=True, stop=True)
                    last.then_inc(R["Gp"][s], 1)
                for s in range(S):
                    pe.wait_ge(R["G"][s], i + 1)
                    if ahead:
                        pe.wait_ge(res.updated[s], i + 2)
                    for j in range(TB):
                        last = pe.matmul(odd[s][:, j * P:(j + 1) * P], G[s][:, j, :], k.Wg[:, 1, :], start=True, stop=True)
                    last.then_inc(R["V2p"][s], 1)
                for s in range(S):
                    pe.wait_ge(R["V2"][s], i + 1)
                    for j in range(TB):
                        last = pe.matmul(even[s][:, j * P:(j + 1) * P], V2[s][:, j, :], k.adjT[:, :], start=True, stop=True)
                    last.then_inc(R["Hp"][s], 1)

            for s in range(S):
                res.turn_over(pe, 0, s)
            looped(pe, n_it, turn)

        @block.vector
        def _(dve):
            def add_bias(src, dst, buf, row, i, s):
                dve.wait_ge(R[src][s], i + 1)
                dve.tensor_tensor(buf[s][:, :, :], as_tile(odd[s]), k.rows[:, row:row + 1, :].broadcast_to([P, TB, P]),
                                  ALU.add).then_inc(R[dst][s], 1)

            def turn(i, ahead):
                for s in range(S):
                    dve.wait_ge(R["Tp"][s], i + 1)
                    dve.tensor_copy(hT[s][:, :, :], as_tile(even[s])).then_inc(R["hT"][s], 1)
                for s in range(S):
                    add_bias("Vp", "V", V, R_G0, i, s)
                if ahead:
                    res.update(dve, i + 1)
                for s in range(S):
                    add_bias("V2p", "V2", V2, R_G1, i, s)

            bn_dve(dve)
            res.update(dve, 0)
            looped(dve, n_it, turn)


GATE_I, GATE_F, GATE_G, GATE_O = range(4)


def split_float32(eng, full, hi, lo, copied, copied_count, tally=None, zeros=None):
    if zeros is not None:
        eng.tensor_tensor(out=hi, in0=full, in1=zeros, op=ALU.add).then_inc(copied, 1)
    else:
        eng.tensor_copy(hi, full).then_inc(copied, 1)
    eng.wait_ge(copied, copied_count)
    if tally is not None:
        eng.sem_inc(tally, 1)
    return eng.tensor_tensor(out=lo, in0=full, in1=hi.bitcast(F32), op=ALU.subtract)


def stage_lstm(k, ctx, HT, p, bufs, sems, used):
    nc, B = k.nc, k.B
    S = 2
    nw = P // p
    nb = max(n for n in (4, 8, 16) if n * nw <= TW)
    N = nb * nw
    n_it = B // nb // S
    bias = k.lstm_bias[:, p - 1, :]
    gates, cell, hid, hid_hi, hid_lo, x_hi, x_lo = (bufs[n] for n in ("gates", "cell", "hid", "hid_hi", "hid_lo", "x_hi", "x_lo"))
    done, act_out, cell_ready, tanh_ready, h_ready, hh_ready, hl_ready, fc_ready, ig_ready, xh_ready, xl_ready = (
        sems[n] for n in ("done", "act", "cell", "tanh", "h", "hh", "hl", "fc", "ig", "xh", "xl"))
    u_done, u_seq, u_rec = used["done"], used["seq"], used["rec"]
    windows = HT[:, :].rearrange("h (b t) -> h b t", t=P)
    order = [GATE_G, GATE_I, GATE_F, GATE_O]

    def node(b0, step):
        if p == 1:
            return windows[:, bass.ds(b0, nb), :]
        return windows[:, bass.ds(b0, nb), 0:nw * p].rearrange("h b (w q) -> h b w q", q=p)[:, :, :, step]

    as3 = lambda ap: ap.rearrange("h (b w) -> h b w", w=nw)

    def n_gate(g, i, step):
        return u_done[g] + (i * (p - 1) + step if g == GATE_F else i * p + step + 1)

    def n_seq(i, step):
        return u_seq + i * p + step + 1

    def n_rec(i, step):
        return u_rec + i * (p - 1) + step

    def gates_of(step):
        return [g for g in order if step or g != GATE_F]

    with nc.Block() as block:
        @block.gpsimd
        def _(pool):
            zeros = k.zero[:, 0:1].unsqueeze(2).broadcast_to([P, nb, nw])
            with pool.Fori(0, n_it) as i:
                for step in range(p):
                    for s in range(S):
                        x = node((i * S + s) * nb, step)
                        pool.wait_ge(sems["x_free"][s], n_seq(i, step))
                        split_float32(pool, x, as3(x_hi[s][:, 0:N]), as3(x_lo[s][:, 0:N]),
                                      xh_ready[s], n_seq(i, step), sems["x_tally"][s],
                                      zeros=zeros).then_inc(xl_ready[s], 1)

        @block.tensor
        def _(pe):
            if p == 1:
                for s in range(S):
                    pe.sem_inc(sems["x_free"][s], 1)

            def product(out, W, g, v_hi, v_lo, start, stop):
                hi, lo = (W[n][:, p - 1, g * P:(g + 1) * P] for n in range(2))
                pe.matmul(out, hi, v_hi[:, 0:N], start=start, stop=False)
                pe.matmul(out, lo, v_hi[:, 0:N], start=False, stop=False)
                return pe.matmul(out, hi, v_lo[:, 0:N], start=False, stop=stop)

            with pe.Fori(0, n_it) as i:
                for step in range(p):
                    for s in range(S):
                        pe.wait_ge(xl_ready[s], n_seq(i, step))
                        for g in gates_of(step):
                            pe.wait_ge(act_out[s][g], n_gate(g, i, step))
                            last = product(k.bank[4 * s + g][:, 0:N], k.Wih, g, x_hi[s], x_lo[s], True, step == 0)
                            if step == 0 and g != GATE_O:
                                last.then_inc(done[s][g], 1)
                        last.then_inc(sems["x_free"][s], 1)
                        if step == 0:
                            pe.wait_ge(sems["x_free"][s], n_seq(i, step) + 1)
                            pe.sem_inc(done[s][GATE_O], 1)
                        else:
                            pe.wait_ge(hl_ready[s], n_rec(i, step))
                            for g in gates_of(step):
                                product(k.bank[4 * s + g][:, 0:N], k.Whh, g, hid_hi[s], hid_lo[s],
                                        False, True).then_inc(done[s][g], 1)

        @block.scalar
        def _(act):
            if p == 1:
                for s in range(S):
                    for g in range(4):
                        act.sem_inc(act_out[s][g], 1)
            with act.Fori(0, n_it) as i:
                for step in range(p):
                    for s in range(S):
                        for g in gates_of(step):
                            act.wait_ge(done[s][g], n_gate(g, i, step))
                            act.activation(gates[s][:, g, 0:N], k.bank[4 * s + g][:, 0:N],
                                           ACT.Tanh if g == GATE_G else ACT.Sigmoid,
                                           bias=bias[:, g:g + 1]).then_inc(act_out[s][g], 1)
                        act.wait_ge(cell_ready[s], n_seq(i, step))
                        act.activation(gates[s][:, GATE_G, 0:N], cell[s][:, 0:N], ACT.Tanh).then_inc(tanh_ready[s], 1)

        @block.vector
        def _(dve):
            with dve.Fori(0, n_it) as i:
                for step in range(p):
                    for s in range(S):
                        G = lambda g: gates[s][:, g, 0:N]
                        c = cell[s][:, 0:N]
                        dve.wait_ge(act_out[s][GATE_G], n_gate(GATE_G, i, step) + 1)
                        dve.wait_ge(act_out[s][GATE_I], n_gate(GATE_I, i, step) + 1)
                        if step == 0:
                            dve.tensor_tensor(c, G(GATE_I), G(GATE_G), ALU.mult).then_inc(cell_ready[s], 1)
                        else:
                            dve.tensor_tensor(G(GATE_I), G(GATE_I), G(GATE_G), ALU.mult).then_inc(ig_ready[s], 1)
                            dve.wait_ge(act_out[s][GATE_F], n_gate(GATE_F, i, step) + 1)
                            dve.tensor_tensor(c, G(GATE_F), c, ALU.mult).then_inc(fc_ready[s], 1)
                            dve.wait_ge(ig_ready[s], n_rec(i, step))
                            dve.wait_ge(fc_ready[s], n_rec(i, step))
                            dve.tensor_tensor(c, G(GATE_I), c, ALU.add).then_inc(cell_ready[s], 1)
                        dve.wait_ge(act_out[s][GATE_O], n_gate(GATE_O, i, step) + 1)
                        dve.wait_ge(tanh_ready[s], n_seq(i, step))
                        if step == p - 1:
                            dve.tensor_tensor(node((i * S + s) * nb, step), as3(G(GATE_O)), as3(G(GATE_G)), ALU.mult)
                        else:
                            hd = hid[s][:, 0:N]
                            dve.tensor_tensor(hd, G(GATE_O), G(GATE_G), ALU.mult).then_inc(h_ready[s], 1)
                            dve.wait_ge(h_ready[s], n_rec(i, step + 1))
                            split_float32(dve, hd, hid_hi[s][:, 0:N], hid_lo[s][:, 0:N], hh_ready[s],
                                          n_rec(i, step + 1)).then_inc(hl_ready[s], 1)

    used["seq"] += n_it * p
    used["rec"] += n_it * (p - 1)
    for g in range(4):
        used["done"][g] += n_it * (p - 1 if g == GATE_F else p)


def stage_lstm_weights(k, ctx, d):
    nc = k.nc
    raw = each(2, lambda s: ctx.enter_context(nc.sbuf_tensor(f"w_raw{s}", [P, 4, 4 * P], F32)))
    loaded, copied, split = each(2, lambda s: k.sem(f"lstm_w_in{s}")), k.sem("w_copied"), k.sem("w_split")
    with nc.Block() as block:
        @block.sync
        def _(sp):
            sp.dma_start(raw[0][:, :, :], d["WihT"].rearrange("p d g -> d p g")).then_inc(loaded[0], 16)
            sp.dma_start(raw[1][:, :, :], d["WhhT"].rearrange("p d g -> d p g")).then_inc(loaded[1], 16)

        @block.vector
        def _(dve):
            dve.tensor_tensor(k.lstm_bias[:, :, :].rearrange("h p g -> h (p g)"), k.cols[:, C_BIH:C_BIH + 16],
                              k.cols[:, C_BHH:C_BHH + 16], ALU.add)
            for n, W in enumerate((k.Wih, k.Whh)):
                dve.wait_ge(loaded[n], 16)
                split_float32(dve, raw[n][:, :, :], W[0][:, :, :], W[1][:, :, :], copied, n + 1)


def stage_edges(k, ctx, d, e):
    nc = k.nc
    E, EC = k.E, k.E // P
    sem = lambda n: k.sem(n)
    sb = lambda n, s, t=F32: ctx.enter_context(nc.sbuf_tensor(n, s, t))
    loaded, w_in, iotas, step, pe_done, lned, evac = (sem(n) for n in (
        "edges_in", "l3_w_in", "iotas", "edge_step", "edge_pe", "edge_ln", "edge_evac"))
    row_i, col_i = sb("edge_row_i", [P, 2, E], I32), sb("edge_col_i", [P, 2, EC], I32)
    row, col = sb("edge_row", [P, 2, E]), sb("edge_col", [P, 2, EC])
    order_row, order_col = sb("order_row", [P, E]), sb("order_col", [P, EC])
    key_row, key_col = sb("key_row", [P, E]), sb("key_col", [P, EC])
    iota_part, rank = sb("iota_part", [P, 1]), sb("rank", [P, EC])
    less, perm, colbc = sb("less", [P, E]), sb("perm", [P, EC, E]), sb("colbc", [P, 2, EC, P])
    sorted_row = sb("sorted_row", [P, 2, E])
    weight = sb("edge_weight", [P, E])
    psS, psD, psU, psW, psT = k.bank[0:5]

    with nc.Block() as block:
        @block.sync
        def _(sp):
            for n, name in enumerate(("src", "dst")):
                sp.dma_start(row_i[:, n, :], d[name].rearrange("(a e) -> a e", a=1).partition_broadcast(P)
                             .rearrange("p a e -> p (a e)")).then_inc(loaded, 16)
                sp.dma_start(col_i[:, n, :], d[name + "_col"]).then_inc(loaded, 16)
            sp.dma_start(e.Wqv[:, :], d["Wqv"]).then_inc(w_in, 16)
            sp.dma_start(e.WoT[:, :], d["WoT"]).then_inc(w_in, 16)
            sp.dma_start(e.a_sign[:, :], d["a"].rearrange("(o a) -> o a", o=1).partition_broadcast(P)
                         .rearrange("p o a -> p (o a)")).then_inc(w_in, 16)
            sp.wait_ge(w_in, 3 * 16)

        @block.gpsimd
        def _(pool):
            pool.iota(order_row[:, :], [[1, E]], base=0, channel_multiplier=0, allow_small_or_imprecise_dtypes=True).then_inc(iotas, 1)
            pool.iota(order_col[:, :], [[P, EC]], base=0, channel_multiplier=1, allow_small_or_imprecise_dtypes=True).then_inc(iotas, 1)
            pool.iota(iota_part[:, :], [[0, 1]], base=0, channel_multiplier=1, allow_small_or_imprecise_dtypes=True).then_inc(iotas, 1)

        @block.vector
        def _(dve):
            n = 0

            def chained(ins):
                nonlocal n
                n += 1
                ins.then_inc(step, 1)
                dve.wait_ge(step, n)

            dve.wait_ge(loaded, 4 * 16)
            dve.wait_ge(w_in, 3 * 16)
            chained(dve.scalar_tensor_tensor(e.Wqv[:, 0:P], e.Wqv[:, 0:P], 0.8, e.a_sign[:, :], ALU.mult, ALU.mult))
            chained(dve.tensor_scalar(e.a_sign[:, :], e.a_sign[:, :], 0.0, 2.0, ALU.is_ge, ALU.mult))
            chained(dve.tensor_scalar(e.a_sign[:, :], e.a_sign[:, :], -1.0, None, ALU.add))
            chained(dve.tensor_tensor(e.Wqv[:, 0:P], e.Wqv[:, 0:P], e.a_sign[:, :], ALU.mult))
            dve.wait_ge(iotas, 3)
            dve.tensor_copy(row[:, :, :], row_i[:, :, :])
            chained(dve.tensor_copy(col[:, :, :], col_i[:, :, :]))
            dve.scalar_tensor_tensor(key_row[:, :], row[:, 0, :], float(E), order_row[:, :], ALU.mult, ALU.add)
            dve.tensor_copy(colbc[:, :, :, :], col[:, :, :].unsqueeze(3).broadcast_to([P, 2, EC, P]))
            chained(dve.scalar_tensor_tensor(key_col[:, :], col[:, 0, :], float(E), order_col[:, :], ALU.mult, ALU.add))
            for c in range(EC):
                chained(dve.tensor_scalar(less[:, :], key_row[:, :], key_col[:, c:c + 1], 0.0, ALU.is_lt, ALU.add,
                                          accum_out=rank[:, c:c + 1]))
            for c in range(EC):
                dve.tensor_scalar(perm[:, c, :], order_row[:, :], rank[:, c:c + 1], None, ALU.is_equal).then_inc(evac, 1)
            dve.wait_ge(pe_done, 2)
            dve.tensor_copy(sorted_row[:, 0, :], psS[:, 0:E])
            chained(dve.tensor_copy(sorted_row[:, 1, :], psD[:, 0:E]))
            dve.tensor_scalar(e.ST[:, :], sorted_row[:, 0, :], iota_part[:, :], None, ALU.is_equal)
            chained(dve.tensor_scalar(e.DT[:, :], sorted_row[:, 1, :], iota_part[:, :], None, ALU.is_equal))
            dve.tensor_tensor(e.PT[:, :], e.ST[:, :], e.DT[:, :], ALU.add).then_inc(evac, 1)
            chained(dve.memset(e.cont[:, :], 0.0))
            chained(dve.tensor_tensor(e.cont[:, 1:E], sorted_row[:, 0, 1:E], sorted_row[:, 0, 0:E - 1], ALU.is_equal))
            dve.tensor_scalar(e.reset[:, :], e.cont[:, :], -1.0, BIG, ALU.add, ALU.mult)
            chained(dve.tensor_scalar(e.is_last[:, :], e.cont[:, 1:E + 1], -1.0, 1.0, ALU.mult, ALU.add))
            dve.wait_ge(pe_done, 3)
            dve.tensor_tensor(weight[:, :], psU[:, 0:E], e.ST[:, :], ALU.mult).then_inc(evac, 1)
            dve.wait_ge(pe_done, 5)
            dve.tensor_copy(e.S1[:, :, :], psT[:, 0:EC * P].rearrange("p (c n) -> p c n", c=EC))
            dve.wait_ge(pe_done, 4)
            chained(dve.tensor_scalar(weight[:, :], psW[:, 0:E], EPS_EDGE, None, ALU.add))
            dve.sem_inc(evac, 1)

        @block.tensor
        def _(pe):
            pe.wait_ge(evac, EC)
            for n, ps in enumerate((psS, psD)):
                for c in range(EC):
                    last = pe.matmul(ps[:, 0:E], colbc[:, n, c, :], perm[:, c, :], start=c == 0, stop=c == EC - 1)
                last.then_inc(pe_done, 1)
            pe.wait_ge(evac, EC + 1)
            pe.matmul(psU[:, 0:E], k.adjT[:, :], e.DT[:, :], start=True, stop=True).then_inc(pe_done, 1)
            pe.wait_ge(evac, EC + 2)
            pe.matmul(psW[:, 0:E], k.ones[:, :], weight[:, :], start=True, stop=True).then_inc(pe_done, 1)
            for c in range(EC):
                last = pe.transpose(psT[:, c * P:(c + 1) * P], e.ST[:, c * P:(c + 1) * P], k.ident[:, :])
            last.then_inc(pe_done, 1)

        @block.scalar
        def _(act):
            act.wait_ge(evac, EC + 3)
            act.activation(e.log_w[:, :], weight[:, :], ACT.Ln)


def stage_scores(k, ctx, HT, Xv, scores, e):
    nc = k.nc
    S = 2
    EC, HEADS = k.E // P, k.HEADS
    HW = TB * HEADS
    sem = lambda n: k.sem(n)
    sb = lambda n, s: ctx.enter_context(nc.sbuf_tensor(n, s, F32))
    h, hT, Xq, Qs = (each(S, lambda s: sb(f"l3_{n}{s}", [P, TB, P])) for n in ("h", "hT", "Xq", "Qs"))
    M = each(S, lambda s: sb(f"l3_M{s}", [P, EC, TW]))
    names = ("h", "Tp", "hT", "Q", "V", "Xq", "Xv", "Qs", "lin", "G", "M", "kept")
    R = {n: each(S, lambda s: sem(f"l3_{n}{s}")) for n in names}
    tally = sem("l3_tally")
    n_it = k.B // TB // S
    psT, psQ, psV, psR = k.bank[0:2], k.bank[2:4], k.bank[4:6], k.bank[6:8]
    as_tile = lambda ps: ps[:, :].rearrange("p (b n) -> p b n", b=TB)
    AHEAD = 2
    res = Residual(k, ctx, "l2r", S, lambda t: HT[:, bass.ds(t * TW, TW)], {}, psR)

    def turns(eng, turn):
        with eng.Fori(0, n_it - AHEAD - 1) as i:
            turn(i, True, True, True)
        turn(n_it - AHEAD - 1, False, True, True)
        for i in range(n_it - AHEAD, n_it):
            turn(i, False, False, i < n_it - 1)

    with nc.Block() as block:
        @block.gpsimd
        def _(pool):
            def turn(i, fetching, residual, following):
                for s in range(S):
                    pool.wait_ge(R["lin"][s], i + 1)
                    pool.wait_ge(R["Xq"][s], i + 1)
                    pool.tensor_tensor(out=Qs[s][:, :, :], in0=Xq[s][:, :, :],
                                       in1=e.a_sign[:, :].unsqueeze(1).broadcast_to([P, TB, P]),
                                       op=ALU.mult).then_inc(R["Qs"][s], 1)
                if residual:
                    res.coefficients(pool, i + AHEAD)

            res.ln.open(pool)
            for s in range(S):
                pool.sem_inc(R["Qs"][s], 1)
            for i in range(AHEAD):
                res.coefficients(pool, i)
            turns(pool, turn)

        @block.scalar
        def _(act):
            def normalise(i, s):
                res.ln.wait(act, s, i)
                normalise_tile(act, k, h[s], (i * S + s) * TB).then_inc(R["h"][s], 1)

            def turn(i, fetching, residual, following):
                for s in range(S):
                    act.wait_ge(R["Tp"][s], i + 1)
                    act.activation(hT[s][:, :, :], as_tile(psT[s]), ACT.Copy).then_inc(R["hT"][s], 1)
                if fetching:
                    for s in range(S):
                        act.wait_ge(res.R_ready[s], i + AHEAD + 1)
                        res.fetch(act, i + AHEAD + 1, s)
                for s in range(S):
                    act.wait_ge(R["Qs"][s], i + 1)
                    act.wait_ge(R["Q"][s], i + 1)
                    act.activation(Xq[s][:, :, :], as_tile(psQ[s]), ACT.Copy).then_inc(R["Xq"][s], 1)
                    act.wait_ge(R["V"][s], i + 1)
                    act.activation(Xv[:, bass.ds((i * S + s) * TB, TB), :], as_tile(psV[s]), ACT.Copy).then_inc(R["Xv"][s], 1)
                    if following:
                        normalise(i + 1, s)

            for i in range(AHEAD + 1):
                for s in range(S):
                    if i:
                        act.wait_ge(res.R_ready[s], i)
                    res.fetch(act, i, s)
            for s in range(S):
                normalise(0, s)
            turns(act, turn)

        @block.tensor
        def _(pe):
            def turn(i, fetching, residual, following):
                for s in range(S):
                    pe.wait_ge(R["h"][s], i + 1)
                    for j in range(TB):
                        last = pe.transpose(psT[s][:, j * P:(j + 1) * P], h[s][:, j, :], k.ident[:, :])
                    last.then_inc(R["Tp"][s], 1)
                    if residual:
                        pe.wait_ge(res.updated[s], i + AHEAD)
                        res.turn_over(pe, i + AHEAD, s)
                for s in range(S):
                    pe.wait_ge(R["hT"][s], i + 1)
                    pe.wait_ge(R["M"][s], i + 1)
                    for n, (ps, done) in enumerate(((psQ[s], R["Q"][s]), (psV[s], R["V"][s]))):
                        for j in range(TB):
                            last = pe.matmul(ps[:, j * P:(j + 1) * P], hT[s][:, j, :], e.Wqv[:, n * P:(n + 1) * P],
                                             start=True, stop=True)
                        last.then_inc(done, 1)
                for s in range(S):
                    for c, (ps, free) in enumerate(((psQ[s], R["Xq"][s]), (psV[s], R["Xv"][s]))):
                        pe.wait_ge(free, i + 1)
                        pe.matmul(ps[:, :], e.PT[:, c * P:(c + 1) * P], Xq[s][:, :, :], start=True, stop=True).then_inc(R["G"][s], 1)

            for s in range(S):
                pe.sem_inc(R["M"][s], 1)
            for i in range(AHEAD):
                for s in range(S):
                    if i:
                        pe.wait_ge(res.updated[s], i)
                    res.turn_over(pe, i, s)
            turns(pe, turn)

        @block.vector
        def _(dve):
            def turn(i, fetching, residual, following):
                if residual:
                    res.update(dve, i + AHEAD)
                for s in range(S):
                    dve.wait_ge(R["kept"][s], i + 1)
                    for c, ps in enumerate((psQ[s], psV[s])):
                        dve.wait_ge(R["G"][s], EC * i + c + 1)
                        last = dve.scalar_tensor_tensor(M[s][:, c, :].rearrange("p (b n) -> p b n", b=TB), as_tile(ps), 0.0,
                                                        e.a_sign[:, :].unsqueeze(1).broadcast_to([P, TB, P]),
                                                        ALU.max, ALU.mult)
                    last.then_inc(R["M"][s], 1)
                for s in range(S):
                    dve.wait_ge(R["M"][s], i + 2)
                    dve.sem_inc(tally, 1)
                    dve.tensor_reduce(scores[:, :, bass.ds((i * S + s) * HW, HW)],
                                      M[s][:, :, :].rearrange("p c (x d) -> p c x d", x=HW),
                                      mybir.AxisListType.X, ALU.add).then_inc(R["kept"][s], 1)
                for s in range(S):
                    dve.wait_ge(R["Qs"][s], i + 2)
                    dve.sem_inc(tally, 1)
                    dve.tensor_reduce(e.q_sums[:, bass.ds((i * S + s) * HW, HW)],
                                      Qs[s][:, :, :].rearrange("p b (x d) -> p (b x) d", x=HEADS),
                                      mybir.AxisListType.X, ALU.add).then_inc(R["lin"][s], 1)

            for s in range(S):
                dve.sem_inc(R["kept"][s], 1)
                dve.sem_inc(R["lin"][s], 1)
            for i in range(AHEAD):
                res.update(dve, i)
            turns(dve, turn)


def stage_softmax(k, ctx, scores, e):
    nc = k.nc
    E, EC = k.E, k.E // P
    NQ = k.B * k.HEADS // P
    sem = lambda n: k.sem(n)
    sb = lambda n, s: ctx.enter_context(nc.sbuf_tensor(n, s, F32))
    r, m, w = (each(NQ, lambda q: sb(f"sm_{n}{q}", [P, E])) for n in ("r", "m", "w"))
    turned, shifted, exped, attn_ready, back, step = (sem(f"sm_{n}") for n in ("turned", "shifted", "exp", "attn", "back", "step"))
    linear, summed = sem("sm_linear"), sem("sm_summed")

    with nc.Block() as block:
        @block.tensor
        def _(pe):
            for c in range(EC):
                pe.matmul(k.bank[4 + c][:, :], e.PT[:, c * P:(c + 1) * P], e.q_sums[:, :], start=True, stop=True).then_inc(linear, 1)
            pe.wait_ge(summed, 1)
            for q in range(NQ):
                for c in range(EC):
                    last = pe.transpose(k.bank[q][:, c * P:(c + 1) * P], scores[:, c, q * P:(q + 1) * P], k.ident[:, :])
                last.then_inc(turned, 1)
            for q in range(NQ):
                pe.wait_ge(attn_ready, q + 1)
                for c in range(EC):
                    last = pe.transpose(k.bank[4 + q][:, c * P:(c + 1) * P], r[q][:, c * P:(c + 1) * P], k.ident[:, :])
                last.then_inc(back, 1)

        @block.scalar
        def _(act):
            for q in range(NQ):
                act.wait_ge(shifted, q + 1)
                act.activation(r[q][:, :], r[q][:, :], ACT.Exp).then_inc(exped, 1)

        @block.vector
        def _(dve):
            n = 0

            def wave(make):
                nonlocal n
                for q in range(NQ):
                    make(q).then_inc(step, 1)
                n += NQ

            def after(q):
                dve.wait_ge(step, n - NQ + q + 1)

            def score_in(q):
                dve.wait_ge(turned, q + 1)
                return dve.tensor_tensor(r[q][:, :], k.bank[q][:, 0:E], e.log_w[:, :], ALU.add)

            def max_forward(q):
                after(q)
                return dve.tensor_tensor_scan(m[q][:, :], e.reset[:, 0:E], r[q][:, :], 0.0, ALU.add, ALU.max)

            def max_backward(q):
                after(q)
                return dve.tensor_tensor_scan(w[q][:, ::-1], e.reset[:, E:0:-1], m[q][:, ::-1], 0.0, ALU.add, ALU.max)

            def subtract_max(q):
                after(q)
                return dve.tensor_tensor(r[q][:, :], r[q][:, :], w[q][:, :], ALU.subtract)

            for c in range(EC):
                dve.wait_ge(linear, c + 1)
                last = dve.scalar_tensor_tensor(scores[:, c, :], k.bank[4 + c][:, :], 0.25, scores[:, c, :], ALU.mult, ALU.add)
            last.then_inc(summed, 1)
            wave(score_in)
            wave(max_forward)
            wave(max_backward)
            n_before = n
            for q in range(NQ):
                dve.wait_ge(step, n_before - NQ + q + 1)
                dve.tensor_tensor(r[q][:, :], r[q][:, :], w[q][:, :], ALU.subtract).then_inc(shifted, 1)

            def sum_forward(q):
                dve.wait_ge(exped, q + 1)
                return dve.tensor_tensor_scan(m[q][:, :], e.cont[:, 0:E], r[q][:, :], 0.0, ALU.mult, ALU.add)

            def keep_last(q):
                after(q)
                return dve.tensor_tensor(m[q][:, :], m[q][:, :], e.is_last[:, :], ALU.mult)

            def sum_backward(q):
                after(q)
                return dve.tensor_tensor_scan(w[q][:, ::-1], e.cont[:, E:0:-1], m[q][:, ::-1], 0.0, ALU.mult, ALU.add)

            def invert(q):
                after(q)
                return dve.reciprocal(w[q][:, :], w[q][:, :])

            wave(sum_forward)
            wave(keep_last)
            wave(sum_backward)
            wave(invert)
            for q in range(NQ):
                dve.wait_ge(step, n - NQ + q + 1)
                dve.tensor_tensor(r[q][:, :], r[q][:, :], w[q][:, :], ALU.mult).then_inc(attn_ready, 1)
            for q in range(NQ):
                dve.wait_ge(back, q + 1)
                dve.tensor_copy(scores[:, :, q * P:(q + 1) * P],
                                k.bank[4 + q][:, 0:E].rearrange("p (c x) -> p c x", c=EC))


def stage_attend(k, ctx, Xv, attn, e, out):
    nc, X = k.nc, k.X
    S = 2
    EC, HEADS, DH = k.E // P, k.HEADS, k.DH
    sem = lambda n: k.sem(n)
    sb = lambda n, s: ctx.enter_context(nc.sbuf_tensor(n, s, F32))
    Vw, YT = each(S, lambda s: sb(f"at_v{s}", [P, EC, TW])), each(S, lambda s: sb(f"at_y{s}", [P, TB, P]))
    R = {n: each(S, lambda s: sem(f"at_{n}{s}")) for n in ("V0", "V1", "Vw", "Yp", "YT", "Op", "O")}
    stored = sem("out_stored")
    n_it = k.B // TB // S
    psV0, psV1, psY, psO = k.bank[0:2], k.bank[2:4], k.bank[4:6], k.bank[6:8]

    with nc.Block() as block:
        @block.tensor
        def _(pe):
            with pe.Fori(0, n_it) as i:
                for s in range(S):
                    v = Xv[:, bass.ds((i * S + s) * TB, TB), :]
                    pe.matmul(psV0[s][:, :], e.DT[:, 0:P], v, start=True, stop=True).then_inc(R["V0"][s], 1)
                    pe.matmul(psV1[s][:, :], e.DT[:, P:2 * P], v, start=True, stop=True).then_inc(R["V1"][s], 1)
                for s in range(S):
                    pe.wait_ge(R["Vw"][s], i + 1)
                    for j in range(TB):
                        for c in range(EC):
                            last = pe.matmul(psY[s][:, j * P:(j + 1) * P], Vw[s][:, c, j * P:(j + 1) * P], e.S1[:, c, :],
                                             start=c == 0, stop=c == EC - 1)
                    last.then_inc(R["Yp"][s], 1)
                for s in range(S):
                    pe.wait_ge(R["YT"][s], i + 1)
                    for j in range(TB):
                        last = pe.matmul(psO[s][:, j * P:(j + 1) * P], YT[s][:, j, :], e.WoT[:, :], start=True, stop=True)
                    last.then_inc(R["Op"][s], 1)

        @block.scalar
        def _(act):
            with act.Fori(0, n_it) as i:
                for s in range(S):
                    act.wait_ge(R["Yp"][s], i + 1)
                    act.activation(YT[s][:, :, :], psY[s][:, :].rearrange("p (b n) -> p b n", b=TB), ACT.Copy).then_inc(R["YT"][s], 1)

        @block.vector
        def _(dve):
            with dve.Fori(0, n_it) as i:
                for s in range(S):
                    t = i * S + s
                    for c, ps in enumerate((psV0, psV1)):
                        dve.wait_ge(R[f"V{c}"][s], i + 1)
                        w = attn[:, c, bass.ds(t * TB * HEADS, TB * HEADS)]
                        last = dve.tensor_tensor(Vw[s][:, c, :].rearrange("p (x y) -> p x y", y=DH),
                                                 ps[s][:, :].rearrange("p (x y) -> p x y", y=DH),
                                                 w.unsqueeze(2).broadcast_to([P, TB * HEADS, DH]), ALU.mult)
                    last.then_inc(R["Vw"][s], 1)
                for s in range(S):
                    xt = X[:, bass.ds((i * S + s) * TB, TB), :]
                    dve.wait_ge(R["Op"][s], i + 1)
                    dve.tensor_tensor(xt, psO[s][:, :].rearrange("p (b n) -> p b n", b=TB), xt, ALU.add).then_inc(R["O"][s], 1)

        @block.sync
        def _(sp):
            with sp.Fori(0, n_it) as i:
                for s in range(S):
                    b0 = (i * S + s) * TB
                    sp.wait_ge(R["O"][s], i + 1)
                    sp.dma_start(out[:, bass.ds(b0, TB), :], X[:, bass.ds(b0, TB), :]).then_inc(stored, 16)
            sp.wait_ge(stored, n_it * S * 16)


def build(nc, d, out):
    _, B, _ = d["x"].shape
    k, e = Shared(), Shared()
    k.nc, k.B, k.E, k.HEADS = nc, B, d["src"].shape[0], 4
    k.DH = P // k.HEADS
    with ExitStack() as ctx:
        sb = lambda n, s: ctx.enter_context(nc.sbuf_tensor(n, s, F32))
        k.X = sb("X", [P, B, P])
        k.adjT, k.AhatT, k.ident, k.ones = (sb(n, [P, P]) for n in ("adjT", "AhatT", "ident", "ones"))
        k.W1T, k.W2T, k.Wg = sb("W1T", [P, 2 * P]), sb("W2T", [P, 2, P]), sb("Wg", [P, 2, P])
        k.cols, k.rows = sb("cols", [P, NCOLS]), sb("rows", [P, 3, P])
        k.rstd, k.nmr = sb("rstd", [P, B]), sb("nmr", [P, B])
        k.zero = sb("zero", [P, 1])
        k.ln_const = {n: sb(f"ln_const{m}", [P, B // 4]) for m, n in enumerate(("-half", "two"))}
        k.bank = each(8, lambda n: ctx.enter_context(nc.psum_tensor(f"bank{n}", [P, TW], F32)))

        with ExitStack() as c0:
            k.W0 = c0.enter_context(nc.sbuf_tensor("W0", [P, 3, P], F32))
            k.A12T = c0.enter_context(nc.sbuf_tensor("A12T", [P, 2, P], F32))
            k.diag_bc = c0.enter_context(nc.sbuf_tensor("diag_bc", [P, P], F32))
            with ExitStack() as c:
                stage_setup(k, c, d)
            with ExitStack() as c:
                stage_layer0(k, c)

        with ExitStack() as c12:
            Y0 = c12.enter_context(nc.sbuf_tensor("Y0", [P, B * P], F32))
            bno6 = c12.enter_context(nc.sbuf_tensor("bno6", [P, 1, B // TB, 6], F32))
            with ExitStack() as c1:
                bn6 = c1.enter_context(nc.sbuf_tensor("bn6", [P, 2, B // TB, 6], F32))
                Y1 = c1.enter_context(nc.sbuf_tensor("Y1", [P, B * P], F32))
                with ExitStack() as c:
                    stage_gcn_hidden(k, c, (Y0, Y1), bn6)
                with ExitStack() as c:
                    stage_gcn_out(k, c, (Y0, Y1), bn6, bno6)
            k.recycle_semaphores()
            HT = Y0
            with ExitStack() as c2:
                sbr = lambda n, s: c2.enter_context(nc.sbuf_tensor(n, s, F32R))
                k.Wih, k.Whh = ([sbr(f"{n}_{part}", [P, 4, 4 * P]) for part in ("hi", "lo")] for n in ("Wih", "Whh"))
                k.lstm_bias = c2.enter_context(nc.sbuf_tensor("lstm_bias", [P, 4, 4], F32))
                with ExitStack() as c:
                    stage_conv(k, c, Y0, bno6, HT)
                with ExitStack() as c:
                    stage_lstm_weights(k, c, d)
                with ExitStack() as c:
                    bufs = {"gates": each(2, lambda s: c.enter_context(nc.sbuf_tensor(f"gates{s}", [P, 4, TW], F32)))}
                    for n in ("cell", "hid", "hid_hi", "hid_lo", "x_hi", "x_lo"):
                        bufs[n] = each(2, lambda s: c.enter_context(nc.sbuf_tensor(f"lstm_{n}{s}", [P, TW], F32R if "_" in n else F32)))
                    sems = {n: each(2, lambda s: each(4, lambda g: k.sem(f"lstm_{n}{s}{g}"))) for n in ("done", "act")}
                    for n in ("cell", "tanh", "h", "hh", "hl", "fc", "ig", "xh", "xl", "x_free", "x_tally"):
                        sems[n] = each(2, lambda s: k.sem(f"lstm_{n}_ready{s}"))
                    used = {"done": [0] * 4, "seq": 0, "rec": 0}
                    for p in range(1, 5):
                        stage_lstm(k, c, HT, p, bufs, sems, used)
            k.recycle_semaphores()
            with ExitStack() as c3:
                sb3 = lambda n, s: c3.enter_context(nc.sbuf_tensor(n, s, F32))
                E, EC = k.E, k.E // P
                e.Wqv, e.WoT, e.a_sign = sb3("Wqv", [P, 2 * P]), sb3("WoT", [P, P]), sb3("a_sign", [P, P])
                e.q_sums = sb3("q_sums", [P, B * k.HEADS])
                e.ST, e.DT, e.PT = (sb3(n, [P, E]) for n in ("ST", "DT", "PT"))
                e.S1, e.cont, e.reset, e.is_last, e.log_w = (sb3("S1", [P, EC, P]), sb3("cont", [P, E + 1]), sb3("reset", [P, E + 1]),
                                                             sb3("is_last", [P, E]), sb3("log_w", [P, E]))
                scores, Xv = sb3("scores", [P, EC, B * k.HEADS]), HT[:, :].rearrange("p (b n) -> p b n", n=P)
                with ExitStack() as c:
                    stage_edges(k, c, d, e)
                with ExitStack() as c:
                    stage_scores(k, c, HT, Xv, scores, e)
                with ExitStack() as c:
                    stage_softmax(k, c, scores, e)
                with ExitStack() as c:
                    stage_attend(k, c, Xv, scores, e, out)


def kernel(**inputs):
    import numpy as np
    import concourse.bacc as bacc
    from concourse.bass_utils import run_bass_kernel_spmd

    g = {n: np.asarray(a) for n, a in inputs.items()}
    B, N, D = g["x"].shape
    per_channel = [g["L1_gnn_b1"].reshape(2, P), g["L1_gnn_g1"].reshape(2, P), g["L1_gnn_be1"].reshape(2, P),
                   g["L1_gnn_b2"].reshape(1, P), g["L1_gnn_g2"].reshape(1, P), g["L1_gnn_be2"].reshape(1, P),
                   g["L2_gnn_bih"].reshape(16, P), g["L2_gnn_bhh"].reshape(16, P)]
    layout = {
        "x": g["x"].transpose(1, 0, 2),
        "adj": g["adj"], "adjT": g["adj"].T,
        "cols": np.concatenate(per_channel, axis=0).T,
        "rows": np.stack([g["L0_gnn_bias"], g["L2_gnn_bg0"], g["L2_gnn_bg1"]]),
        "L0_W": g["L0_gnn_W"], "W1T": g["L1_gnn_W1"].T, "W2T": g["L1_gnn_W2"].T,
        "Wg0": g["L2_gnn_Wg0"], "Wg1": g["L2_gnn_Wg1"],
        "WihT": g["L2_gnn_Wih"].transpose(0, 2, 1), "WhhT": g["L2_gnn_Whh"].transpose(0, 2, 1),
        "Wqv": np.concatenate([g["L3_gnn_W_lin"].T, g["L3_gnn_W_val"].T], axis=1), "WoT": g["L3_gnn_W_out"].T,
        "a": g["L3_gnn_a"].reshape(D),
        "src": g["L3_gnn_src"], "dst": g["L3_gnn_dst"],
        "src_col": g["L3_gnn_src"].reshape(-1, P).T, "dst_col": g["L3_gnn_dst"].reshape(-1, P).T,
    }
    nc = bacc.Bacc("TRN2", target_bir_lowering=False, num_devices=1, dynamic_dma_scratch_size=2048)
    arrays, d = {}, {}
    for name, a in layout.items():
        arrays[f"in_{name}"] = np.ascontiguousarray(a)
        d[name] = nc.dram_tensor(f"in_{name}", a.shape, mybir.dt.from_np(a.dtype), kind="ExternalInput").ap()
    out = nc.dram_tensor("out", (N, B, D), F32, kind="ExternalOutput").ap()
    build(nc, d, out)
    r = run_bass_kernel_spmd(nc, [arrays], core_ids=[0])
    return np.ascontiguousarray(r.results[0]["out"].transpose(1, 0, 2))
```

```python
from contextlib import ExitStack

import concourse.bass as bass
from concourse import mybir

ALU = mybir.AluOpType
ACT = mybir.ActivationFunctionType
F32 = mybir.dt.float32
F32R = mybir.dt.float32r
I32 = mybir.dt.int32
P = 128
EPS = 1e-5
EPS_EDGE = 1e-8
TB = 4
TW = TB * P
BIG = 1.0e30

C_B1, C_G1, C_BE1 = 0, 2, 4
C_B2, C_G2, C_BE2 = 6, 7, 8
C_BIH, C_BHH = 9, 25
C_BG0 = 41
NCOLS = 42
R_L0, R_G1 = 0, 1


class Shared:
    sems = ()

    def sem(self, name):
        handle = self.nc.alloc_semaphore(name)
        self.sems += (handle,)
        return handle

    def recycle_semaphores(self):
        self.nc.clear_and_free_semaphores(list(self.sems))
        self.nc.all_engine_barrier()
        self.sems = ()


def each(n, make):
    return [make(i) for i in range(n)]


class LayerNormTail:

    GROUPS = 5

    def __init__(self, k, ctx, name, S, nb=TB, per=2):
        sb = lambda n: ctx.enter_context(k.nc.sbuf_tensor(f"{name}_{n}", [P, per * nb], F32))
        self.k, self.S, self.nb, self.per, self.batches = k, S, nb, per, S // per
        self.st6 = ctx.enter_context(k.nc.sbuf_tensor(f"{name}_st6", [P, S * nb, 6], F32))
        self.sum, self.diff, self.m2 = sb("sum"), sb("diff"), sb("m2")
        self.stats_ready = each(S, lambda s: k.sem(f"{name}_stats{s}"))
        self.stats_free, self.ready = (each(S // per, lambda q: k.sem(f"{name}_{n}{q}")) for n in ("stfree", "coef"))
        self.step, self.tally, self.dve_tally = (k.sem(f"{name}_{n}") for n in ("step", "tally", "dve_tally"))

    def open(self, pool):
        for free in self.stats_free:
            pool.sem_inc(free, 1)

    def wait(self, eng, s, turn):
        eng.wait_ge(self.ready[s // self.per], turn + 1)

    def stats(self, dve, xt, s, turn):
        dve.wait_ge(self.stats_free[s // self.per], turn + 1)
        dve.sem_inc(self.dve_tally, 1)
        for j in range(self.nb):
            last = dve.bn_stats(self.st6[:, s * self.nb + j, :], xt[:, j, :])
        last.then_inc(self.stats_ready[s], 1)

    def coefficients(self, pool, turn):
        for q in range(self.batches):
            self.batch(pool, turn, q)

    def batch(self, pool, turn, q):
        k, c = self.k, self.k.ln_const
        width = self.per * self.nb
        st6 = self.st6[:, q * width:(q + 1) * width, :]
        su, di, m2 = self.sum[:, :], self.diff[:, :], self.m2[:, :]
        base = (turn * self.batches + q) * self.GROUPS
        rows = bass.ds((turn * self.batches + q) * width, width)
        rstd, nmr = k.rstd[:, rows], k.nmr[:, rows]

        def tt(out, a, b, op):
            return pool.tensor_tensor(out=out, in0=a, in1=b, op=op)

        def group(n):
            pool.wait_ge(self.step, base + n)
            pool.sem_inc(self.tally, 1)

        for s in range(q * self.per, (q + 1) * self.per):
            pool.wait_ge(self.stats_ready[s], turn + 1)
        pool.sem_inc(self.tally, 1)
        tt(su, st6[:, :, 1], st6[:, :, 4], ALU.add)
        tt(di, st6[:, :, 1], st6[:, :, 4], ALU.subtract)
        tt(m2, st6[:, :, 2], st6[:, :, 5], ALU.add).then_inc(self.step, 1)
        group(1)
        pool.sem_inc(self.stats_free[q], 1)
        tt(di, di, di, ALU.mult)
        pool.tensor_scalar(su, su, -1.0, 0.0, ALU.mult, ALU.add)
        pool.tensor_scalar(m2, m2, 4.0 / P, 4.0 * EPS, ALU.mult, ALU.add).then_inc(self.step, 1)
        group(2)
        tt(m2, m2, di, ALU.add).then_inc(self.step, 1)
        group(3)
        tt(m2, m2, c["-half"][:, 0:width], ALU.pow).then_inc(self.step, 1)
        group(4)
        tt(rstd, m2, c["two"][:, 0:width], ALU.mult)
        tt(nmr, su, m2, ALU.mult).then_inc(self.step, 1)
        pool.wait_ge(self.step, base + 5)
        pool.sem_inc(self.ready[q], 1)


def normalise_tile(act, k, h, b0):
    for j in range(TB):
        last = act.activation(h[:, j, :], k.X[:, bass.ds(b0, TB), :][:, j, :], ACT.Relu,
                              bias=k.nmr[:, bass.ds(b0, TB)][:, j:j + 1], scale=k.rstd[:, bass.ds(b0, TB)][:, j:j + 1])
    return last


def exists(t, tiles):
    return not isinstance(t, int) or 0 <= t < tiles


def since(t, back):
    return not isinstance(t, int) or t >= back


def looped(eng, n, turn):
    with eng.Fori(0, n - 1) as i:
        turn(i, True)
    turn(n - 1, False)


def stage_setup(k, ctx, d, e):
    nc, X = k.nc, k.X
    sem = lambda n: k.sem(n)
    sb = lambda n, s, t=F32: ctx.enter_context(nc.sbuf_tensor(n, s, t))
    CH = 8
    CB = k.B // CH
    k.x_in = each(CH, lambda c: sem(f"x_in{c}"))
    e.loaded, e.w_in = sem("edges_in"), sem("l3_w_in")
    adj_in, w_in, cols_in = sem("adj_in"), sem("w_in"), sem("cols_in")
    cst, masks, deg, dinv_p, dinv_bc, ahat = (sem(n) for n in ("cst", "masks", "deg", "dinv_p", "dinv_bc", "ahat"))
    diag_ready, sep = (sem(n) for n in ("diag_ready", "setup_sep"))
    adj = sb("adj_rows", [P, P])
    onesPP = k.ones
    rs = sb("deg_parts", [P, 4])
    tmp = sb("setup_tmp", [P, P])
    tmp2 = sb("setup_tmp2", [P, P])
    dinv = sb("dinv", [P, 1])
    bank_dg, bank_di = k.bank[0], k.bank[1]

    with nc.Block() as block:
        @block.sync
        def _(sp):
            sp.dma_start(adj[:, :], d["adj"]).then_inc(adj_in, 16)
            sp.dma_start(k.adjT[:, :], d["adjT"]).then_inc(adj_in, 16)
            for n, name in enumerate(("src", "dst")):
                sp.dma_start(e.row_i[:, n, :], d[name].rearrange("(a e) -> a e", a=1).partition_broadcast(P)
                             .rearrange("p a e -> p (a e)")).then_inc(e.loaded, 16)
                sp.dma_start(e.col_i[:, n, :], d[name + "_col"]).then_inc(e.loaded, 16)
            sp.dma_start(e.Wqv[:, :], d["Wqv"]).then_inc(e.w_in, 16)
            sp.dma_start(e.WoT[:, :], d["WoT"]).then_inc(e.w_in, 16)
            sp.dma_start(e.a_sign[:, :], d["a"].rearrange("(o a) -> o a", o=1).partition_broadcast(P)
                         .rearrange("p o a -> p (o a)")).then_inc(e.w_in, 16)
            for c in range(CH):
                sp.dma_start(X[:, c * CB:(c + 1) * CB, :], d["x"][:, c * CB:(c + 1) * CB, :]).then_inc(k.x_in[c], 16)

        @block.scalar
        def _(act):
            act.dma_start(k.cols[:, :], d["cols"]).then_inc(cols_in, 16)
            act.dma_start(k.rows[:, :, :], d["rows"].partition_broadcast(P)).then_inc(cols_in, 16)
            act.dma_start(k.W0[:, :, :], d["L0_W"].rearrange("k f o -> f k o")).then_inc(w_in, 16)
            act.dma_start(k.W1T[:, :], d["W1T"]).then_inc(w_in, 16)
            act.dma_start(k.W2T[:, :, :], d["W2T"].rearrange("(h c) o -> c h o", h=2)).then_inc(w_in, 16)
            act.dma_start(k.Wg[:, 0, :], d["Wg0"]).then_inc(w_in, 16)
            act.dma_start(k.Wg[:, 1, :], d["Wg1"]).then_inc(w_in, 16)
            act.wait_ge(w_in, 5 * 16)
            act.wait_ge(cols_in, 2 * 16)

        @block.gpsimd
        def _(pool):
            for name, value in (("-half", -0.5), ("two", 2.0)):
                pool.memset(k.ln_const[name][:, :], value)
            pool.memset(k.zero[:, :], 0.0)
            pool.memset(onesPP[:, :], 1.0).then_inc(cst, 1)
            pool.memset(k.ident[:, :], 0.0).then_inc(sep, 1)
            pool.wait_ge(sep, 1)
            pool.affine_select(out=k.ident[:, :], in_=k.ident[:, :], compare_op=ALU.not_equal, fill=1.0,
                               base=0, pattern=[[-1, P]], channel_multiplier=1).then_inc(cst, 1)
            pool.wait_ge(adj_in, 32)
            pool.affine_select(out=k.A12T[:, 0, :], in_=k.adjT[:, :], compare_op=ALU.is_gt, fill=0.0,
                               base=0, pattern=[[-1, P]], channel_multiplier=1).then_inc(masks, 1)
            pool.affine_select(out=k.A12T[:, 1, :], in_=k.adjT[:, :], compare_op=ALU.is_gt, fill=0.0,
                               base=0, pattern=[[1, P]], channel_multiplier=-1).then_inc(masks, 1)
            pool.wait_ge(deg, 5)
            pool.tensor_tensor(out=dinv[:, :], in0=rs[:, 3:4], in1=k.ln_const["-half"][:, 0:1], op=ALU.pow).then_inc(dinv_p, 1)

        @block.tensor
        def _(pe):
            pe.wait_ge(cst, 2)
            pe.wait_ge(deg, 1)
            pe.matmul(bank_dg[:, 0:P], onesPP[:, :], tmp[:, :], start=True, stop=True).then_inc(diag_ready, 1)
            pe.wait_ge(dinv_bc, 1)
            pe.matmul(bank_di[:, 0:P], onesPP[:, :], tmp2[:, :], start=True, stop=True).then_inc(diag_ready, 1)

        @block.vector
        def _(dve):
            dve.wait_ge(adj_in, 32)
            dve.wait_ge(cst, 2)
            dve.tensor_tensor(tmp[:, :], adj[:, :], k.ident[:, :], ALU.mult).then_inc(deg, 1)
            dve.wait_ge(deg, 1)
            dve.reduce_sum(rs[:, 0:1], adj[:, :], mybir.AxisListType.X)
            dve.reduce_sum(rs[:, 1:2], k.adjT[:, :], mybir.AxisListType.X)
            dve.reduce_sum(rs[:, 2:3], tmp[:, :], mybir.AxisListType.X).then_inc(deg, 1)
            dve.wait_ge(deg, 2)
            dve.tensor_tensor(rs[:, 0:1], rs[:, 0:1], rs[:, 1:2], ALU.add).then_inc(deg, 1)
            dve.wait_ge(deg, 3)
            dve.tensor_tensor(rs[:, 3:4], rs[:, 0:1], rs[:, 2:3], ALU.subtract).then_inc(deg, 1)
            dve.wait_ge(deg, 4)
            dve.tensor_scalar(rs[:, 3:4], rs[:, 3:4], 1.0, None, ALU.add).then_inc(deg, 1)
            dve.tensor_tensor(k.AhatT[:, :], k.adjT[:, :], k.ident[:, :], ALU.add).then_inc(ahat, 1)
            dve.wait_ge(dinv_p, 1)
            dve.tensor_scalar(tmp2[:, :], k.ident[:, :], dinv[:, :], None, ALU.mult).then_inc(dinv_bc, 1)
            dve.wait_ge(ahat, 1)
            dve.tensor_scalar(k.AhatT[:, :], k.AhatT[:, :], dinv[:, :], None, ALU.mult).then_inc(ahat, 1)
            dve.wait_ge(diag_ready, 1)
            dve.tensor_copy(k.diag_bc[:, :], bank_dg[:, 0:P])
            dve.wait_ge(diag_ready, 2)
            dve.wait_ge(ahat, 2)
            dve.tensor_tensor(k.AhatT[:, :], bank_di[:, 0:P], k.AhatT[:, :], ALU.mult).then_inc(ahat, 1)

def stage_layer0(k, ctx):
    nc, X = k.nc, k.X
    S = k.x_ln.S
    sem = lambda n: k.sem(n)
    sb = lambda n, s: ctx.enter_context(nc.sbuf_tensor(n, s, F32))
    h = each(S, lambda s: sb(f"l0_h{s}", [P, TB, P]))
    Z0 = each(S, lambda s: sb(f"l0_z0{s}", [P, TB, P]))
    Z12 = each(S, lambda s: sb(f"l0_z12{s}", [P, TB, 2, P]))
    h_hi, h_lo = (each(S, lambda s: ctx.enter_context(nc.sbuf_tensor(f"l0_{n}{s}", [P, TB, P], F32R))) for n in ("h_hi", "h_lo"))
    A_hi, A_lo = (ctx.enter_context(nc.sbuf_tensor(f"l0_{n}", [P, 2, P], F32R)) for n in ("A_hi", "A_lo"))
    hi_ready, lo_ready = (each(S, lambda s: sem(f"l0_{n}{s}")) for n in ("hi", "lo"))
    A_ready = sem("l0_A")
    psT, psA, psB, psO = k.bank[0:2], k.bank[2:4], k.bank[4:6], k.bank[6:8]
    h_ready = each(S, lambda s: sem(f"l0_h_ready{s}"))
    T_ready, AB_ready = each(S, lambda s: sem(f"l0_T_ready{s}")), each(S, lambda s: sem(f"l0_AB_ready{s}"))
    Z0_ready, Z12_ready = each(S, lambda s: sem(f"l0_Z0_ready{s}")), each(S, lambda s: sem(f"l0_Z12_ready{s}"))
    out_ready, biased, updated = (each(S, lambda s: sem(f"l0_{n}{s}")) for n in ("out_ready", "biased", "updated"))
    ln, x_ln, AHEAD = LayerNormTail(k, ctx, "l0", S), k.x_ln, k.X_AHEAD
    n_it = k.B // TB // S
    tile = lambda i, s: X[:, bass.ds((i * S + s) * TB, TB), :]

    with nc.Block() as block:
        @block.gpsimd
        def _(pool):
            def turn(i, more):
                if more:
                    x_ln.coefficients(pool, i + AHEAD)
                ln.coefficients(pool, i)

            ln.open(pool)
            with pool.Fori(0, n_it - AHEAD) as i:
                turn(i, True)
            for i in range(n_it - AHEAD, n_it):
                turn(i, False)

        @block.scalar
        def _(act):
            def normalise(i):
                for s in range(S):
                    x_ln.wait(act, s, i)
                    normalise_tile(act, k, h[s], (i * S + s) * TB).then_inc(h_ready[s], 1)
                    act.wait_ge(h_ready[s], i + 1)
                    act.activation(h_hi[s][:, :, :], h[s][:, :, :], ACT.Copy).then_inc(hi_ready[s], 1)

            def turn(i, ahead):
                for s in range(S):
                    act.wait_ge(AB_ready[s], i + 1)
                    act.activation(Z12[s][:, 0:2, :, :], psA[s][:, :], ACT.Copy)
                    act.activation(Z12[s][:, 2:4, :, :], psB[s][:, :], ACT.Copy).then_inc(Z12_ready[s], 1)
                if ahead:
                    normalise(i + 1)

            normalise(0)
            looped(act, n_it, turn)

        @block.tensor
        def _(pe):
            pe.wait_ge(A_ready, 2)
            with pe.Fori(0, n_it) as i:
                for s in range(S):
                    pe.wait_ge(h_ready[s], i + 1)
                    for j in range(TB):
                        last = pe.transpose(psT[s][:, j * P:(j + 1) * P], h[s][:, j, :], k.ident[:, :])
                    last.then_inc(T_ready[s], 1)
                    pe.wait_ge(lo_ready[s], i + 1)
                    for j in range(TB):
                        out = (psA, psB)[j // 2][s][:, (j % 2) * 2 * P:(j % 2 + 1) * 2 * P]
                        pe.matmul(out, h_hi[s][:, j, :], A_hi[:, :, :], start=True, stop=False)
                        pe.matmul(out, h_hi[s][:, j, :], A_lo[:, :, :], start=False, stop=False)
                        last = pe.matmul(out, h_lo[s][:, j, :], A_hi[:, :, :], start=False, stop=True)
                    last.then_inc(AB_ready[s], 1)
                for s in range(S):
                    pe.wait_ge(Z0_ready[s], i + 1)
                    pe.wait_ge(Z12_ready[s], i + 1)
                    for j in range(TB):
                        o = psO[s][:, j * P:(j + 1) * P]
                        pe.matmul(o, Z0[s][:, j, :], k.W0[:, 0, :], start=True, stop=False)
                        pe.matmul(o, Z12[s][:, j, 0, :], k.W0[:, 1, :], start=False, stop=False)
                        last = pe.matmul(o, Z12[s][:, j, 1, :], k.W0[:, 2, :], start=False, stop=True)
                    last.then_inc(out_ready[s], 1)

        @block.vector
        def _(dve):
            def h_low(i, s):
                dve.wait_ge(hi_ready[s], i + 1)
                dve.tensor_tensor(h_lo[s][:, :, :], h[s][:, :, :], h_hi[s][:, :, :], ALU.subtract).then_inc(lo_ready[s], 1)

            def turn(i, more, following=True):
                for s in range(S):
                    dve.wait_ge(T_ready[s], i + 1)
                    dve.tensor_tensor(Z0[s][:, :, :], psT[s][:, :].rearrange("p (b n) -> p b n", b=TB),
                                      k.diag_bc[:, :].unsqueeze(1).broadcast_to([P, TB, P]),
                                      ALU.mult).then_inc(Z0_ready[s], 1)
                    dve.tensor_tensor(tile(i, s), tile(i, s), k.rows[:, R_L0:R_L0 + 1, :].broadcast_to([P, TB, P]),
                                      ALU.add).then_inc(biased[s], 1)
                if more:
                    k.x_stats(dve, i + AHEAD)
                for s in range(S):
                    if following:
                        h_low(i + 1, s)
                    dve.wait_ge(biased[s], i + 1)
                    dve.wait_ge(out_ready[s], i + 1)
                    dve.tensor_tensor(tile(i, s), psO[s][:, :].rearrange("p (b n) -> p b n", b=TB), tile(i, s),
                                      ALU.add).then_inc(updated[s], 1)
                for s in range(S):
                    dve.wait_ge(updated[s], i + 1)
                    ln.stats(dve, tile(i, s), s, i)

            split_float32(dve, k.A12T[:, :, :], A_hi[:, :, :], A_lo[:, :, :], A_ready, 1).then_inc(A_ready, 1)
            for s in range(S):
                h_low(0, s)
            for arrived in k.x_in[1:]:
                dve.wait_ge(arrived, 16)
            with dve.Fori(0, n_it - AHEAD) as i:
                turn(i, True)
            for i in range(n_it - AHEAD, n_it):
                turn(i, False, i < n_it - 1)


def stage_gcn_hidden(k, ctx, Y, bn6):
    nc = k.nc
    S = 2
    sb = lambda n, s: ctx.enter_context(nc.sbuf_tensor(n, s, F32))
    h, ZT = each(S, lambda s: sb(f"l1_h{s}", [P, TB, P])), each(S, lambda s: sb(f"l1_z{s}", [P, TW]))
    psZ, psY = k.bank[0:2], (k.bank[2:4], k.bank[4:6])
    h_done, Z_done, ZT_done, Y_done, Y0_stored, Y1_stored, tally = (
        k.sem(f"l1_{n}") for n in ("h", "Z", "ZT", "Y", "Y0s", "Y1s", "tally"))
    tiles = k.B // TB
    there = lambda t: exists(t, tiles)
    n_it = tiles // S
    y_at = lambda c, t: Y[c][:, bass.ds(t * TW, TW)]

    def steps(eng, step):
        for t in range(-S, 2 * S):
            step(t, t % S)
        with eng.Fori(2, n_it - 1) as i:
            for s in range(S):
                step(i * S + s, s)
        for t in range(tiles - S, tiles + 2 * S):
            step(t, t % S)

    with nc.Block() as block:
        @block.scalar
        def _(act):
            def step(t, s):
                if there(t + 1):
                    if since(t + 1, S):
                        act.wait_ge(Z_done, t + 1 - S + 1)
                    normalise_tile(act, k, h[(s + 1) % S], (t + 1) * TB).then_inc(h_done, 1)
                if there(t - 2):
                    act.wait_ge(Y_done, t - 2 + 1)
                    act.activation(y_at(0, t - 2), psY[s][0][:, :], ACT.Identity,
                                   bias=k.cols[:, C_B1:C_B1 + 1]).then_inc(Y0_stored, 1)

            steps(act, step)

        @block.tensor
        def _(pe):
            def step(t, s):
                if there(t - 2):
                    pe.wait_ge(ZT_done, t - 2 + 1)
                    if since(t - 2, S):
                        pe.wait_ge(Y0_stored, t - 2 - S + 1)
                        pe.wait_ge(Y1_stored, t - 2 - S + 1)
                    for c in range(2):
                        last = pe.matmul(psY[s][c][:, :], k.W1T[:, c * P:(c + 1) * P], ZT[s][:, :], start=True, stop=True)
                    last.then_inc(Y_done, 1)
                if there(t):
                    pe.wait_ge(h_done, t + 1)
                    for j in range(TB):
                        last = pe.matmul(psZ[s][:, j * P:(j + 1) * P], h[s][:, j, :], k.AhatT[:, :], start=True, stop=True)
                    last.then_inc(Z_done, 1)

            steps(pe, step)

        @block.vector
        def _(dve):
            def step(t, s):
                if there(t - 2):
                    dve.wait_ge(Y_done, t - 2 + 1)
                    dve.tensor_scalar(y_at(1, t - 2), psY[s][1][:, :], k.cols[:, C_B1 + 1:C_B1 + 2], None,
                                      ALU.add).then_inc(Y1_stored, 1)
                if there(t):
                    dve.wait_ge(Z_done, t + 1)
                    dve.tensor_copy(ZT[s][:, :], psZ[s][:, :]).then_inc(ZT_done, 1)
                if there(t - 3):
                    dve.wait_ge(Y0_stored, t - 3 + 1)
                    dve.wait_ge(Y1_stored, t - 3 + 1)
                    dve.sem_inc(tally, 1)
                    for c in range(2):
                        dve.bn_stats(bn6[:, c, bass.ds(t - 3, 1), :], y_at(c, t - 3))

            steps(dve, step)


def batchnorm_coefficients(k, ctx, name, bn6, halves, c_gamma, c_beta, coef):
    nc = k.nc
    mv = ctx.enter_context(nc.sbuf_tensor(f"{name}_mv", [P, halves, 2], F32))
    sem = lambda n: k.sem(f"{name}_{n}")
    aggregated, shifted, powed, scaled, ready = (sem(n) for n in ("aggr", "shift", "pow", "scale", "bn_ready"))

    def on_vector(dve):
        for c in range(halves):
            last = dve.bn_aggr(mv[:, c, :], bn6[:, c, :, :])
        last.then_inc(aggregated, 1)
        dve.wait_ge(aggregated, 1)
        dve.tensor_scalar(mv[:, :, 1], mv[:, :, 1], EPS, None, ALU.add).then_inc(shifted, 1)
        dve.wait_ge(powed, 1)
        dve.tensor_tensor(coef[:, :, 0], k.cols[:, c_gamma:c_gamma + halves], mv[:, :, 1], ALU.mult).then_inc(scaled, 1)
        dve.wait_ge(scaled, 1)
        dve.tensor_tensor(mv[:, :, 0], mv[:, :, 0], coef[:, :, 0], ALU.mult).then_inc(scaled, 1)
        dve.wait_ge(scaled, 2)
        dve.tensor_tensor(coef[:, :, 1], k.cols[:, c_beta:c_beta + halves], mv[:, :, 0], ALU.subtract).then_inc(ready, 1)

    def on_pool(pool):
        pool.wait_ge(shifted, 1)
        pool.tensor_tensor(out=mv[:, :, 1], in0=mv[:, :, 1], in1=k.ln_const["-half"][:, 0:halves], op=ALU.pow).then_inc(powed, 1)

    return on_vector, on_pool, ready


def stage_gcn_out(k, ctx, Y, bn6, bno6):
    nc = k.nc
    S = 2
    sem = lambda n: k.sem(n)
    sb = lambda n, s: ctx.enter_context(nc.sbuf_tensor(n, s, F32))
    h2 = each(S, lambda s: sb(f"l1b_h{s}", [P, 2, TW]))
    coef = sb("l1b_coef", [P, 2, 2])
    psO = k.bank[0:2]
    h2_ready, O_ready, O_stored = (each(S, lambda s: sem(f"l1b_{n}{s}")) for n in ("h", "O", "Os"))
    coef_dve, coef_pool, coef_ready = batchnorm_coefficients(k, ctx, "bn1", bn6, 2, C_G1, C_BE1, coef)
    tally = sem("l1b_tally")
    n_it = k.B // TB // S

    with nc.Block() as block:
        @block.gpsimd
        def _(pool):
            coef_pool(pool)

        @block.scalar
        def _(act):
            act.wait_ge(coef_ready, 1)
            with act.Fori(0, n_it) as i:
                for s in range(S):
                    act.wait_ge(O_ready[s], i + 1)
                    for c in range(2):
                        last = act.activation(h2[s][:, c, :], Y[c][:, bass.ds((i * S + s) * TW, TW)], ACT.Relu,
                                              bias=coef[:, c, 1:2], scale=coef[:, c, 0:1])
                    last.then_inc(h2_ready[s], 1)

        @block.tensor
        def _(pe):
            for s in range(S):
                pe.sem_inc(O_ready[s], 1)
            with pe.Fori(0, n_it) as i:
                for s in range(S):
                    pe.wait_ge(h2_ready[s], i + 1)
                    pe.wait_ge(O_stored[s], i + 1)
                    pe.matmul(psO[s][:, :], k.W2T[:, 0, :], h2[s][:, 0, :], start=True, stop=False)
                    pe.matmul(psO[s][:, :], k.W2T[:, 1, :], h2[s][:, 1, :], start=False, stop=True).then_inc(O_ready[s], 1)

        @block.vector
        def _(dve):
            coef_dve(dve)
            for s in range(S):
                dve.sem_inc(O_stored[s], 1)
            with dve.Fori(0, n_it) as i:
                for s in range(S):
                    t = i * S + s
                    o = Y[0][:, bass.ds(t * TW, TW)]
                    dve.wait_ge(O_ready[s], i + 2)
                    dve.tensor_scalar(o, psO[s][:, :], k.cols[:, C_B2:C_B2 + 1], None, ALU.add).then_inc(O_stored[s], 1)
                    dve.wait_ge(O_stored[s], i + 2)
                    dve.sem_inc(tally, 1)
                    dve.bn_stats(bno6[:, 0, bass.ds(t, 1), :], o)


class Residual:

    def __init__(self, k, ctx, name, S, source, affine, banks):
        self.k, self.S, self.source, self.affine, self.banks = k, S, source, affine, banks
        self.o = each(S, lambda s: ctx.enter_context(k.nc.sbuf_tensor(f"{name}_o{s}", [P, TW], F32)))
        self.o_ready, self.R_ready, self.updated = (each(S, lambda s: k.sem(f"{name}_{n}{s}")) for n in ("o", "R", "upd"))
        self.ln = LayerNormTail(k, ctx, name, S)

    def fetch(self, act, i, s):
        act.activation(self.o[s][:, :], self.source(i * self.S + s), ACT.Identity, **self.affine).then_inc(self.o_ready[s], 1)

    def turn_over(self, pe, i, s):
        pe.wait_ge(self.o_ready[s], i + 1)
        for j in range(TB):
            last = pe.transpose(self.banks[s][:, j * P:(j + 1) * P], self.o[s][:, j * P:(j + 1) * P], self.k.ident[:, :])
        last.then_inc(self.R_ready[s], 1)

    def update(self, dve, i, slots):
        xt = each(self.S, lambda s: self.k.X[:, bass.ds((i * self.S + s) * TB, TB), :])
        for s in slots:
            dve.wait_ge(self.R_ready[s], i + 1)
            dve.tensor_tensor(xt[s], self.banks[s][:, :].rearrange("p (b n) -> p b n", b=TB), xt[s],
                              ALU.add).then_inc(self.updated[s], 1)
        for s in slots:
            dve.wait_ge(self.updated[s], i + 1)
            self.ln.stats(dve, xt[s], s, i)

    def coefficients(self, pool, i):
        self.ln.coefficients(pool, i)


def stage_conv(k, ctx, O, bno6, HT, d):
    nc = k.nc
    S = 2
    RES, FETCH = 4, 5
    sem = lambda n: k.sem(n)
    sb = lambda n: ctx.enter_context(nc.sbuf_tensor(n, [P, TB, P], F32))
    h = each(S, lambda s: sb(f"l2_h{s}"))
    Z, Gb, G, V2 = (sb(f"l2_{n}") for n in ("Z", "Gb", "G", "V2"))
    shift = ctx.enter_context(nc.sbuf_tensor("l2_shift", [P, P], F32))
    h_done, Zp_done, Z_done, Gp_done, Gb_done, G_done, V2p_done, V2_done, Hp_done, H_done, sums_done = (
        sem(f"l2_{n}") for n in ("h", "Zp", "Z", "Gp", "Gb", "G", "V2p", "V2", "Hp", "H", "sums"))
    w_raw = each(2, lambda n: ctx.enter_context(nc.sbuf_tensor(f"w_raw{n}", [P, 4, 4 * P], F32)))
    w_in, w_copied, w_tally = each(2, lambda n: sem(f"lstm_w_in{n}")), sem("w_copied"), sem("w_tally")
    tiles = k.B // TB
    there = lambda t: exists(t, tiles)
    n_it = tiles // S
    psR = k.bank[0:2]
    psZ, psG, psV2, psH, psS = k.bank[2:7]
    as_tile = lambda ps: ps[:, :].rearrange("p (b n) -> p b n", b=TB)
    coef = ctx.enter_context(nc.sbuf_tensor("l1c_coef", [P, 1, 2], F32))
    bn_dve, bn_pool, bn_ready = batchnorm_coefficients(k, ctx, "bn2", bno6, 1, C_G2, C_BE2, coef)
    res = Residual(k, ctx, "l1r", S, lambda t: O[:, bass.ds(t * TW, TW)],
                   dict(bias=coef[:, 0, 1:2], scale=coef[:, 0, 0:1]), psR)

    def steps(eng, step):
        for i in range(-3, 2):
            for s in range(S):
                step(i, s)
        with eng.Fori(2, n_it - 3) as i:
            for s in range(S):
                step(i, s)
        for i in range(n_it - 3, n_it + 2):
            for s in range(S):
                step(i, s)

    with nc.Block() as block:
        @block.gpsimd
        def _(pool):
            res.ln.open(pool)
            bn_pool(pool)
            zeros = k.zero[:, 0:1].unsqueeze(2).broadcast_to([P, 1, 4 * P])
            for n, W in enumerate((k.Wih, k.Whh)):
                pool.wait_ge(w_in[n], 16)
                with pool.Fori(4 * n, 4 * n + 4) as i:
                    res.coefficients(pool, i)
                    at = bass.ds(i - 4 * n, 1)
                    split_float32(pool, w_raw[n][:, at, :], W[0][:, at, :], W[1][:, at, :], w_copied, i + 1, w_tally, zeros)
            with pool.Fori(8, n_it) as i:
                res.coefficients(pool, i)

        @block.sync
        def _(sp):
            sp.dma_start(w_raw[0][:, :, :], d["WihT"].rearrange("p d g -> d p g")).then_inc(w_in[0], 16)
            sp.dma_start(w_raw[1][:, :, :], d["WhhT"].rearrange("p d g -> d p g")).then_inc(w_in[1], 16)

        @block.scalar
        def _(act):
            def step(i, s):
                t = i * S + s
                if there(t + FETCH):
                    q, turn = (s + FETCH) % S, i + (s + FETCH) // S
                    if since(t + FETCH, S):
                        act.wait_ge(res.R_ready[q], turn)
                    res.fetch(act, turn, q)
                if there(t - 3):
                    act.wait_ge(Hp_done, t - 3 + 1)
                    act.activation(HT[:, bass.ds((t - 3) * TW, TW)], psH[:, :], ACT.Relu).then_inc(H_done, 1)
                if there(t + 1):
                    q, turn = (s + 1) % S, i + (s + 1) // S
                    if since(t + 1, S):
                        act.wait_ge(Zp_done, t + 1 - S + 1)
                    res.ln.wait(act, q, turn)
                    normalise_tile(act, k, h[q], (t + 1) * TB).then_inc(h_done, 1)
                if there(t - 1):
                    act.wait_ge(Gb_done, t - 1 + 1)
                    act.activation(G[:, :, :], Gb[:, :, :], ACT.Relu).then_inc(G_done, 1)

            act.wait_ge(bn_ready, 1)
            steps(act, step)

        @block.tensor
        def _(pe):
            def product(ps, lhs, rhs, done):
                for j in range(TB):
                    last = pe.matmul(ps[:, j * P:(j + 1) * P], lhs[:, j, :], rhs, start=True, stop=True)
                last.then_inc(done, 1)

            def step(i, s):
                t = i * S + s
                if there(t + RES):
                    turn = i + RES // S
                    if since(t + RES, S):
                        pe.wait_ge(res.updated[s], turn)
                    res.turn_over(pe, turn, s)
                if there(t - 3):
                    pe.wait_ge(V2_done, t - 3 + 1)
                    if since(t - 3, 1):
                        pe.wait_ge(H_done, t - 4 + 1)
                    product(psH, V2, k.adjT[:, :], Hp_done)
                if there(t - 2):
                    pe.wait_ge(G_done, t - 2 + 1)
                    product(psV2, G, k.Wg[:, 1, :], V2p_done)
                if there(t - 1):
                    pe.wait_ge(Z_done, t - 1 + 1)
                    pe.matmul(psG[:, :], k.Wg[:, 0, :], Z[:, :, :], start=True, stop=True).then_inc(Gp_done, 1)
                if there(t):
                    pe.wait_ge(h_done, t + 1)
                    product(psZ, h[s], k.adjT[:, :], Zp_done)

            pe.matmul(psS[:, 0:P], k.ones[:, :], k.adjT[:, :], start=True, stop=True).then_inc(sums_done, 1)
            steps(pe, step)

        @block.vector
        def _(dve):
            def step(i, s):
                t = i * S + s
                if there(t + RES):
                    res.update(dve, i + RES // S, [s])
                if there(t - 2):
                    dve.wait_ge(V2p_done, t - 2 + 1)
                    dve.tensor_tensor(V2[:, :, :], as_tile(psV2), k.rows[:, R_G1:R_G1 + 1, :].broadcast_to([P, TB, P]),
                                      ALU.add).then_inc(V2_done, 1)
                if there(t - 1):
                    dve.wait_ge(Gp_done, t - 1 + 1)
                    if since(t - 1, 1):
                        dve.wait_ge(G_done, t - 2 + 1)
                    dve.tensor_tensor(Gb[:, :, :], as_tile(psG), shift[:, :].unsqueeze(1).broadcast_to([P, TB, P]),
                                      ALU.add).then_inc(Gb_done, 1)
                if there(t):
                    dve.wait_ge(Zp_done, t + 1)
                    dve.tensor_copy(Z[:, :, :], as_tile(psZ)).then_inc(Z_done, 1)

            bn_dve(dve)
            dve.tensor_tensor(k.lstm_bias[:, :, :].rearrange("h p g -> h (p g)"), k.cols[:, C_BIH:C_BIH + 16],
                              k.cols[:, C_BHH:C_BHH + 16], ALU.add)
            dve.wait_ge(sums_done, 1)
            dve.tensor_scalar(shift[:, :], psS[:, 0:P], k.cols[:, C_BG0:C_BG0 + 1], None, ALU.mult).then_inc(sums_done, 1)
            dve.wait_ge(sums_done, 2)
            steps(dve, step)


GATE_I, GATE_F, GATE_G, GATE_O = range(4)
LSTM_SLOTS = 2
MAX_WINDOW = 4


def split_float32(eng, full, hi, lo, copied, copied_count, tally=None, zeros=None):
    if zeros is not None:
        eng.tensor_tensor(out=hi, in0=full, in1=zeros, op=ALU.add).then_inc(copied, 1)
    else:
        eng.tensor_copy(hi, full).then_inc(copied, 1)
    eng.wait_ge(copied, copied_count)
    if tally is not None:
        eng.sem_inc(tally, 1)
    return eng.tensor_tensor(out=lo, in0=full, in1=hi.bitcast(F32), op=ALU.subtract)


class Windows:

    def __init__(self, k, HT, p, before):
        self.p, self.nw = p, P // p
        self.nb = max(n for n in (4, 8, 16) if n * self.nw <= TW)
        self.N = self.nb * self.nw
        self.turns = k.B // self.nb // LSTM_SLOTS
        self.HT = HT[:, :].rearrange("h (b t) -> h b t", t=P)
        self.before = before
        zero = before is None
        steps = 0 if zero else before.turns * before.p
        handed_on = 0 if zero else before.turns * (before.p - 1)
        self.steps0 = 0 if zero else before.steps0 + steps
        self.handed_on0 = 0 if zero else before.handed_on0 + handed_on
        self.x0 = [0, 0] if zero else [before.x0[b] + before.turns * len(range(b, before.p, 2)) for b in range(2)]
        self.written0 = 0 if zero else before.written0 + before.turns * LSTM_SLOTS
        self.bias = k.lstm_bias[:, p - 1, :]

    def node(self, i, s, step):
        rows = bass.ds((i * LSTM_SLOTS + s) * self.nb, self.nb)
        if self.p == 1:
            return self.HT[:, rows, :]
        return self.HT[:, rows, 0:self.nw * self.p].rearrange("h b (w q) -> h b w q", q=self.p)[:, :, :, step]

    def as3(self, ap):
        return ap.rearrange("h (b w) -> h b w", w=self.nw)

    def n_seq(self, i, step):
        return self.steps0 + i * self.p + step + 1

    def n_rec(self, i, step):
        return self.handed_on0 + i * (self.p - 1) + step

    def n_x(self, i, step):
        return self.x0[step % 2] + i * len(range(step % 2, self.p, 2)) + step // 2 + 1

    def n_gate(self, g, i, step):
        return self.n_rec(i, step) if g == GATE_F else self.n_seq(i, step)

    def n_source(self, i, s):
        return self.before.written0 + (i * LSTM_SLOTS + s + 1) * (self.nb // self.before.nb)

    def gates_of(self, step):
        return [g for g in (GATE_G, GATE_I, GATE_F, GATE_O) if step or g != GATE_F]


def stage_lstm(k, ctx, HT):
    nc = k.nc
    S = LSTM_SLOTS
    sb = lambda n, t=F32: each(S, lambda s: ctx.enter_context(nc.sbuf_tensor(f"lstm_{n}{s}", [P, TW], t)))
    gates = each(S, lambda s: ctx.enter_context(nc.sbuf_tensor(f"gates{s}", [P, 4, TW], F32)))
    cell = sb("cell")
    hid_hi, hid_lo = (sb(n, F32R) for n in ("hid_hi", "hid_lo"))
    x_hi, x_lo = (each(2, lambda b: sb(f"{n}{b}", F32R)) for n in ("x_hi", "x_lo"))
    done, act_out = (each(S, lambda s: each(4, lambda g: k.sem(f"lstm_{n}{s}{g}"))) for n in ("done", "act"))
    cell_ready, tanh_ready, h_ready, hh_ready, hl_ready, fc_ready, ig_ready, x_tally = (
        each(S, lambda s: k.sem(f"lstm_{n}{s}"))
        for n in ("cell", "tanh", "h", "hh", "hl", "fc", "ig", "x_tally"))
    xh_ready, xl_ready, x_free = (each(2, lambda b: each(S, lambda s: k.sem(f"lstm_{n}{b}{s}"))) for n in ("xh", "xl", "x_free"))
    written = k.sem("lstm_written")
    lengths = [Windows(k, HT, 1, None)]
    for p in range(2, MAX_WINDOW + 1):
        lengths.append(Windows(k, HT, p, lengths[-1]))

    with nc.Block() as block:
        @block.gpsimd
        def _(pool):
            first = lengths[0]
            with pool.Fori(0, first.turns) as i:
                for s in range(S):
                    pool.wait_ge(xh_ready[0][s], first.n_x(i, 0))
                    pool.sem_inc(x_tally[s], 1)
                    pool.tensor_tensor(out=first.as3(x_lo[0][s][:, 0:first.N]), in0=first.node(i, s, 0),
                                       in1=first.as3(x_hi[0][s][:, 0:first.N]).bitcast(F32), op=ALU.subtract).then_inc(xl_ready[0][s], 1)
            for w in lengths[1:]:
                zeros = k.zero[:, 0:1].unsqueeze(2).broadcast_to([P, w.nb, w.nw])
                with pool.Fori(0, w.turns) as i:
                    for step in range(w.p):
                        for s in range(S):
                            if step == 0:
                                pool.wait_ge(written, w.n_source(i, s))
                            b = step % 2
                            pool.wait_ge(x_free[b][s], w.n_x(i, step))
                            split_float32(pool, w.node(i, s, step), w.as3(x_hi[b][s][:, 0:w.N]), w.as3(x_lo[b][s][:, 0:w.N]),
                                          xh_ready[b][s], w.n_x(i, step), x_tally[s], zeros=zeros).then_inc(xl_ready[b][s], 1)

        @block.tensor
        def _(pe):
            for s in range(S):
                for b in range(2):
                    pe.sem_inc(x_free[b][s], 1)

            def product(w, out, W, g, v_hi, v_lo, start, stop):
                hi, lo = (W[n][:, w.p - 1, g * P:(g + 1) * P] for n in range(2))
                pe.matmul(out, hi, v_hi[:, 0:w.N], start=start, stop=False)
                pe.matmul(out, lo, v_hi[:, 0:w.N], start=False, stop=False)
                return pe.matmul(out, hi, v_lo[:, 0:w.N], start=False, stop=stop)

            for w in lengths:
                with pe.Fori(0, w.turns) as i:
                    for step in range(w.p):
                        for s in range(S):
                            b = step % 2
                            pe.wait_ge(xl_ready[b][s], w.n_x(i, step))
                            for g in w.gates_of(step):
                                pe.wait_ge(act_out[s][g], w.n_gate(g, i, step))
                                last = product(w, k.bank[4 * s + g][:, 0:w.N], k.Wih, g, x_hi[b][s], x_lo[b][s], True, step == 0)
                                if step == 0:
                                    last.then_inc(done[s][g], 1)
                            if step:
                                last.then_inc(x_free[b][s], 1)
                                pe.wait_ge(hl_ready[s], w.n_rec(i, step))
                                for g in w.gates_of(step):
                                    product(w, k.bank[4 * s + g][:, 0:w.N], k.Whh, g, hid_hi[s], hid_lo[s],
                                            False, True).then_inc(done[s][g], 1)

        @block.scalar
        def _(act):
            for s in range(S):
                for g in range(4):
                    act.sem_inc(act_out[s][g], 1)

            def gate(w, i, step, s, g):
                act.wait_ge(done[s][g], w.n_gate(g, i, step))
                if step == 0 and g == GATE_O:
                    act.sem_inc(x_free[0][s], 1)
                act.activation(gates[s][:, g, 0:w.N], k.bank[4 * s + g][:, 0:w.N],
                               ACT.Tanh if g == GATE_G else ACT.Sigmoid,
                               bias=w.bias[:, g:g + 1]).then_inc(act_out[s][g], 1)

            first = lengths[0]

            def tanh_in_place(i, s):
                act.wait_ge(cell_ready[s], first.n_seq(i, 0))
                c = cell[s][:, 0:first.N]
                act.activation(c, c, ACT.Tanh).then_inc(tanh_ready[s], 1)

            def half_turn(i, s, previous):
                gate(first, i, 0, s, GATE_G)
                gate(first, i, 0, s, GATE_I)
                if previous:
                    tanh_in_place(*previous)
                if since(i, 1):
                    act.wait_ge(written, S * (i - 1) + s + 1)
                gate(first, i, 0, s, GATE_O)

            half_turn(0, 0, None)
            half_turn(0, 1, (0, 0))
            with act.Fori(1, first.turns) as i:
                half_turn(i, 0, (i - 1, 1))
                half_turn(i, 1, (i, 0))
            tanh_in_place(first.turns - 1, 1)
            act.wait_ge(written, S * first.turns)

            for w in lengths[1:]:
                with act.Fori(0, w.turns) as i:
                    for step in range(w.p):
                        for s in range(S):
                            for g in w.gates_of(step):
                                gate(w, i, step, s, g)
                            act.wait_ge(cell_ready[s], w.n_seq(i, step))
                            act.activation(gates[s][:, GATE_G, 0:w.N], cell[s][:, 0:w.N], ACT.Tanh).then_inc(tanh_ready[s], 1)

        @block.vector
        def _(dve):
            def gate(w, s, g):
                return gates[s][:, g, 0:w.N]

            def new_cell(w, i, step, s):
                c = cell[s][:, 0:w.N]
                dve.wait_ge(act_out[s][GATE_G], w.n_gate(GATE_G, i, step) + 1)
                dve.wait_ge(act_out[s][GATE_I], w.n_gate(GATE_I, i, step) + 1)
                if step == 0:
                    dve.tensor_tensor(c, gate(w, s, GATE_I), gate(w, s, GATE_G), ALU.mult).then_inc(cell_ready[s], 1)
                    return
                dve.tensor_tensor(gate(w, s, GATE_I), gate(w, s, GATE_I), gate(w, s, GATE_G), ALU.mult).then_inc(ig_ready[s], 1)
                dve.wait_ge(act_out[s][GATE_F], w.n_gate(GATE_F, i, step) + 1)
                dve.tensor_tensor(c, gate(w, s, GATE_F), c, ALU.mult).then_inc(fc_ready[s], 1)
                dve.wait_ge(ig_ready[s], w.n_rec(i, step))
                dve.wait_ge(fc_ready[s], w.n_rec(i, step))
                dve.tensor_tensor(c, gate(w, s, GATE_I), c, ALU.add).then_inc(cell_ready[s], 1)

            def new_hidden(w, i, step, s):
                dve.wait_ge(act_out[s][GATE_O], w.n_gate(GATE_O, i, step) + 1)
                dve.wait_ge(tanh_ready[s], w.n_seq(i, step))
                if step == w.p - 1:
                    dve.tensor_tensor(w.node(i, s, step), w.as3(gate(w, s, GATE_O)), w.as3(gate(w, s, GATE_G)),
                                      ALU.mult).then_inc(written, 1)
                    return
                hd = gate(w, s, GATE_I)
                dve.tensor_tensor(hd, gate(w, s, GATE_O), gate(w, s, GATE_G), ALU.mult).then_inc(h_ready[s], 1)
                dve.wait_ge(h_ready[s], w.n_rec(i, step + 1))
                split_float32(dve, hd, hid_hi[s][:, 0:w.N], hid_lo[s][:, 0:w.N], hh_ready[s],
                              w.n_rec(i, step + 1)).then_inc(hl_ready[s], 1)

            first = lengths[0]

            def x_high(i, s):
                dve.wait_ge(x_free[0][s], first.n_x(i, 0))
                dve.tensor_scalar(first.as3(x_hi[0][s][:, 0:first.N]), first.node(i, s, 0), 0.0, None, ALU.add).then_inc(xh_ready[0][s], 1)

            def write_tile(i, s):
                dve.wait_ge(act_out[s][GATE_O], first.n_gate(GATE_O, i, 0) + 1)
                dve.wait_ge(tanh_ready[s], first.n_seq(i, 0))
                dve.tensor_tensor(first.node(i, s, 0), first.as3(gate(first, s, GATE_O)), first.as3(cell[s][:, 0:first.N]),
                                  ALU.mult).then_inc(written, 1)

            def half_turn(i, s, ahead, previous):
                if since(i, 1):
                    dve.wait_ge(written, S * (i - 1) + s + 1)
                new_cell(first, i, 0, s)
                if ahead:
                    x_high(i + 1, s)
                if previous:
                    write_tile(*previous)

            for s in range(S):
                x_high(0, s)
            half_turn(0, 0, True, None)
            half_turn(0, 1, True, (0, 0))
            with dve.Fori(1, first.turns - 1) as i:
                half_turn(i, 0, True, (i - 1, 1))
                half_turn(i, 1, True, (i, 0))
            i = first.turns - 1
            half_turn(i, 0, False, (i - 1, 1))
            half_turn(i, 1, False, (i, 0))
            write_tile(i, 1)
            dve.wait_ge(written, S * first.turns)
            for w in lengths[1:]:
                with dve.Fori(0, w.turns) as i:
                    for step in range(w.p):
                        for s in range(S):
                            new_cell(w, i, step, s)
                            new_hidden(w, i, step, s)


def stage_edges(k, ctx, e):
    nc = k.nc
    E, EC = k.E, k.E // P
    sem = lambda n: k.sem(n)
    sb = lambda n, s, t=F32: ctx.enter_context(nc.sbuf_tensor(n, s, t))
    iotas, step, pe_done, lned, evac = (sem(n) for n in (
        "iotas", "edge_step", "edge_pe", "edge_ln", "edge_evac"))
    row, col = sb("edge_row", [P, 2, E]), sb("edge_col", [P, 2, EC])
    order_row, order_col = sb("order_row", [P, E]), sb("order_col", [P, EC])
    key_row, key_col = sb("key_row", [P, E]), sb("key_col", [P, EC])
    iota_part, rank = sb("iota_part", [P, 1]), sb("rank", [P, EC])
    less, perm, colbc = sb("less", [P, E]), sb("perm", [P, EC, E]), sb("colbc", [P, 2, EC, P])
    sorted_row = sb("sorted_row", [P, 2, E])
    weight = sb("edge_weight", [P, E])
    ST, DT = sb("ST", [P, E]), sb("DT", [P, E])
    psS, psD, psU, psW, psT = k.bank[0:5]

    with nc.Block() as block:
        @block.gpsimd
        def _(pool):
            pool.iota(order_row[:, :], [[1, E]], base=0, channel_multiplier=0, allow_small_or_imprecise_dtypes=True).then_inc(iotas, 1)
            pool.iota(order_col[:, :], [[P, EC]], base=0, channel_multiplier=1, allow_small_or_imprecise_dtypes=True).then_inc(iotas, 1)
            pool.iota(iota_part[:, :], [[0, 1]], base=0, channel_multiplier=1, allow_small_or_imprecise_dtypes=True).then_inc(iotas, 1)
            k.x_ln.open(pool)
            for i in range(k.X_AHEAD):
                k.x_ln.coefficients(pool, i)

        @block.vector
        def _(dve):
            n = 0

            def chained(ins):
                nonlocal n
                n += 1
                ins.then_inc(step, 1)
                dve.wait_ge(step, n)

            dve.wait_ge(e.loaded, 4 * 16)
            dve.wait_ge(e.w_in, 3 * 16)
            chained(dve.scalar_tensor_tensor(e.Wqv[:, 0:P], e.Wqv[:, 0:P], 0.8, e.a_sign[:, :], ALU.mult, ALU.mult))
            chained(dve.tensor_scalar(e.a_sign[:, :], e.a_sign[:, :], 0.0, 2.0, ALU.is_ge, ALU.mult))
            chained(dve.tensor_scalar(e.a_sign[:, :], e.a_sign[:, :], -1.0, None, ALU.add))
            chained(dve.tensor_tensor(e.Wqv[:, 0:P], e.Wqv[:, 0:P], e.a_sign[:, :], ALU.mult))
            dve.wait_ge(iotas, 3)
            dve.tensor_copy(row[:, :, :], e.row_i[:, :, :])
            chained(dve.tensor_copy(col[:, :, :], e.col_i[:, :, :]))
            dve.scalar_tensor_tensor(key_row[:, :], row[:, 0, :], float(E), order_row[:, :], ALU.mult, ALU.add)
            dve.tensor_copy(colbc[:, :, :, :], col[:, :, :].unsqueeze(3).broadcast_to([P, 2, EC, P]))
            chained(dve.scalar_tensor_tensor(key_col[:, :], col[:, 0, :], float(E), order_col[:, :], ALU.mult, ALU.add))
            for c in range(EC):
                chained(dve.tensor_scalar(less[:, :], key_row[:, :], key_col[:, c:c + 1], 0.0, ALU.is_lt, ALU.add,
                                          accum_out=rank[:, c:c + 1]))
            for c in range(EC):
                dve.tensor_scalar(perm[:, c, :], order_row[:, :], rank[:, c:c + 1], None, ALU.is_equal).then_inc(evac, 1)
            dve.wait_ge(k.x_in[0], 16)
            for i in range(k.X_AHEAD):
                k.x_stats(dve, i)
            dve.wait_ge(pe_done, 2)
            dve.tensor_copy(sorted_row[:, 0, :], psS[:, 0:E])
            chained(dve.tensor_copy(sorted_row[:, 1, :], psD[:, 0:E]))
            dve.tensor_scalar(ST[:, :], sorted_row[:, 0, :], iota_part[:, :], None, ALU.is_equal)
            chained(dve.tensor_scalar(DT[:, :], sorted_row[:, 1, :], iota_part[:, :], None, ALU.is_equal))
            dve.tensor_copy(e.DTr[:, :], DT[:, :])
            dve.tensor_tensor(e.PT[:, :], ST[:, :], DT[:, :], ALU.add).then_inc(evac, 1)
            chained(dve.memset(e.cont[:, :], 0.0))
            chained(dve.tensor_tensor(e.cont[:, 1:E], sorted_row[:, 0, 1:E], sorted_row[:, 0, 0:E - 1], ALU.is_equal))
            dve.tensor_scalar(e.reset[:, :], e.cont[:, :], -1.0, BIG, ALU.add, ALU.mult)
            chained(dve.tensor_scalar(e.is_last[:, :], e.cont[:, 1:E + 1], -1.0, 1.0, ALU.mult, ALU.add))
            dve.wait_ge(pe_done, 3)
            dve.tensor_tensor(weight[:, :], psU[:, 0:E], ST[:, :], ALU.mult).then_inc(evac, 1)
            dve.wait_ge(pe_done, 5)
            dve.tensor_copy(e.S1[:, :, :], psT[:, 0:EC * P].rearrange("p (c n) -> p c n", c=EC))
            dve.wait_ge(pe_done, 4)
            chained(dve.tensor_scalar(weight[:, :], psW[:, 0:E], EPS_EDGE, None, ALU.add))
            dve.sem_inc(evac, 1)

        @block.tensor
        def _(pe):
            pe.wait_ge(evac, EC)
            for n, ps in enumerate((psS, psD)):
                for c in range(EC):
                    last = pe.matmul(ps[:, 0:E], colbc[:, n, c, :], perm[:, c, :], start=c == 0, stop=c == EC - 1)
                last.then_inc(pe_done, 1)
            pe.wait_ge(evac, EC + 1)
            pe.matmul(psU[:, 0:E], k.adjT[:, :], DT[:, :], start=True, stop=True).then_inc(pe_done, 1)
            pe.wait_ge(evac, EC + 2)
            pe.matmul(psW[:, 0:E], k.ones[:, :], weight[:, :], start=True, stop=True).then_inc(pe_done, 1)
            for c in range(EC):
                last = pe.transpose(psT[:, c * P:(c + 1) * P], ST[:, c * P:(c + 1) * P], k.ident[:, :])
            last.then_inc(pe_done, 1)

        @block.scalar
        def _(act):
            act.wait_ge(evac, EC + 3)
            act.activation(e.log_w[:, :], weight[:, :], ACT.Ln).then_inc(lned, 1)
            act.wait_ge(lned, 1)
            act.activation(weight[:, 0:1], weight[:, 0:1], ACT.Sigmoid)


def stage_scores(k, ctx, HT, Xv, scores, e):
    nc = k.nc
    S = 2
    EC, HEADS = k.E // P, k.HEADS
    HW = TB * HEADS
    sem = lambda n: k.sem(n)
    sb = lambda n, s: ctx.enter_context(nc.sbuf_tensor(n, s, F32))
    h, hT, Xq, Qs = (each(S, lambda s: sb(f"l3_{n}{s}", [P, TB, P])) for n in ("h", "hT", "Xq", "Qs"))
    M = each(S, lambda s: sb(f"l3_M{s}", [P, EC, TW]))
    names = ("h", "Tp", "hT", "Q", "V", "Xq", "Xv", "Qs", "lin", "G", "M", "kept")
    R = {n: each(S, lambda s: sem(f"l3_{n}{s}")) for n in names}
    tally = sem("l3_tally")
    n_it = k.B // TB // S
    psT, psQ, psV, psR = k.bank[0:2], k.bank[2:4], k.bank[4:6], k.bank[6:8]
    as_tile = lambda ps: ps[:, :].rearrange("p (b n) -> p b n", b=TB)
    AHEAD = 2
    res = Residual(k, ctx, "l2r", S, lambda t: HT[:, bass.ds(t * TW, TW)], {}, psR)

    def turns(eng, turn):
        with eng.Fori(0, n_it - AHEAD - 1) as i:
            turn(i, True, True, True)
        turn(n_it - AHEAD - 1, False, True, True)
        for i in range(n_it - AHEAD, n_it):
            turn(i, False, False, i < n_it - 1)

    with nc.Block() as block:
        @block.gpsimd
        def _(pool):
            def turn(i, fetching, residual, following):
                for s in range(S):
                    pool.wait_ge(R["lin"][s], i + 1)
                    pool.wait_ge(R["Xq"][s], i + 1)
                    pool.tensor_tensor(out=Qs[s][:, :, :], in0=Xq[s][:, :, :],
                                       in1=e.a_sign[:, :].unsqueeze(1).broadcast_to([P, TB, P]),
                                       op=ALU.mult).then_inc(R["Qs"][s], 1)
                if residual:
                    res.coefficients(pool, i + AHEAD)

            res.ln.open(pool)
            for s in range(S):
                pool.sem_inc(R["Qs"][s], 1)
            for i in range(AHEAD):
                res.coefficients(pool, i)
            turns(pool, turn)

        @block.scalar
        def _(act):
            def normalise(i, s):
                res.ln.wait(act, s, i)
                normalise_tile(act, k, h[s], (i * S + s) * TB).then_inc(R["h"][s], 1)

            def turn(i, fetching, residual, following):
                for s in range(S):
                    act.wait_ge(R["Tp"][s], i + 1)
                    act.activation(hT[s][:, :, :], as_tile(psT[s]), ACT.Copy).then_inc(R["hT"][s], 1)
                if fetching:
                    for s in range(S):
                        act.wait_ge(res.R_ready[s], i + AHEAD + 1)
                        res.fetch(act, i + AHEAD + 1, s)
                for s in range(S):
                    act.wait_ge(R["Qs"][s], i + 1)
                    act.wait_ge(R["Q"][s], i + 1)
                    act.activation(Xq[s][:, :, :], as_tile(psQ[s]), ACT.Copy).then_inc(R["Xq"][s], 1)
                    act.wait_ge(R["V"][s], i + 1)
                    act.activation(Xv[:, bass.ds((i * S + s) * TB, TB), :], as_tile(psV[s]), ACT.Copy).then_inc(R["Xv"][s], 1)
                    if following:
                        normalise(i + 1, s)

            for i in range(AHEAD + 1):
                for s in range(S):
                    if i:
                        act.wait_ge(res.R_ready[s], i)
                    res.fetch(act, i, s)
            for s in range(S):
                normalise(0, s)
            turns(act, turn)

        @block.tensor
        def _(pe):
            def turn(i, fetching, residual, following):
                for s in range(S):
                    pe.wait_ge(R["h"][s], i + 1)
                    for j in range(TB):
                        last = pe.transpose(psT[s][:, j * P:(j + 1) * P], h[s][:, j, :], k.ident[:, :])
                    last.then_inc(R["Tp"][s], 1)
                    if residual:
                        pe.wait_ge(res.updated[s], i + AHEAD)
                        res.turn_over(pe, i + AHEAD, s)
                for s in range(S):
                    pe.wait_ge(R["hT"][s], i + 1)
                    pe.wait_ge(R["M"][s], i + 1)
                    for n, (ps, done) in enumerate(((psQ[s], R["Q"][s]), (psV[s], R["V"][s]))):
                        for j in range(TB):
                            last = pe.matmul(ps[:, j * P:(j + 1) * P], hT[s][:, j, :], e.Wqv[:, n * P:(n + 1) * P],
                                             start=True, stop=True)
                        last.then_inc(done, 1)
                for s in range(S):
                    for c, (ps, free) in enumerate(((psQ[s], R["Xq"][s]), (psV[s], R["Xv"][s]))):
                        pe.wait_ge(free, i + 1)
                        pe.matmul(ps[:, :], e.PT[:, c * P:(c + 1) * P], Xq[s][:, :, :], start=True, stop=True).then_inc(R["G"][s], 1)

            for s in range(S):
                pe.sem_inc(R["M"][s], 1)
            for i in range(AHEAD):
                for s in range(S):
                    if i:
                        pe.wait_ge(res.updated[s], i)
                    res.turn_over(pe, i, s)
            turns(pe, turn)

        @block.vector
        def _(dve):
            def turn(i, fetching, residual, following):
                if residual:
                    res.update(dve, i + AHEAD, range(S))
                for s in range(S):
                    dve.wait_ge(R["kept"][s], i + 1)
                    for c, ps in enumerate((psQ[s], psV[s])):
                        dve.wait_ge(R["G"][s], EC * i + c + 1)
                        last = dve.scalar_tensor_tensor(M[s][:, c, :].rearrange("p (b n) -> p b n", b=TB), as_tile(ps), 0.0,
                                                        e.a_sign[:, :].unsqueeze(1).broadcast_to([P, TB, P]),
                                                        ALU.max, ALU.mult)
                    last.then_inc(R["M"][s], 1)
                for s in range(S):
                    dve.wait_ge(R["M"][s], i + 2)
                    dve.sem_inc(tally, 1)
                    dve.tensor_reduce(scores[:, :, bass.ds((i * S + s) * HW, HW)],
                                      M[s][:, :, :].rearrange("p c (x d) -> p c x d", x=HW),
                                      mybir.AxisListType.X, ALU.add).then_inc(R["kept"][s], 1)
                for s in range(S):
                    dve.wait_ge(R["Qs"][s], i + 2)
                    dve.sem_inc(tally, 1)
                    dve.tensor_reduce(e.q_sums[:, bass.ds((i * S + s) * HW, HW)],
                                      Qs[s][:, :, :].rearrange("p b (x d) -> p (b x) d", x=HEADS),
                                      mybir.AxisListType.X, ALU.add).then_inc(R["lin"][s], 1)

            for s in range(S):
                dve.sem_inc(R["kept"][s], 1)
                dve.sem_inc(R["lin"][s], 1)
            for i in range(AHEAD):
                res.update(dve, i, range(S))
            turns(dve, turn)


def softmax_programs(k, ctx, scores, e):
    nc = k.nc
    E, EC = k.E, k.E // P
    NQ = k.B * k.HEADS // P
    sem = lambda n: k.sem(n)
    sb = lambda n, s: ctx.enter_context(nc.sbuf_tensor(n, s, F32))
    r, m, w = (each(NQ, lambda q: sb(f"sm_{n}{q}", [P, E])) for n in ("r", "m", "w"))
    turned, shifted, exped, attn_ready, back, step = (sem(f"sm_{n}") for n in ("turned", "shifted", "exp", "attn", "back", "step"))
    linear, summed = sem("sm_linear"), sem("sm_summed")
    attn_kept = sem("sm_kept")

    def on_tensor(pe):
        for c in range(EC):
            pe.matmul(k.bank[4 + c][:, :], e.PT[:, c * P:(c + 1) * P], e.q_sums[:, :], start=True, stop=True).then_inc(linear, 1)
        pe.wait_ge(summed, 1)
        for q in range(NQ):
            for c in range(EC):
                last = pe.transpose(k.bank[q][:, c * P:(c + 1) * P], scores[:, c, q * P:(q + 1) * P], k.ident[:, :])
            last.then_inc(turned, 1)
        for q in range(NQ):
            pe.wait_ge(attn_ready, q + 1)
            for c in range(EC):
                last = pe.transpose(k.bank[4 + q][:, c * P:(c + 1) * P], r[q][:, c * P:(c + 1) * P], k.ident[:, :])
            last.then_inc(back, 1)

    def on_scalar(act):
        for q in range(NQ):
            act.wait_ge(shifted, q + 1)
            act.activation(r[q][:, :], r[q][:, :], ACT.Exp).then_inc(exped, 1)

    def on_vector(dve):
        n = 0

        def wave(make):
            nonlocal n
            for q in range(NQ):
                make(q).then_inc(step, 1)
            n += NQ

        def after(q):
            dve.wait_ge(step, n - NQ + q + 1)

        def score_in(q):
            dve.wait_ge(turned, q + 1)
            return dve.tensor_tensor(r[q][:, :], k.bank[q][:, 0:E], e.log_w[:, :], ALU.add)

        def max_forward(q):
            after(q)
            return dve.tensor_tensor_scan(m[q][:, :], e.reset[:, 0:E], r[q][:, :], 0.0, ALU.add, ALU.max)

        def max_backward(q):
            after(q)
            return dve.tensor_tensor_scan(w[q][:, ::-1], e.reset[:, E:0:-1], m[q][:, ::-1], 0.0, ALU.add, ALU.max)

        def subtract_max(q):
            after(q)
            return dve.tensor_tensor(r[q][:, :], r[q][:, :], w[q][:, :], ALU.subtract)

        for c in range(EC):
            dve.wait_ge(linear, c + 1)
            last = dve.scalar_tensor_tensor(scores[:, c, :], k.bank[4 + c][:, :], 0.25, scores[:, c, :], ALU.mult, ALU.add)
        last.then_inc(summed, 1)
        wave(score_in)
        wave(max_forward)
        wave(max_backward)
        n_before = n
        for q in range(NQ):
            dve.wait_ge(step, n_before - NQ + q + 1)
            dve.tensor_tensor(r[q][:, :], r[q][:, :], w[q][:, :], ALU.subtract).then_inc(shifted, 1)

        def sum_forward(q):
            dve.wait_ge(exped, q + 1)
            return dve.tensor_tensor_scan(m[q][:, :], e.cont[:, 0:E], r[q][:, :], 0.0, ALU.mult, ALU.add)

        def keep_last(q):
            after(q)
            return dve.tensor_tensor(m[q][:, :], m[q][:, :], e.is_last[:, :], ALU.mult)

        def sum_backward(q):
            after(q)
            return dve.tensor_tensor_scan(w[q][:, ::-1], e.cont[:, E:0:-1], m[q][:, ::-1], 0.0, ALU.mult, ALU.add)

        def invert(q):
            after(q)
            return dve.reciprocal(w[q][:, :], w[q][:, :])

        wave(sum_forward)
        wave(keep_last)
        wave(sum_backward)
        wave(invert)
        for q in range(NQ):
            dve.wait_ge(step, n - NQ + q + 1)
            dve.tensor_tensor(r[q][:, :], r[q][:, :], w[q][:, :], ALU.mult).then_inc(attn_ready, 1)
        for q in range(NQ):
            dve.wait_ge(back, q + 1)
            dve.tensor_copy(scores[:, :, q * P:(q + 1) * P],
                            k.bank[4 + q][:, 0:E].rearrange("p (c x) -> p c x", c=EC)).then_inc(attn_kept, 1)
        dve.wait_ge(attn_kept, NQ)

    return on_tensor, on_scalar, on_vector


def stage_attend(k, ctx, Xv, attn, e, out):
    nc, X = k.nc, k.X
    S = 4
    EC, HEADS, DH = k.E // P, k.HEADS, k.DH
    HW = TB * HEADS
    sem = lambda n: k.sem(n)
    sb = lambda n, s, t=F32: ctx.enter_context(nc.sbuf_tensor(n, s, t))
    v_hi, v_lo = (each(2, lambda s: sb(f"at_{n}{s}", [P, TB, P], F32R)) for n in ("v_hi", "v_lo"))
    Vw = each(2, lambda s: sb(f"at_w{s}", [P, EC, TW]))
    Y, YT = (each(2, lambda s: sb(f"at_{n}{s}", [P, TB, P])) for n in ("y", "yT"))
    w_hi, w_lo = (each(S, lambda s: sb(f"at_{n}{s}", [P, EC, TW], F32R)) for n in ("w_hi", "w_lo"))
    vhi_done, vlo_done, V_done, Vw_done, whi_done, wlo0_done, wlo1_done, Yp_done, Y_done, Tp_done, YT_done, O_done, added, stored = (
        sem(f"at_{n}") for n in ("vhi", "vlo", "V", "Vw", "whi", "wlo0", "wlo1", "Yp", "Y", "Tp", "YT", "O", "added", "stored"))
    at_tally = sem("at_tally")
    softmax_on_tensor, softmax_on_scalar, softmax_on_vector = softmax_programs(k, ctx, attn, e)
    tiles = k.B // TB
    there = lambda t: exists(t, tiles)
    n_it = tiles // S
    psV, psY, psT, psO = (k.bank[0:2], k.bank[2:4]), k.bank[4:6], k.bank[6], k.bank[7]
    as_tile = lambda ps: ps[:, :].rearrange("p (b n) -> p b n", b=TB)
    tile_of = lambda buf, t: buf[:, bass.ds(t * TB, TB), :]

    def steps(eng, step):
        for i in (-1, 0):
            for s in range(S):
                step(S * i + s, s)
        with eng.Fori(1, n_it - 1) as i:
            for s in range(S):
                step(i * S + s, s)
        for i in (n_it - 1, n_it):
            for s in range(S):
                step(S * i + s, s)

    def wait(eng, done, t, back=0):
        if since(t, back):
            eng.wait_ge(done, t - back + 1)

    with nc.Block() as block:
        @block.tensor
        def _(pe):
            def scatter(t, s):
                wait(pe, wlo0_done, t)
                wait(pe, wlo1_done, t)
                wait(pe, Y_done, t, 2)
                for n, (part, c) in enumerate((part, c) for part in (w_hi, w_lo) for c in range(EC)):
                    last = pe.matmul(psY[s % 2][:, :], e.S1[:, c, :], part[s][:, c, :], start=n == 0, stop=n == 2 * EC - 1)
                last.then_inc(Yp_done, 1)

            def gather(t, s):
                wait(pe, vlo_done, t)
                wait(pe, Vw_done, t, 2)
                for c in range(EC):
                    for part in (v_hi, v_lo):
                        last = pe.matmul(psV[s % 2][c][:, :], e.DTr[:, c * P:(c + 1) * P], part[s % 2][:, :, :],
                                         start=part is v_hi, stop=part is v_lo)
                last.then_inc(V_done, 1)

            def turn_over(t, s):
                wait(pe, Y_done, t)
                wait(pe, YT_done, t, 1)
                for j in range(TB):
                    last = pe.transpose(psT[:, j * P:(j + 1) * P], Y[s % 2][:, j, :], k.ident[:, :])
                last.then_inc(Tp_done, 1)

            def project(t, s):
                wait(pe, YT_done, t)
                wait(pe, added, t, 1)
                for j in range(TB):
                    last = pe.matmul(psO[:, j * P:(j + 1) * P], YT[s % 2][:, j, :], e.WoT[:, :], start=True, stop=True)
                last.then_inc(O_done, 1)

            def step(t, s):
                if there(t):
                    scatter(t, s)
                if there(t + 3):
                    gather(t + 3, (s + 3) % S)
                if there(t - 1):
                    turn_over(t - 1, (s - 1) % S)
                if there(t - 2):
                    project(t - 2, (s - 2) % S)

            softmax_on_tensor(pe)
            steps(pe, step)

        @block.scalar
        def _(act):
            def step(t, s):
                if there(t):
                    wait(act, Yp_done, t)
                    wait(act, Tp_done, t, 2)
                    act.activation(Y[s % 2][:, :, :], as_tile(psY[s % 2]), ACT.Copy).then_inc(Y_done, 1)
                if there(t + 4):
                    wait(act, V_done, t + 4, 2)
                    wait(act, vlo_done, t + 4, 2)
                    act.activation(v_hi[s % 2][:, :, :], tile_of(Xv, t + 4), ACT.Copy).then_inc(vhi_done, 1)
                if there(t - 1):
                    wait(act, Tp_done, t - 1)
                    wait(act, O_done, t - 1, 2)
                    act.activation(YT[(s - 1) % 2][:, :, :], as_tile(psT), ACT.Copy).then_inc(YT_done, 1)
                if there(t + 3):
                    wait(act, Vw_done, t + 3)
                    wait(act, Yp_done, t + 3, 4)
                    act.activation(w_hi[(s + 3) % S][:, :, :], Vw[(s + 3) % 2][:, :, :], ACT.Copy).then_inc(whi_done, 1)

            softmax_on_scalar(act)
            steps(act, step)

        @block.gpsimd
        def _(pool):
            def step(t, s):
                if there(t + 4):
                    wait(pool, vhi_done, t + 4)
                    pool.sem_inc(at_tally, 1)
                    pool.tensor_tensor(out=v_lo[s % 2][:, :, :], in0=tile_of(Xv, t + 4), in1=v_hi[s % 2][:, :, :],
                                       op=ALU.subtract).then_inc(vlo_done, 1)
                if there(t + 3):
                    wait(pool, whi_done, t + 3)
                    q, r = (s + 3) % S, (s + 3) % 2
                    pool.tensor_tensor(out=w_lo[q][:, 1, :], in0=Vw[r][:, 1, :], in1=w_hi[q][:, 1, :],
                                       op=ALU.subtract).then_inc(wlo1_done, 1)

            steps(pool, step)

        @block.vector
        def _(dve):
            def step(t, s):
                if there(t + 2):
                    q, r = (s + 2) % S, s % 2
                    wait(dve, whi_done, t + 2)
                    dve.tensor_tensor(w_lo[q][:, 0, :], Vw[r][:, 0, :], w_hi[q][:, 0, :], ALU.subtract).then_inc(wlo0_done, 1)
                if there(t + 3):
                    r = (s + 3) % 2
                    wait(dve, V_done, t + 3)
                    wait(dve, wlo0_done, t + 3, 2)
                    wait(dve, wlo1_done, t + 3, 2)
                    for c in range(EC):
                        w = attn[:, c, bass.ds((t + 3) * HW, HW)]
                        last = dve.tensor_tensor(Vw[r][:, c, :].rearrange("p (x y) -> p x y", y=DH),
                                                 psV[r][c][:, :].rearrange("p (x y) -> p x y", y=DH),
                                                 w.unsqueeze(2).broadcast_to([P, HW, DH]), ALU.mult)
                    last.then_inc(Vw_done, 1)
                if there(t - 2):
                    wait(dve, O_done, t - 2)
                    xt = tile_of(X, t - 2)
                    dve.tensor_tensor(xt, as_tile(psO), xt, ALU.add).then_inc(added, 1)

            softmax_on_vector(dve)
            steps(dve, step)

        @block.sync
        def _(sp):
            with sp.Fori(0, tiles) as t:
                sp.wait_ge(added, t + 1)
                sp.dma_start(tile_of(out, t), tile_of(X, t)).then_inc(stored, 16)
            sp.wait_ge(stored, tiles * 16)


def build(nc, d, out):
    _, B, _ = d["x"].shape
    k, e = Shared(), Shared()
    k.nc, k.B, k.E, k.HEADS = nc, B, d["src"].shape[0], 4
    k.DH = P // k.HEADS
    with ExitStack() as ctx:
        sb = lambda n, s: ctx.enter_context(nc.sbuf_tensor(n, s, F32))
        k.X = sb("X", [P, B, P])
        k.adjT, k.AhatT, k.ident, k.ones = (sb(n, [P, P]) for n in ("adjT", "AhatT", "ident", "ones"))
        k.W1T, k.W2T, k.Wg = sb("W1T", [P, 2 * P]), sb("W2T", [P, 2, P]), sb("Wg", [P, 2, P])
        k.cols, k.rows = sb("cols", [P, NCOLS]), sb("rows", [P, 2, P])
        k.rstd, k.nmr = sb("rstd", [P, B]), sb("nmr", [P, B])
        k.zero = sb("zero", [P, 1])
        k.ln_const = {n: sb(f"ln_const{m}", [P, B // 4]) for m, n in enumerate(("-half", "two"))}
        E, EC = k.E, k.E // P
        e.Wqv, e.WoT, e.a_sign = sb("Wqv", [P, 2 * P]), sb("WoT", [P, P]), sb("a_sign", [P, P])
        e.S1, e.DTr = (ctx.enter_context(nc.sbuf_tensor(n, [P] + w, F32R)) for n, w in (("S1", [EC, P]), ("DTr", [E])))
        e.PT, e.is_last, e.log_w = (sb(n, [P, E]) for n in ("PT", "is_last", "log_w"))
        e.cont, e.reset = (sb(n, [P, E + 1]) for n in ("cont", "reset"))
        k.bank = each(8, lambda n: ctx.enter_context(nc.psum_tensor(f"bank{n}", [P, TW], F32)))

        with ExitStack() as c0:
            k.W0 = c0.enter_context(nc.sbuf_tensor("W0", [P, 3, P], F32))
            k.A12T = c0.enter_context(nc.sbuf_tensor("A12T", [P, 2, P], F32))
            k.diag_bc = c0.enter_context(nc.sbuf_tensor("diag_bc", [P, P], F32))
            k.X_AHEAD, k.x_ln = 2, LayerNormTail(k, c0, "x", 2)
            k.x_stats = lambda dve, i: each(2, lambda s: k.x_ln.stats(dve, k.X[:, bass.ds((i * 2 + s) * TB, TB), :], s, i))
            with ExitStack() as ce:
                e.row_i, e.col_i = (ce.enter_context(nc.sbuf_tensor(n, s, I32)) for n, s in (
                    ("edge_row_i", [P, 2, E]), ("edge_col_i", [P, 2, EC])))
                with ExitStack() as c:
                    stage_setup(k, c, d, e)
                with ExitStack() as c:
                    stage_edges(k, c, e)
            with ExitStack() as c:
                stage_layer0(k, c)

        with ExitStack() as c12:
            Y0 = c12.enter_context(nc.sbuf_tensor("Y0", [P, B * P], F32))
            bno6 = c12.enter_context(nc.sbuf_tensor("bno6", [P, 1, B // TB, 6], F32))
            with ExitStack() as c1:
                bn6 = c1.enter_context(nc.sbuf_tensor("bn6", [P, 2, B // TB, 6], F32))
                Y1 = c1.enter_context(nc.sbuf_tensor("Y1", [P, B * P], F32))
                with ExitStack() as c:
                    stage_gcn_hidden(k, c, (Y0, Y1), bn6)
                with ExitStack() as c:
                    stage_gcn_out(k, c, (Y0, Y1), bn6, bno6)
            k.recycle_semaphores()
            HT = Y0
            with ExitStack() as c2:
                sbr = lambda n, s: c2.enter_context(nc.sbuf_tensor(n, s, F32R))
                k.Wih, k.Whh = ([sbr(f"{n}_{part}", [P, 4, 4 * P]) for part in ("hi", "lo")] for n in ("Wih", "Whh"))
                k.lstm_bias = c2.enter_context(nc.sbuf_tensor("lstm_bias", [P, 4, 4], F32))
                with ExitStack() as c:
                    stage_conv(k, c, Y0, bno6, HT, d)
                with ExitStack() as c:
                    stage_lstm(k, c, HT)
            k.recycle_semaphores()
            with ExitStack() as c3:
                sb3 = lambda n, s: c3.enter_context(nc.sbuf_tensor(n, s, F32))
                e.q_sums = sb3("q_sums", [P, B * k.HEADS])
                scores, Xv = sb3("scores", [P, EC, B * k.HEADS]), HT[:, :].rearrange("p (b n) -> p b n", n=P)
                with ExitStack() as c:
                    stage_scores(k, c, HT, Xv, scores, e)
                with ExitStack() as c:
                    stage_attend(k, c, Xv, scores, e, out)


def kernel(**inputs):
    import numpy as np
    import concourse.bacc as bacc
    from concourse.bass_utils import run_bass_kernel_spmd

    g = {n: np.asarray(a) for n, a in inputs.items()}
    B, N, D = g["x"].shape
    per_channel = [g["L1_gnn_b1"].reshape(2, P), g["L1_gnn_g1"].reshape(2, P), g["L1_gnn_be1"].reshape(2, P),
                   g["L1_gnn_b2"].reshape(1, P), g["L1_gnn_g2"].reshape(1, P), g["L1_gnn_be2"].reshape(1, P),
                   g["L2_gnn_bih"].reshape(16, P), g["L2_gnn_bhh"].reshape(16, P), g["L2_gnn_bg0"].reshape(1, P)]
    layout = {
        "x": g["x"].transpose(1, 0, 2),
        "adj": g["adj"], "adjT": g["adj"].T,
        "cols": np.concatenate(per_channel, axis=0).T,
        "rows": np.stack([g["L0_gnn_bias"], g["L2_gnn_bg1"]]),
        "L0_W": g["L0_gnn_W"], "W1T": g["L1_gnn_W1"].T, "W2T": g["L1_gnn_W2"].T,
        "Wg0": g["L2_gnn_Wg0"], "Wg1": g["L2_gnn_Wg1"],
        "WihT": g["L2_gnn_Wih"].transpose(0, 2, 1), "WhhT": g["L2_gnn_Whh"].transpose(0, 2, 1),
        "Wqv": np.concatenate([g["L3_gnn_W_lin"].T, g["L3_gnn_W_val"].T], axis=1), "WoT": g["L3_gnn_W_out"].T,
        "a": g["L3_gnn_a"].reshape(D),
        "src": g["L3_gnn_src"], "dst": g["L3_gnn_dst"],
        "src_col": g["L3_gnn_src"].reshape(-1, P).T, "dst_col": g["L3_gnn_dst"].reshape(-1, P).T,
    }
    nc = bacc.Bacc("TRN2", target_bir_lowering=False, num_devices=1, dynamic_dma_scratch_size=2048)
    arrays, d = {}, {}
    for name, a in layout.items():
        arrays[f"in_{name}"] = np.ascontiguousarray(a)
        d[name] = nc.dram_tensor(f"in_{name}", a.shape, mybir.dt.from_np(a.dtype), kind="ExternalInput").ap()
    out = nc.dram_tensor("out", (N, B, D), F32, kind="ExternalOutput").ap()
    build(nc, d, out)
    r = run_bass_kernel_spmd(nc, [arrays], core_ids=[0])
    return np.ascontiguousarray(r.results[0]["out"].transpose(1, 0, 2))
```
